# Optimizing a Trainium2 kernel written in Bass

```python
import numpy as np
import jax
import jax.numpy as jnp

def _softmax(x, axis=-1):
    return jax.nn.softmax(x, axis=axis)

def _gelu(x):
    return jax.nn.gelu(x, approximate=True)

def _silu(x):
    return jax.nn.silu(x)

def _sigmoid(x):
    return jax.nn.sigmoid(x)

def _layernorm(x, axis=-1, eps=1e-05):
    m = jnp.mean(x, axis=axis, keepdims=True)
    v = jnp.var(x, axis=axis, keepdims=True)
    return (x - m) / jnp.sqrt(v + eps)

def _scatter_add(tgt, idx, src, axis=0):
    return tgt.at[idx].add(src)

def _segment_sum(src, seg, n):
    return jax.ops.segment_sum(src, seg, n)
kernel_name = 'mk_conv_attn_hybrid_d2_conv_nchw256_r4_2a9b12'

def setup_inputs(seed: int=0):
    np.random.seed(seed)
    _w = jnp.asarray

    def _rec_inputs():
        import jax
        import jax.numpy as jnp
        _gk = jax.random.key(seed)
        x = -0.0003482 + 1 * jax.random.normal(jax.random.fold_in(_gk, 1), (32, 64, 48, 48), jnp.float32)
        return x
    x = _rec_inputs()

    def _L0_conv_setup():
        import jax, jax.numpy as jnp
        import numpy as np
        GAMMA = 2
        EPS = 1e-08
        key = jax.random.key(seed)
        k1, k2 = jax.random.split(key, 2)
        B, C, H, W = (32, 64, 48, 48)
        x = jax.random.normal(k1, (B, C, H, W), jnp.float32)
        Wc = jax.random.normal(k2, (C, C), jnp.float32) * (1.0 / np.sqrt(C))
        bc = jnp.zeros((C,), jnp.float32)
        return {'x': x, 'Wc': Wc, 'bc': bc}
    _L0_conv_all = _L0_conv_setup()
    _L0_conv_in = {k: v for k, v in _L0_conv_all.items() if k in ('Wc', 'bc')}
    del _L0_conv_all

    def _L1_attn_setup():
        import jax, jax.numpy as jnp
        import numpy as np
        D_MODEL = 64
        D_STATE = 16
        D_CONV = 4
        EXPAND = 2
        HEADDIM = 16
        D_INNER = EXPAND * D_MODEL
        NHEADS = D_INNER // HEADDIM
        CONV_DIM = D_INNER + 2 * D_STATE
        BATCH = 8
        SEQ = 1024

        def _rmsnorm(x, w, eps):
            return x * jax.lax.rsqrt(jnp.mean(x * x, axis=-1, keepdims=True) + eps) * w
        key = jax.random.key(seed)
        ks = jax.random.split(key, 6)
        x = jax.random.normal(ks[0], (BATCH, SEQ, D_MODEL), jnp.float32)
        d_in_proj = 2 * D_INNER + 2 * D_STATE + NHEADS
        W_in = jax.random.normal(ks[1], (d_in_proj, D_MODEL), jnp.float32) / np.sqrt(D_MODEL)
        conv_w = jax.random.normal(ks[2], (CONV_DIM, D_CONV), jnp.float32) / np.sqrt(D_CONV)
        conv_b = jnp.zeros((CONV_DIM,), jnp.float32)
        dt = jnp.exp(jax.random.uniform(ks[3], (NHEADS,), jnp.float32, np.log(0.001), np.log(0.1)))
        dt_bias = dt + jnp.log(-jnp.expm1(-dt))
        A_log = jnp.log(jax.random.uniform(ks[4], (NHEADS,), jnp.float32, 1.0, 16.0))
        Dp = jnp.ones((NHEADS,), jnp.float32)
        gnorm_w = jnp.ones((D_INNER,), jnp.float32)
        norm_w = jnp.ones((D_MODEL,), jnp.float32)
        W_out = jax.random.normal(ks[5], (D_MODEL, D_INNER), jnp.float32) / np.sqrt(D_INNER)
        return {'x': x, 'W_in': W_in, 'conv_w': conv_w, 'conv_b': conv_b, 'dt_bias': dt_bias, 'A_log': A_log, 'Dp': Dp, 'gnorm_w': gnorm_w, 'norm_w': norm_w, 'W_out': W_out}
    _L1_attn_all = _L1_attn_setup()
    _L1_attn_in = {k: v for k, v in _L1_attn_all.items() if k in ('W_in', 'conv_w', 'conv_b', 'dt_bias', 'A_log', 'Dp', 'gnorm_w', 'norm_w', 'W_out')}
    del _L1_attn_all

    def _L1_ffn_setup():
        import math
        import jax, jax.numpy as jnp
        import numpy as np
        CAPACITY_FACTOR = 1.25
        key = jax.random.key(seed)
        ks = jax.random.split(key, 5)
        B, L, D, F, E = (8, 2048, 64, 256, 8)
        h = jax.random.normal(ks[0], (B, L, D), dtype=jnp.float32)
        gate_w = jax.random.normal(ks[1], (D, E), dtype=jnp.float32) * 0.02
        gate_b = jnp.zeros((E,), dtype=jnp.float32)
        w1 = jax.random.normal(ks[2], (E, D, F), dtype=jnp.float32) * (1.0 / math.sqrt(D))
        b1 = jnp.zeros((E, F), dtype=jnp.float32)
        w2 = jax.random.normal(ks[3], (E, F, D), dtype=jnp.float32) * (1.0 / math.sqrt(F))
        b2 = jnp.zeros((E, D), dtype=jnp.float32)
        return {'h': h, 'gate_w': gate_w, 'gate_b': gate_b, 'w1': w1, 'b1': b1, 'w2': w2, 'b2': b2}
    _L1_ffn_all = _L1_ffn_setup()
    _L1_ffn_in = {k: v for k, v in _L1_ffn_all.items() if k in ('gate_w', 'gate_b', 'w1', 'b1', 'w2', 'b2')}
    del _L1_ffn_all
    return {'x': x, 'L0_conv_Wc': _L0_conv_in['Wc'], 'L0_conv_bc': _L0_conv_in['bc'], 'L1_attn_W_in': _L1_attn_in['W_in'], 'L1_attn_conv_w': _L1_attn_in['conv_w'], 'L1_attn_conv_b': _L1_attn_in['conv_b'], 'L1_attn_dt_bias': _L1_attn_in['dt_bias'], 'L1_attn_A_log': _L1_attn_in['A_log'], 'L1_attn_Dp': _L1_attn_in['Dp'], 'L1_attn_gnorm_w': _L1_attn_in['gnorm_w'], 'L1_attn_norm_w': _L1_attn_in['norm_w'], 'L1_attn_W_out': _L1_attn_in['W_out'], 'L1_ffn_gate_w': _L1_ffn_in['gate_w'], 'L1_ffn_gate_b': _L1_ffn_in['gate_b'], 'L1_ffn_w1': _L1_ffn_in['w1'], 'L1_ffn_b1': _L1_ffn_in['b1'], 'L1_ffn_w2': _L1_ffn_in['w2'], 'L1_ffn_b2': _L1_ffn_in['b2']}

def reference(x, L0_conv_Wc, L0_conv_bc, L1_attn_W_in, L1_attn_conv_w, L1_attn_conv_b, L1_attn_dt_bias, L1_attn_A_log, L1_attn_Dp, L1_attn_gnorm_w, L1_attn_norm_w, L1_attn_W_out, L1_ffn_gate_w, L1_ffn_gate_b, L1_ffn_w1, L1_ffn_b1, L1_ffn_w2, L1_ffn_b2):
    import jax
    import jax.numpy as jnp

    def _L0_conv_ref(x, Wc, bc):
        import jax, jax.numpy as jnp
        import numpy as np
        GAMMA = 2
        EPS = 1e-08
        B, C, H, W = x.shape
        P = H * W
        xf = x.reshape(B, C, P)
        nrm = jnp.maximum(jnp.sqrt(jnp.sum(xf * xf, axis=1)), EPS)
        xn = xf / nrm[:, None, :]
        s = jax.nn.relu(jnp.einsum('bcp,bcq->bpq', xn, xn)) ** GAMMA
        g = jnp.einsum('oc,bcp->bop', Wc, xf) + bc[None, :, None]
        out = jnp.einsum('bpq,bcq->bcp', s, g)
        return out.reshape(B, C, H, W)

    def _L1_attn_ref(x, W_in, conv_w, conv_b, dt_bias, A_log, Dp, gnorm_w, norm_w, W_out):
        import jax, jax.numpy as jnp
        import numpy as np
        D_MODEL = 64
        D_STATE = 16
        D_CONV = 4
        EXPAND = 2
        HEADDIM = 16
        D_INNER = EXPAND * D_MODEL
        NHEADS = D_INNER // HEADDIM
        CONV_DIM = D_INNER + 2 * D_STATE
        BATCH = 8
        SEQ = 1024

        def _rmsnorm(x, w, eps):
            return x * jax.lax.rsqrt(jnp.mean(x * x, axis=-1, keepdims=True) + eps) * w
        Bsz, L, _ = x.shape
        xn = _rmsnorm(x, norm_w, jnp.finfo(x.dtype).eps)
        zxbcdt = jnp.einsum('bld,ed->ble', xn, W_in)
        z = zxbcdt[..., :D_INNER]
        xBC = zxbcdt[..., D_INNER:D_INNER + CONV_DIM]
        dt = zxbcdt[..., -NHEADS:]
        xpad = jnp.pad(xBC, ((0, 0), (D_CONV - 1, 0), (0, 0)))
        conv = sum((xpad[:, k:k + L, :] * conv_w[:, k] for k in range(D_CONV))) + conv_b
        xBC = jax.nn.silu(conv)
        xs = xBC[..., :D_INNER].reshape(Bsz, L, NHEADS, HEADDIM)
        Bm = xBC[..., D_INNER:D_INNER + D_STATE]
        Cm = xBC[..., D_INNER + D_STATE:]
        dt = jax.nn.softplus(dt + dt_bias)
        dA = jnp.exp(dt * -jnp.exp(A_log))

        def step(state, inp):
            dA_t, dt_t, B_t, C_t, x_t = inp
            state = state * dA_t[:, :, None, None] + (dt_t[:, :, None] * x_t)[..., None] * B_t[:, None, None, :]
            y = jnp.einsum('bhpn,bn->bhp', state, C_t)
            return (state, y)
        init = jnp.zeros((Bsz, NHEADS, HEADDIM, D_STATE), x.dtype)
        tm = lambda a: jnp.moveaxis(a, 1, 0)
        _, ys = jax.lax.scan(step, init, (tm(dA), tm(dt), tm(Bm), tm(Cm), tm(xs)))
        y = jnp.moveaxis(ys, 0, 1) + Dp[None, None, :, None] * xs
        y = y.reshape(Bsz, L, D_INNER)
        y = _rmsnorm(y * jax.nn.silu(z), gnorm_w, 1e-05)
        return x + jnp.einsum('ble,de->bld', y, W_out)

    def _L1_ffn_ref(h, gate_w, gate_b, w1, b1, w2, b2):
        import math
        import jax, jax.numpy as jnp
        import numpy as np
        CAPACITY_FACTOR = 1.25
        B, L, D = h.shape
        E = gate_w.shape[1]
        T = B * L
        C = max(1, math.ceil(CAPACITY_FACTOR * T / E))
        x = h.reshape(T, D)
        logits = x @ gate_w + gate_b
        probs = jax.nn.softmax(logits, axis=-1)
        idx = jnp.argmax(probs, axis=-1)
        prb = jnp.take_along_axis(probs, idx[:, None], axis=1)[:, 0]
        one_hot = jax.nn.one_hot(idx, E, dtype=jnp.float32)
        pos = (jnp.cumsum(one_hot, axis=0) * one_hot).sum(-1).astype(jnp.int32) - 1
        kept = pos < C
        pos_safe = jnp.where(kept, pos, C)
        buf = jnp.zeros((E, C, D), dtype=h.dtype).at[idx, pos_safe].set(x, mode='drop')
        hmid = jax.nn.relu(jnp.einsum('ecd,edf->ecf', buf, w1) + b1[:, None, :])
        ybuf = jnp.einsum('ecf,efd->ecd', hmid, w2) + b2[:, None, :]
        pos_g = jnp.minimum(pos, C - 1)
        y_tok = ybuf[idx, pos_g] * (prb * kept)[:, None]
        y = y_tok.reshape(B, L, D)
        y = jnp.nan_to_num(y, nan=0.0, posinf=10000.0, neginf=-10000.0)
        return y

    def _gn(v, G=32, eps=1e-05):
        B_, C_, H_, W_ = v.shape
        g = v.reshape(B_, G, C_ // G, H_, W_)
        m = jnp.mean(g, axis=(2, 3, 4), keepdims=True)
        s = jnp.var(g, axis=(2, 3, 4), keepdims=True)
        return ((g - m) / jnp.sqrt(s + eps)).reshape(v.shape)

    def _ln_c(v, eps=1e-06):
        m = jnp.mean(v, axis=1, keepdims=True)
        s = jnp.var(v, axis=1, keepdims=True)
        return (v - m) / jnp.sqrt(s + eps)

    def _ln_t(v, eps=1e-05):
        m = jnp.mean(v, axis=-1, keepdims=True)
        s = jnp.var(v, axis=-1, keepdims=True)
        return (v - m) / jnp.sqrt(s + eps)

    def _to_tokens(v):
        B_, C_, H_, W_ = v.shape
        return v.reshape(B_, C_, H_ * W_).transpose(0, 2, 1)

    def _from_tokens(t, like):
        B_, C_, H_, W_ = like.shape
        return t.transpose(0, 2, 1).reshape(B_, C_, H_, W_)
    x = x + _L0_conv_ref(_gn(x), L0_conv_Wc, L0_conv_bc)
    t = _to_tokens(x)
    t = t + _L1_attn_ref(_ln_t(t), L1_attn_W_in, L1_attn_conv_w, L1_attn_conv_b, L1_attn_dt_bias, L1_attn_A_log, L1_attn_Dp, L1_attn_gnorm_w, L1_attn_norm_w, L1_attn_W_out)
    t = t + _L1_ffn_ref(_ln_t(t), L1_ffn_gate_w, L1_ffn_gate_b, L1_ffn_w1, L1_ffn_b1, L1_ffn_w2, L1_ffn_b2)
    x = _from_tokens(t, x)
    return x

_drawn_inputs = setup_inputs


def setup_inputs(seed=0):
    import zlib

    import numpy as np

    out = dict(_drawn_inputs(seed))
    spreads = {'L0_conv_bc': (0.0, 0.1),
     'L1_attn_conv_b': (0.0, 0.498),
     'L1_attn_Dp': (1.0, 0.6),
     'L1_attn_gnorm_w': (1.0, 0.2),
     'L1_attn_norm_w': (1.0, 0.2),
     'L1_ffn_gate_b': (0.0, 0.647),
     'L1_ffn_b1': (0.0, 0.8),
     'L1_ffn_b2': (0.0, 2.0)}
    factors = {'L1_attn_A_log': 3.069, 'L1_ffn_gate_w': 4.081, 'L1_ffn_w1': 4.575, 'L1_ffn_w2': 3.847}
    for name, (base, spread) in spreads.items():
        noise = np.random.default_rng([zlib.crc32(name.encode()), seed]).standard_normal(out[name].shape)
        drawn = base * np.exp(spread * noise) if base else spread * noise
        out[name] = jnp.asarray(drawn.astype(out[name].dtype))
    for name, factor in factors.items():
        out[name] = (out[name] * factor).astype(out[name].dtype)
    return out
```

```python
from contextlib import ExitStack

import concourse.bass as bass
from concourse import mybir

F32 = mybir.dt.float32
F16 = mybir.dt.float16
I32 = mybir.dt.int32
U32 = mybir.dt.uint32
ALU = mybir.AluOpType
ACT = mybir.ActivationFunctionType
AX = mybir.AxisListType.X

P = 128
C = 64
HEADS = 8
HD = 16
NS = 16
DI = HEADS * HD
XBC = DI + 2 * NS
ZX = XBC + DI + HEADS
E = 8
FF = 256
XF_SCALE = 256.0
PB = 384
PAD = 2
BIG = 1.0e6
FBLK = 768
FLT_MAX = 3.4028234663852886e38


def build(nc, x, Wc, bc, W_in, conv_w, conv_b, dt_bias, A_log, Dp, gnorm_w, norm_w, W_out,
          gate_w, gate_b, w1, b1, w2, b2, out):
    B = x.shape[0]
    T = x.shape[2] * x.shape[3]
    TILES = T // P
    NPB = T // PB
    QP = TILES // 2
    UNITS = NPB * QP
    UPC = UNITS // TILES
    assert T % PB == 0 and TILES % 2 == 0 and UNITS % TILES == 0
    CAP = max(1, -(-5 * B * T // (4 * E)))
    FB = -(-CAP // FBLK)
    STRIDE = FB * FBLK
    x_d = x.rearrange("b c h w -> b c (h w)")
    out_d = out.rearrange("b c h w -> b c (h w)")

    with ExitStack() as ctx:
        def sb(name, shape, dt=F32):
            return ctx.enter_context(nc.sbuf_tensor(name, shape, dt))

        def sem(name):
            return ctx.enter_context(nc.semaphore(name))

        buf_d = nc.dram_tensor("expert_in", [E * STRIDE, C], F32).ap()
        yb_d = nc.dram_tensor("expert_out", [E * STRIDE, C], F32).ap()
        t2_d = nc.dram_tensor("tokens_mid", [B * T, C], F32).ap()

        ident = sb("ident", [P, P])
        tri_le = sb("tri_le", [P, P])
        tri_gt = sb("tri_gt", [P, P])
        ones = sb("ones", [P, P])
        pair = sb("pair", [P, P])
        half = sb("half", [P, TILES])
        eights = sb("eights", [P, E])
        wr = sb("wr", [P, P])
        wa = sb("wa", [P, ZX])
        wb = sb("wb", [P, XBC])
        wo = sb("wo", [P, P])
        gwd = sb("gwd", [P, 2 * E])
        bc_b = sb("bc_b", [P, C])
        cb_b = sb("cb_b", [P, XBC])
        dtb_b = sb("dtb_b", [P, HEADS])
        nega_b = sb("nega_b", [P, HEADS])
        dp_b = sb("dp_b", [P, HEADS])
        gb_b = sb("gb_b", [P, E])
        b2_b = sb("b2_b", [P, E, C])
        b1_c = sb("b1_c", [P, E, 2])
        carry = sb("carry", [P, E])
        slot_g = sb("slot_g", [P, B * TILES], I32)
        gain = sb("gain", [P, B * TILES])

        psum = ctx.enter_context(nc.psum_tensor("psum", [P, 8, 512], F32))

        def bank(b, w=512):
            return psum[:, b, 0:w]

        with ExitStack() as c0:
            def sb0(name, shape, dt=F32):
                return c0.enter_context(nc.sbuf_tensor(name, shape, dt))
            wci = sb0("wci", [C, C])
            win = sb0("win", [P, 3, C])
            wout = sb0("wout", [C, DI])
            wt = sb0("wt", [P, ZX])
            nw = sb0("nw", [P, 1])
            gw = sb0("gw", [DI, 1])
            cwb = sb0("cwb", [P, XBC, 4])
            al = sb0("al", [P, HEADS])
            zero = sb0("zero", [P, STRIDE * C // P])
            c_load = c0.enter_context(nc.semaphore("c_load"))
            c_pool = c0.enter_context(nc.semaphore("c_pool"))
            c_dve = c0.enter_context(nc.semaphore("c_dve"))
            c_pe = c0.enter_context(nc.semaphore("c_pe"))
            c_act = c0.enter_context(nc.semaphore("c_act"))
            c_zero = c0.enter_context(nc.semaphore("c_zero"))
            with nc.Block() as block:
                loads = [
                    (wci[:, :], Wc), (win[:, 0, :], W_in[0:P, :]), (win[:, 1, :], W_in[P:2 * P, :]),
                    (win[0:ZX - 2 * P, 2, :], W_in[2 * P:ZX, :]), (wout[:, :], W_out),
                    (nw[0:C, :], norm_w.unsqueeze(1)), (nw[C:P, :], norm_w.unsqueeze(1)), (gw[:, :], gnorm_w.unsqueeze(1)),
                    (cwb[:, :, :], conv_w.partition_broadcast(P)), (al[:, :], A_log.partition_broadcast(P)),
                    (bc_b[:, :], bc.partition_broadcast(P)), (cb_b[:, :], conv_b.partition_broadcast(P)),
                    (dtb_b[:, :], dt_bias.partition_broadcast(P)), (dp_b[:, :], Dp.partition_broadcast(P)),
                    (gb_b[:, :], gate_b.partition_broadcast(P)), (b2_b[:, :, :], b2.partition_broadcast(P)),
                    (gwd[0:C, 0:E], gate_w), (gwd[C:P, E:2 * E], gate_w),
                    (b1_c[:, :, :], b1.rearrange("e (h f) -> f e h", f=P)),
                ]

                @block.sync
                def _(sp):
                    sp.wait_ge(c_pool, 12)
                    with nc.allow_non_contiguous_dma(reason="small constants"):
                        for dst, src in loads:
                            sp.dma_start(dst, src).then_inc(c_load, 16)
                    sp.wait_ge(c_dve, 1)
                    bz = buf_d.rearrange("(n p r) c -> n p (r c)", p=P, n=E)
                    for n in range(E):
                        sp.dma_start(bz[n], zero[:, :]).then_inc(c_zero, 16)
                    sp.wait_ge(c_load, 16 * len(loads))
                    sp.wait_ge(c_zero, 16 * E)

                @block.gpsimd
                def _(pool):
                    for t in (ident, pair):
                        pool.memset(t[:, :], 0.0).then_inc(c_pool, 1)
                    for t in (tri_le, tri_gt, ones):
                        pool.memset(t[:, :], 1.0).then_inc(c_pool, 1)
                    pool.memset(half[:, :], -0.5).then_inc(c_pool, 1)
                    pool.memset(wr[:, :], 0.0).then_inc(c_pool, 1)
                    pool.memset(wa[:, :], 0.0).then_inc(c_pool, 1)
                    pool.memset(wo[:, :], 0.0).then_inc(c_pool, 1)
                    pool.memset(gwd[:, :], 0.0).then_inc(c_pool, 1)
                    pool.memset(carry[:, :], 0.0).then_inc(c_pool, 1)
                    pool.iota(eights[:, :], pattern=[[-1, E]], base=E, channel_multiplier=0,
                              allow_small_or_imprecise_dtypes=True).then_inc(c_pool, 1)
                    pool.wait_ge(c_pool, 12)
                    pool.affine_select(out=ident[:, :], in_=ident[:, :], compare_op=ALU.not_equal, fill=1.0, base=0,
                                       pattern=[[-1, P]], channel_multiplier=1).then_inc(c_pool, 1)
                    pool.affine_select(out=tri_le[:, :], in_=tri_le[:, :], compare_op=ALU.is_ge, fill=0.0, base=0,
                                       pattern=[[1, P]], channel_multiplier=-1).then_inc(c_pool, 1)
                    pool.affine_select(out=tri_gt[:, :], in_=tri_gt[:, :], compare_op=ALU.is_gt, fill=0.0, base=0,
                                       pattern=[[-1, P]], channel_multiplier=1).then_inc(c_pool, 1)
                    pv = pair[:, :].rearrange("p (g k) -> p g k", k=2)
                    pool.affine_select(out=pv, in_=pv, compare_op=ALU.not_equal, fill=0.5, base=0,
                                       pattern=[[-2, P // 2], [0, 2]], channel_multiplier=1).then_inc(c_pool, 1)
                    pool.wait_ge(c_pool, 16)
                    pool.affine_select(out=pv, in_=pv, compare_op=ALU.not_equal, fill=0.5, base=-1,
                                       pattern=[[-2, P // 2], [0, 2]], channel_multiplier=1).then_inc(c_pool, 1)

                @block.tensor
                def _(pe):
                    pe.wait_ge(c_load, 16 * len(loads))
                    pe.wait_ge(c_pool, 17)
                    pe.transpose(psum[0:C, 0, 0:C], wci[:, :], ident[0:C, 0:C])
                    for k, w in ((0, P), (1, P), (2, ZX - 2 * P)):
                        pe.transpose(psum[0:C, 1, k * P:k * P + w], win[0:w, k, :], ident[0:w, 0:w])
                    pe.transpose(psum[0:DI, 2, 0:C], wout[:, :], ident[0:C, 0:C]).then_inc(c_pe, 1)

                @block.scalar
                def _(act):
                    act.wait_ge(c_load, 16 * len(loads))
                    act.activation(al[:, :], al[:, :], ACT.Exp).then_inc(c_act, 1)

                @block.vector
                def _(dve):
                    dve.memset(zero[:, :], 0.0).then_inc(c_dve, 1)
                    dve.wait_ge(c_pe, 1)
                    dve.wait_ge(c_act, 1)
                    dve.tensor_scalar(nega_b[:, :], al[:, :], -1.0, None, ALU.mult)
                    dve.tensor_scalar(wr[0:C, 0:C], psum[0:C, 0, 0:C], 1.0 / XF_SCALE, None, ALU.mult)
                    dve.tensor_copy(wr[0:C, C:P], ident[0:C, 0:C])
                    dve.tensor_scalar(wo[:, 0:C], psum[0:DI, 2, 0:C], gw[:, 0:1], None, ALU.mult)
                    for h in (0, 1):
                        rows = slice(C * h, C * h + C)
                        dve.tensor_scalar(wt[rows, 0:XBC], psum[0:C, 1, DI:DI + XBC], nw[0:C, 0:1], None, ALU.mult)
                        dve.tensor_scalar(wt[rows, XBC:XBC + DI], psum[0:C, 1, 0:DI], nw[0:C, 0:1], None, ALU.mult)
                        dve.tensor_scalar(wt[rows, XBC + DI:ZX], psum[0:C, 1, DI + XBC:ZX], nw[0:C, 0:1], None,
                                          ALU.mult).then_inc(c_dve, 1)
                    dve.wait_ge(c_dve, 3)
                    dve.tensor_copy(wa[0:C, XBC:ZX], wt[0:C, XBC:ZX])
                    for h in (0, 1):
                        rows = slice(C * h, C * h + C)
                        dve.tensor_tensor(wa[rows, 0:XBC], wt[rows, 0:XBC], cwb[rows, :, 3 - h], ALU.mult)
                        dve.tensor_tensor(wb[rows, :], wt[rows, 0:XBC], cwb[rows, :, 1 - h], ALU.mult)

        with ExitStack() as c1:
            def sb1(name, shape, dt=F32):
                return c1.enter_context(nc.sbuf_tensor(name, shape, dt))

            names = []

            def sem1(name):
                s = c1.enter_context(nc.semaphore(name))
                names.append(s)
                return s

            xd = sb1("xd", [P, T])
            hh = sb1("hh", [P, T], F16)
            ll = sb1("ll", [P, T], F16)
            st = sb1("st", [P, T], F16)
            stats = sb1("stats", [P, NPB, 6])
            mv = sb1("mv", [P, 8])
            xtm = sb1("xtm", [P, TILES, C])
            gt = sb1("gt", [P, TILES, C])
            rn2 = sb1("rn2", [P, TILES])
            rel = sb1("rel", [P, 2, 2, PB])
            scr = sb1("scr", [P, 2, 2, PB])
            osb = sb1("osb", [P, T])
            big = sb1("big", [P, 2 * T])
            tmp = sb1("tmp", [P, T])
            xf = big[:, 0:T]
            tok1 = sb1("tok1", [P, TILES, C])
            res = sb1("res", [P, TILES, C])
            xl = sb1("xl", [P, TILES, C])
            col = sb1("col", [P, 8, TILES])
            x2 = sb1("x2", [P, T + 2 * PAD])
            xbc = sb1("xbc", [P, TILES, XBC])
            zs = sb1("zs", [P, TILES, DI])
            dts = sb1("dts", [P, 6, TILES, HEADS])
            dec = sb1("dec", [P, 3, TILES, HEADS])
            xp = sb1("xp", [P, TILES, DI + HD])
            yi = sb1("yi", [P, TILES, DI])
            gm = sb1("gm", [P, TILES, P])
            states = sb1("states", [NS, TILES, DI])
            sdec = sb1("sdec", [NS, DI])
            at = sb1("at", [P, HEADS, P])
            el = sb1("el", [P, HEADS, P])
            yts = sb1("yts", [P, 2, P])
            tok2 = sb1("tok2", [P, TILES, C])
            tok3 = sb1("tok3", [P, TILES, C])
            rt = sb1("rt", [P, 6, TILES, E])
            slot_s = sb1("slot_s", [P, TILES], I32)

            scattered = c1.enter_context(nc.semaphore("scattered"))
            x_in = sem1("x_in")
            x_free = sem1("x_free")
            pool_s = sem1("pool_s")
            dve_s = sem1("dve_s")
            act_s = sem1("act_s")
            gn_mean = sem1("gn_mean")
            gn_dev = sem1("gn_dev")
            gn_var = sem1("gn_var")
            gn_ve = sem1("gn_ve")
            gn_rs = sem1("gn_rs")
            gn_ready = sem1("gn_ready")
            hh_done = sem1("hh_done")
            ll_done = sem1("ll_done")
            xf_done = sem1("xf_done")
            st_done = sem1("st_done")
            gx_mm = sem1("gx_mm")
            gx_out = sem1("gx_out")
            gt_done = sem1("gt_done")
            qk_done = sem1("qk_done")
            rel_done = sem1("rel_done")
            sq_done = sem1("sq_done")
            av_done = sem1("av_done")
            o_done = sem1("o_done")
            at_done = sem1("at_done")
            d_done = sem1("d_done")
            el_done = sem1("el_done")
            m_done = sem1("m_done")
            yt_done = sem1("yt_done")
            yts_done = sem1("yts_done")
            ytt_done = sem1("ytt_done")
            y_done = sem1("y_done")
            f_sem = {n: sem1("f_" + n) for n in (
                "yz", "sq", "var", "pow", "yt", "yts", "op", "opo", "t2", "c2", "c2q", "var2", "pow2", "t3",
                "tt", "tts", "lg", "exp_in", "exp", "oh", "rank", "rank_o", "slot", "store")}
            q_sem = {n: sem1("q_" + n) for n in (
                "ot", "oth", "ots", "c1", "c1q", "var", "pow", "rv", "pow2", "xn", "xt", "x2a", "x2d", "ip", "pre", "zsil",
                "spin", "e", "u", "ln", "a", "cum", "dec", "xp", "xpp", "yd", "bc", "bcs", "g", "gm", "ds", "st", "in", "ino")}
            assert P == 128

            with nc.Block() as block:
                @block.gpsimd
                def _(pool):
                    pool.memset(x2[:, 0:PAD + 1], 0.0)
                    pool.memset(xp[:, :, DI:DI + HD], 0.0)
                    pool.memset(states[:, 0, :], 0.0)

                @block.sync
                def _(sp):
                    sp.dma_start(xd[0:C, :], x_d[0]).then_inc(x_in, 16)
                    sp.dma_start(xd[C:P, :], x_d[0]).then_inc(x_in, 16)
                    sp.wait_ge(x_in, 32)

            def clear():
                ids = sorted(s.num for s in names)
                assert ids == list(range(ids[0], ids[0] + len(ids)))
                nc.all_engine_barrier()
                nc.sync.sem_clear(range(ids[0], ids[-1] + 1))
                nc.all_engine_barrier()

            clear()

            def tile3(ap, n=TILES):
                return ap.rearrange("p (t c) -> p t c", t=n)

            def bt(ap, n):
                return ap.unsqueeze(len(ap.shape)).to_broadcast(list(ap.shape) + [n])

            GROUPS4 = [(g, min(4, TILES - g)) for g in range(0, TILES, 4)]

            def iteration(bi, conv, ssm, nxt):
                ng = TILES // 6
                nblk = len(GROUPS4)
                with nc.Block() as block:
                    @block.sync
                    def _(sp):
                        if conv and nxt is not None:
                            sp.wait_ge(x_free, 2)
                            sp.wait_ge(gx_out, 2 * ng)
                            sp.dma_start(xd[0:C, :], x_d[nxt]).then_inc(x_in, 16)
                            sp.dma_start(xd[C:P, :], x_d[nxt]).then_inc(x_in, 16)
                        if ssm:
                            sp.wait_ge(f_sem["t2"], 1)
                            sp.dma_start(t2_d[bass.ds((bi - 1) * T, T), :].rearrange("(t p) c -> p t c", p=P),
                                         tok2[:, :, :]).then_inc(f_sem["store"], 16)
                            sp.wait_ge(f_sem["store"], 16)
                        if conv and nxt is not None:
                            sp.wait_ge(x_in, 32)

                    @block.gpsimd
                    def _(pool):
                        if conv:
                            pool.wait_ge(gn_ve, 1)
                            pool.tensor_tensor(mv[:, 5:6], mv[:, 4:5], half[:, 0:1], ALU.pow).then_inc(gn_rs, 1)
                            pool.wait_ge(hh_done, 1)
                            pool.tensor_copy(st[0:C, :], hh[0:C, :]).then_inc(st_done, 1)
                            pool.wait_ge(ll_done, 1)
                            pool.tensor_copy(st[C:P, :], ll[C:P, :]).then_inc(st_done, 1)
                            pool.wait_ge(st_done, 2)
                        if ssm:
                            for c in range(TILES):
                                if c >= 1:
                                    pool.wait_ge(d_done, c)
                                pool.tensor_tensor(at[:, :, :], tri_le[:, :].unsqueeze(1).to_broadcast([P, HEADS, P]),
                                                   bt(dts[:, 5, c, :], P), ALU.mult).then_inc(at_done, 1)
                            pool.wait_ge(f_sem["var"], 1)
                            pool.tensor_tensor(col[:, 0, :], col[:, 1, :], half[:, :], ALU.pow).then_inc(f_sem["pow"], 1)
                            pool.wait_ge(f_sem["var2"], 1)
                            pool.tensor_tensor(col[:, 4, :], col[:, 3, :], half[:, :], ALU.pow).then_inc(f_sem["pow2"], 1)
                            pool.wait_ge(f_sem["slot"], 1)
                            for j in range(TILES):
                                pool.indirect_dma_start(
                                    out=buf_d, out_offset=bass.IndirectOffsetOnAxis(ap=slot_s[:, j:j + 1].bitcast(U32), axis=0),
                                    in_=tok3[:, j, :], in_offset=None, bounds_check=E * STRIDE - 1, oob_is_err=False,
                                ).then_inc(scattered, 16)
                        if conv:
                            pool.wait_ge(q_sem["var"], 1)
                            pool.tensor_tensor(col[:, 4, :], col[:, 3, :], half[:, :], ALU.pow).then_inc(q_sem["pow"], 1)
                            pool.wait_ge(q_sem["rv"], 1)
                            pool.tensor_tensor(col[:, 6, :], col[:, 5, :], half[:, :], ALU.pow).then_inc(q_sem["pow2"], 1)
                            pool.wait_ge(q_sem["zsil"], TILES // 2)
                            xv = xbc[:, :, 0:DI].rearrange("p t (h d) -> p t h d", h=HEADS)
                            for j in range(TILES):
                                ins = pool.tensor_tensor(yi[:, j, :].rearrange("p (h d) -> p h d", h=HEADS), xv[:, j],
                                                         bt(dp_b[:, :], HD), ALU.mult)
                            ins.then_inc(q_sem["yd"], 1)
                            pool.wait_ge(q_sem["a"], 1)
                            for j in range(TILES):
                                ins = pool.tensor_tensor(xp[:, j, 0:DI].rearrange("p (h d) -> p h d", h=HEADS), xv[:, j],
                                                         bt(dts[:, 4, j, :], HD), ALU.mult)
                            ins.then_inc(q_sem["xp"], 1)
                            pool.wait_ge(q_sem["xp"], 1)
                            pool.wait_ge(q_sem["dec"], 1)
                            for j in range(TILES):
                                ins = pool.tensor_tensor(tmp[:, j * P:(j + 1) * P].rearrange("p (h d) -> p h d", h=HEADS),
                                                         xp[:, j, 0:DI].rearrange("p (h d) -> p h d", h=HEADS),
                                                         bt(dec[:, 1, j, :], HD), ALU.mult)
                            ins.then_inc(q_sem["xpp"], 1)
                        if ssm:
                            pool.wait_ge(scattered, bi * (16 * TILES))

                    @block.tensor
                    def _(pe):
                        if conv:
                            pe.wait_ge(gn_mean, 1)
                            pe.matmul(psum[:, 7, 0:1], pair[:, :], mv[:, 0:1], start=True, stop=True).then_inc(gn_dev, 1)
                            pe.wait_ge(gn_var, 1)
                            pe.matmul(psum[:, 6, 0:1], pair[:, :], mv[:, 3:4], start=True, stop=True).then_inc(gn_dev, 1)
                            pe.wait_ge(xf_done, 1)
                            for g in range(ng):
                                b0 = 3 * (g % 2)
                                if g >= 2:
                                    pe.wait_ge(gx_out, 2 * (g - 1))
                                flat = psum[:, b0:b0 + 2, :].rearrange("p b n -> p (b n)")
                                for k in range(6):
                                    t = 6 * g + k
                                    pe.matmul(flat[:, k * P:(k + 1) * P], xf[:, t * P:(t + 1) * P], wr[:, :],
                                              start=True, stop=True, skip_group_check=True)
                                for k in range(6):
                                    t = 6 * g + k
                                    ins = pe.transpose(psum[:, b0 + 2, k * C:(k + 1) * C], xd[0:C, t * P:(t + 1) * P],
                                                       ident[0:C, 0:C])
                                ins.then_inc(gx_mm, 1)

                        def qk(u):
                            pb, qp = divmod(u, QP)
                            if u >= 2:
                                pe.wait_ge(sq_done, u - 1)
                            for h in (0, 1):
                                q = 2 * qp + h
                                o = psum[:, 2 * (u % 2) + h, 0:PB]
                                pe.matmul(o, st[:, q * P:(q + 1) * P], hh[:, pb * PB:(pb + 1) * PB], start=True, stop=False)
                                ins = pe.matmul(o, st[:, q * P:(q + 1) * P], ll[:, pb * PB:(pb + 1) * PB], start=False,
                                                stop=True)
                            ins.then_inc(qk_done, 1)

                        def av(u):
                            pb, qp = divmod(u, QP)
                            pe.wait_ge(sq_done, u + 1)
                            if qp == 0 and pb >= 1:
                                pe.wait_ge(o_done, pb)
                            for h in (0, 1):
                                ins = pe.matmul(psum[C * h:C * h + C, 4, 0:PB], gt[:, 2 * qp + h, :], scr[:, u % 2, h, :],
                                                start=(qp == 0), stop=(qp == QP - 1))
                            ins.then_inc(av_done, 1)

                        def d_mm(c):
                            pe.wait_ge(at_done, c + 1)
                            if c >= 1:
                                pe.wait_ge(el_done, c)
                            atf = at[:, :, :].rearrange("p h t -> p (h t)")
                            for k in (0, 1):
                                ins = pe.matmul(bank(5 + k), tri_gt[:, :], atf[:, 512 * k:512 * k + 512], start=True, stop=True)
                            ins.then_inc(d_done, 1)

                        def yt_mm(c):
                            pe.wait_ge(m_done, c + 1)
                            if c >= 1:
                                pe.wait_ge(y_done, c)
                            for h in range(HEADS):
                                q, r = h % 4, h // 4
                                ins = pe.matmul(psum[32 * q:32 * q + 32, 7, r * P:(r + 1) * P],
                                                xp[:, c, HD * h:HD * h + 2 * HD], el[:, h, :], start=(r == 0), stop=True,
                                                skip_group_check=True)
                            ins.then_inc(yt_done, 1)

                        def ytt(c):
                            pe.wait_ge(yts_done, c + 1)
                            for r in (0, 1):
                                ins = pe.transpose(psum[:, 7, (2 + r) * P:(3 + r) * P], yts[:, r, :], ident[:, :])
                            ins.then_inc(ytt_done, 1)

                        if conv:
                            pe.wait_ge(st_done, 2)
                            pe.wait_ge(gt_done, 1)
                            qk(0)
                            qk(1)
                        for c in range(TILES + 1):
                            if ssm and c < TILES:
                                d_mm(c)
                            for k in range(UPC):
                                u = UPC * c + k
                                if conv and u < UNITS:
                                    av(u)
                                    if u + 2 < UNITS:
                                        qk(u + 2)
                                if ssm and c >= 1 and k == 0:
                                    yt_mm(c - 1)
                                if ssm and c >= 1 and k == 1:
                                    ytt(c - 1)

                        if ssm:
                            pe.wait_ge(f_sem["yz"], 1)
                            for n, (g, k) in enumerate(GROUPS4):
                                if n == 0 and conv:
                                    pe.wait_ge(sq_done, UNITS)
                                for j in range(g, g + k):
                                    ins = pe.transpose(psum[:, n, (j - g) * P:(j - g + 1) * P], yi[:, j, :], ident[:, :])
                                ins.then_inc(f_sem["yt"], 1)
                            pe.wait_ge(f_sem["yts"], nblk)
                            for n, (g, k) in enumerate(GROUPS4):
                                for j in range(g, g + k):
                                    ins = pe.matmul(psum[:, n, (j - g) * P:(j - g + 1) * P], tmp[:, j * P:(j + 1) * P], wo[:, :],
                                                    start=True, stop=True, skip_group_check=True)
                                ins.then_inc(f_sem["op"], 1)
                            pe.wait_ge(f_sem["t3"], 1)
                            for j in range(TILES // 2):
                                ins = pe.transpose(psum[:, 5 + j // 4, (j % 4) * P:(j % 4 + 1) * P],
                                                   tok3[:, 2 * j:2 * j + 2, :].rearrange("p t c -> p (t c)"), ident[:, :])
                            ins.then_inc(f_sem["tt"], 1)
                            pe.wait_ge(f_sem["tts"], 1)
                            for j in range(TILES // 2):
                                ins = pe.matmul(psum[:, 5, 16 * j:16 * j + 16], big[:, j * P:(j + 1) * P], gwd[:, :],
                                                start=True, stop=True, skip_group_check=True)
                            ins.then_inc(f_sem["lg"], 1)
                            pe.wait_ge(f_sem["oh"], 1)
                            ohf = rt[:, 2].rearrange("p t e -> p (t e)")
                            pe.matmul(psum[:, 6, 0:TILES * E], tri_le[:, :], ohf, start=True, stop=True)
                            pe.matmul(psum[:, 7, 0:TILES * E], ones[:, :], ohf, start=True, stop=True).then_inc(f_sem["rank"], 1)

                        if conv:
                            pe.wait_ge(o_done, NPB)
                            if ssm:
                                pe.wait_ge(f_sem["opo"], nblk)
                            for n, (g, k) in enumerate(GROUPS4):
                                for j in range(g, g + k):
                                    ins = pe.transpose(psum[:, n, (j - g) * P:(j - g + 1) * P], osb[:, j * P:(j + 1) * P],
                                                       ident[:, :])
                                ins.then_inc(q_sem["ot"], 1)
                            pe.wait_ge(q_sem["xn"], 1)
                            pe.wait_ge(q_sem["ots"], nblk)
                            for j in range(TILES // 2):
                                ins = pe.transpose(psum[:, j // 4, (j % 4) * P:(j % 4 + 1) * P],
                                                   xl[:, 2 * j:2 * j + 2, :].rearrange("p t c -> p (t c)"), ident[:, :])
                            ins.then_inc(q_sem["xt"], 1)
                            pe.wait_ge(q_sem["x2a"], 1)
                            pe.wait_ge(q_sem["x2d"], 1)
                            for g in range(TILES // 2):
                                b0 = 2 * (g % 2)
                                if g >= 2:
                                    pe.wait_ge(q_sem["zsil"], g - 1)
                                for h in (0, 1):
                                    o = PAD + (2 * g + h) * P
                                    pe.matmul(psum[:, b0 + h, 0:ZX], x2[:, o:o + P], wa[:, :], start=True, stop=False,
                                              skip_group_check=True)
                                    ins = pe.matmul(psum[:, b0 + h, 0:XBC], x2[:, o - 2:o - 2 + P], wb[:, :], start=False,
                                                    stop=True, skip_group_check=True)
                                ins.then_inc(q_sem["ip"], 1)
                            pe.wait_ge(q_sem["zsil"], TILES // 2)
                            if ssm:
                                pe.wait_ge(f_sem["rank_o"], 1)
                            bcn = 0
                            for w in (0, 1):
                                for n, (g, k) in enumerate(GROUPS4):
                                    if bcn >= 2:
                                        pe.wait_ge(q_sem["bcs"], bcn - 1)
                                    for j in range(g, g + k):
                                        o = DI + NS * w
                                        ins = pe.transpose(psum[0:NS, 4 + bcn % 2, (j - g) * P:(j - g + 1) * P],
                                                           xbc[:, j, o:o + NS], ident[:, :])
                                    ins.then_inc(q_sem["bc"], 1)
                                    bcn += 1
                            pe.wait_ge(q_sem["a"], 1)
                            af = dts[:, 5].rearrange("p t h -> p (t h)")
                            for k, m in enumerate((tri_le, tri_gt, ones)):
                                ins = pe.matmul(psum[:, 6, k * TILES * HEADS:(k + 1) * TILES * HEADS], m[:, :], af, start=True,
                                                stop=True, skip_group_check=True)
                            ins.then_inc(q_sem["cum"], 1)
                            pe.wait_ge(q_sem["bcs"], 2 * nblk)
                            for n, (g, k) in enumerate(GROUPS4):
                                if n >= 2:
                                    pe.wait_ge(q_sem["gm"], n - 1)
                                for j in range(g, g + k):
                                    ins = pe.matmul(psum[:, n % 2, (j - g) * P:(j - g + 1) * P], big[0:NS, j * P:(j + 1) * P],
                                                    big[0:NS, T + j * P:T + (j + 1) * P], start=True, stop=True,
                                                    skip_group_check=True)
                                ins.then_inc(q_sem["g"], 1)
                            pe.wait_ge(q_sem["xpp"], 1)
                            for n, (g, k) in enumerate(GROUPS4):
                                if n >= 2:
                                    pe.wait_ge(q_sem["st"], 4 * (n - 1))
                                for j in range(g, g + k):
                                    ins = pe.matmul(psum[0:NS, 2 + n % 2, (j - g) * P:(j - g + 1) * P], xbc[:, j, DI:DI + NS],
                                                    tmp[:, j * P:(j + 1) * P], start=True, stop=True, skip_group_check=True)
                                ins.then_inc(q_sem["ds"], 1)
                            for n, (g, k) in enumerate(GROUPS4):
                                pe.wait_ge(q_sem["st"], min(g + k, TILES - 1))
                                if n >= 2:
                                    pe.wait_ge(q_sem["ino"], n - 1)
                                for j in range(g, g + k):
                                    ins = pe.matmul(psum[:, 4 + n % 2, (j - g) * P:(j - g + 1) * P],
                                                    big[0:NS, T + j * P:T + (j + 1) * P], states[:, j, :], start=True, stop=True,
                                                    skip_group_check=True)
                                ins.then_inc(q_sem["in"], 1)

                    @block.scalar
                    def _(act):
                        if conv:
                            act.wait_ge(gn_ready, 1)
                            act.activation(hh[:, :], xd[:, :], ACT.Identity, bias=mv[:, 7:8], scale=mv[:, 6:7]).then_inc(hh_done, 1)
                            for g in range(ng):
                                b0 = 3 * (g % 2)
                                act.wait_ge(gx_mm, g + 1)
                                flat = psum[:, b0:b0 + 2, :].rearrange("p b n -> p (b n)")
                                act.activation(tmp[:, 768 * g:768 * g + 768], flat[:, 0:768], ACT.Copy).then_inc(gx_out, 1)
                                act.activation(xtm[:, 6 * g:6 * g + 6, :].rearrange("p t c -> p (t c)"),
                                               psum[:, b0 + 2, 0:6 * C], ACT.Copy).then_inc(gx_out, 1)

                        def relu(u):
                            act.wait_ge(qk_done, u + 1)
                            if u >= 2:
                                act.wait_ge(sq_done, u - 1)
                            act.activation(rel[:, u % 2], psum[:, 2 * (u % 2):2 * (u % 2) + 2, 0:PB], ACT.Relu).then_inc(rel_done, 1)

                        def o_out(pb):
                            act.wait_ge(av_done, QP * (pb + 1))
                            act.activation(osb[:, pb * PB:(pb + 1) * PB], psum[:, 4, 0:PB], ACT.Copy).then_inc(o_done, 1)

                        def exp_d(c):
                            act.wait_ge(d_done, c + 1)
                            if c >= 1:
                                act.wait_ge(yt_done, c)
                            act.activation(el[:, :, :].rearrange("p h t -> p (h t)").rearrange("p (b n) -> p b n", b=2),
                                           psum[:, 5:7, :], ACT.Exp).then_inc(el_done, 1)

                        def yt_out(c):
                            act.wait_ge(yt_done, c + 1)
                            if c >= 1:
                                act.wait_ge(ytt_done, c)
                            act.activation(yts[:, :, :].rearrange("p r t -> p (r t)"), psum[:, 7, 0:2 * P], ACT.Copy)\
                               .then_inc(yts_done, 1)

                        if conv:
                            relu(0)
                            relu(1)
                        for c in range(TILES + 1):
                            for k in range(UPC):
                                u = UPC * c + k
                                if conv and u + 2 < UNITS:
                                    relu(u + 2)
                                if conv and u < UNITS and u % QP == QP - 1:
                                    o_out(u // QP)
                                if ssm and k == 0 and c >= 1:
                                    yt_out(c - 1)
                                if ssm and k == 1 and c < TILES:
                                    exp_d(c)

                        if ssm:
                            act.wait_ge(f_sem["yz"], 1)
                            act.activation(big[:, 0:T], yi[:, :, :].rearrange("p t c -> p (t c)"), ACT.Square)\
                               .then_inc(f_sem["sq"], 1)
                            for n, (g, k) in enumerate(GROUPS4):
                                act.wait_ge(f_sem["yt"], n + 1)
                                act.activation(tmp[:, g * P:(g + k) * P], psum[:, n, 0:k * P], ACT.Copy).then_inc(f_sem["yts"], 1)
                            act.wait_ge(f_sem["c2"], 1)
                            act.activation(big[:, 0:TILES * C], tok3[:, :, :].rearrange("p t c -> p (t c)"), ACT.Square)\
                               .then_inc(f_sem["c2q"], 1)
                            act.wait_ge(f_sem["tt"], 1)
                            flat = psum[:, 5:8, :].rearrange("p b n -> p (b n)")
                            act.activation(big[:, 0:TILES * C], flat[:, 0:TILES * C], ACT.Copy).then_inc(f_sem["tts"], 1)
                            act.wait_ge(f_sem["exp_in"], 1)
                            act.activation(rt[:, 1], rt[:, 0], ACT.Exp).then_inc(f_sem["exp"], 1)
                        if conv:
                            for n, (g, k) in enumerate(GROUPS4):
                                act.wait_ge(q_sem["ot"], n + 1)
                                act.activation(tok1[:, g:g + k, :],
                                               psum[:, n, 0:k * P].rearrange("p (t c) -> p t c", c=P)[:, :, C:P], ACT.Copy)\
                                   .then_inc(q_sem["oth"], 1)
                            act.wait_ge(q_sem["c1"], 1)
                            act.activation(tmp[:, 0:TILES * C], xl[:, :, :].rearrange("p t c -> p (t c)"), ACT.Square)\
                               .then_inc(q_sem["c1q"], 1)
                            act.wait_ge(q_sem["xt"], 1)
                            flat = psum[:, 0:3, :].rearrange("p b n -> p (b n)")
                            ev = x2[:, PAD:PAD + T].rearrange("p (j h t) -> p j h t", h=2, t=P)
                            od = x2[:, PAD + 1:PAD + 1 + T].rearrange("p (j h t) -> p j h t", h=2, t=P)
                            src = flat[0:C, 0:TILES * C].rearrange("p (j t) -> p j t", t=P)
                            act.activation(ev[0:C, :, 0, :], src, ACT.Copy)
                            act.activation(od[C:P, :, 0, :], src, ACT.Copy).then_inc(q_sem["x2a"], 1)
                            for g in range(TILES // 2):
                                b0 = 2 * (g % 2)
                                act.wait_ge(q_sem["pre"], g + 1)
                                act.activation(xbc[:, 2 * g:2 * g + 2, :], xbc[:, 2 * g:2 * g + 2, :], ACT.Silu)
                                act.activation(zs[:, 2 * g:2 * g + 2, :], psum[:, b0:b0 + 2, XBC:XBC + DI], ACT.Silu)\
                                   .then_inc(q_sem["zsil"], 1)
                            act.wait_ge(q_sem["spin"], 1)
                            act.activation(dts[:, 2], dts[:, 1], ACT.Exp).then_inc(q_sem["e"], 1)
                            act.wait_ge(q_sem["u"], 1)
                            act.activation(dts[:, 4], dts[:, 3], ACT.Ln).then_inc(q_sem["ln"], 1)
                            bcn = 0
                            for w in (0, 1):
                                for n, (g, k) in enumerate(GROUPS4):
                                    act.wait_ge(q_sem["bc"], bcn + 1)
                                    act.activation(big[0:NS, w * T + g * P:w * T + (g + k) * P],
                                                   psum[0:NS, 4 + bcn % 2, 0:k * P], ACT.Copy).then_inc(q_sem["bcs"], 1)
                                    bcn += 1
                            act.wait_ge(q_sem["cum"], 1)
                            act.activation(dec[:, :, :, :].rearrange("p k t h -> p (k t h)"), psum[:, 6, 0:3 * TILES * HEADS],
                                           ACT.Exp).then_inc(q_sem["dec"], 1)

                    @block.vector
                    def _(dve):
                        chain = [0]

                        def link(ins):
                            chain[0] += 1
                            ins.then_inc(dve_s, 1)
                            dve.wait_ge(dve_s, chain[0])

                        def wait_chain():
                            dve.wait_ge(dve_s, chain[0])

                        if conv:
                            for k in range(NPB):
                                ins = dve.bn_stats(stats[:, k, :], xd[:, k * PB:(k + 1) * PB])
                            link(ins)
                            link(dve.bn_aggr(mv[:, 0:2], stats[:, :, :]))
                            dve.engine_nop().then_inc(gn_mean, 1)
                            dve.wait_ge(gn_dev, 1)
                            link(dve.tensor_copy(mv[:, 2:3], psum[:, 7, 0:1]))
                            link(dve.tensor_tensor(mv[:, 4:5], mv[:, 0:1], mv[:, 2:3], ALU.subtract))
                            dve.scalar_tensor_tensor(out=mv[:, 3:4], in0=mv[:, 4:5], scalar=mv[:, 4:5], in1=mv[:, 1:2],
                                                     op0=ALU.mult, op1=ALU.add).then_inc(gn_var, 1)
                            dve.wait_ge(gn_dev, 2)
                            dve.wait_ge(gn_var, 1)
                            dve.tensor_scalar(mv[:, 4:5], psum[:, 6, 0:1], 1e-5, None, ALU.add).then_inc(gn_ve, 1)
                            dve.wait_ge(gn_rs, 1)
                            link(dve.tensor_scalar(mv[:, 6:7], mv[:, 5:6], XF_SCALE, None, ALU.mult))
                            dve.scalar_tensor_tensor(out=mv[:, 7:8], in0=mv[:, 2:3], scalar=-1.0, in1=mv[:, 6:7],
                                                     op0=ALU.mult, op1=ALU.mult).then_inc(gn_ready, 1)
                            dve.wait_ge(gn_ready, 1)
                            dve.tensor_scalar(xf, xd[:, :], mv[:, 6:7], mv[:, 7:8], ALU.mult, ALU.add).then_inc(xf_done, 1)
                            dve.wait_ge(xf_done, 1)
                            dve.wait_ge(hh_done, 1)
                            dve.tensor_tensor(ll[:, :], xf, hh[:, :], ALU.subtract).then_inc(ll_done, 1)
                            dve.engine_nop().then_inc(x_free, 2)
                            dve.wait_ge(gx_out, 2 * ng)
                            gx = tmp[:, :].rearrange("p (t c) -> p t c", c=P)
                            link(dve.tensor_tensor(xl[:, :, :], gx[:, :, C:P], gx[:, :, C:P], ALU.mult))
                            link(dve.tensor_reduce(rn2[:, :], xl[:, :, :], AX, ALU.add))
                            link(dve.tensor_scalar(rn2[:, :], rn2[:, :], (1e-8 * XF_SCALE) ** 2, None, ALU.max))
                            link(dve.reciprocal(rn2[:, :], rn2[:, :]))
                            link(dve.tensor_tensor(gt[:, :, :], gx[:, :, 0:C],
                                                   bc_b[:, :].unsqueeze(1).to_broadcast([P, TILES, C]), ALU.add))
                            dve.tensor_tensor(gt[:, :, :], gt[:, :, :], bt(rn2[:, :], C), ALU.mult).then_inc(gt_done, 1)

                        def square(u):
                            dve.wait_ge(rel_done, u + 1)
                            if u >= 2:
                                dve.wait_ge(av_done, u - 1)
                            dve.tensor_tensor(scr[:, u % 2], rel[:, u % 2], psum[:, 2 * (u % 2):2 * (u % 2) + 2, 0:PB],
                                              ALU.mult).then_inc(sq_done, 1)

                        def weights(c):
                            dve.wait_ge(el_done, c + 1)
                            dve.tensor_tensor(el[:, :, :], el[:, :, :], gm[:, c, :].unsqueeze(1).to_broadcast([P, HEADS, P]),
                                              ALU.mult).then_inc(m_done, 1)

                        def y_add(c):
                            dve.wait_ge(ytt_done, c + 1)
                            yv = yi[:, c, :].rearrange("p (h d) -> p h d", h=HEADS)
                            pv = psum[:, 7, 2 * P:4 * P].rearrange("p (h d) -> p h d", d=32)[:, :, 0:HD]
                            dve.tensor_tensor(yv, yv, pv, ALU.add).then_inc(y_done, 1)

                        for c in range(TILES + 1):
                            for k in range(UPC):
                                u = UPC * c + k
                                if conv and u < UNITS:
                                    square(u)
                                if ssm and k == 1 and c < TILES:
                                    weights(c)
                                if ssm and k == UPC - 1 and c >= 1:
                                    y_add(c - 1)

                        def layer_norm(dst, src, s, inv_eps):
                            link(dve.tensor_reduce(col[:, 2, :], src[:, :, :], AX, ALU.add))
                            link(dve.tensor_scalar(col[:, 2, :], col[:, 2, :], 1.0 / C, None, ALU.mult))
                            dve.tensor_tensor(dst[:, :, :], src[:, :, :], bt(col[:, 2, :], C), ALU.subtract).then_inc(s[0], 1)
                            dve.wait_ge(s[1], 1)
                            sq = s[4]
                            link(dve.tensor_reduce(col[:, 7, :], sq[:, 0:TILES * C].rearrange("p (t c) -> p t c", c=C), AX, ALU.add))
                            dve.tensor_scalar(col[:, 3, :], col[:, 7, :], 1.0 / C, inv_eps, ALU.mult, ALU.add).then_inc(s[2], 1)
                            dve.wait_ge(s[3], 1)

                        if ssm:
                            if TILES:
                                dve.wait_ge(y_done, TILES)
                            yf = yi[:, :, :].rearrange("p t c -> p (t c)")
                            dve.tensor_tensor(yf, yf, zs[:, :, :].rearrange("p t c -> p (t c)"), ALU.mult)\
                               .then_inc(f_sem["yz"], 1)
                            dve.wait_ge(f_sem["sq"], 1)
                            link(dve.tensor_reduce(col[:, 1, :], big[:, 0:T].rearrange("p (t c) -> p t c", c=P), AX, ALU.add))
                            dve.tensor_scalar(col[:, 1, :], col[:, 1, :], 1.0 / DI, 1e-5, ALU.mult, ALU.add).then_inc(f_sem["var"], 1)
                            dve.wait_ge(f_sem["pow"], 1)
                            for n, (g, k) in enumerate(GROUPS4):
                                dve.wait_ge(f_sem["op"], n + 1)
                                dve.tensor_tensor(tok2[:, g:g + k, :],
                                                  psum[:, n, 0:k * P].rearrange("p (t c) -> p t c", c=P)[:, :, 0:C],
                                                  bt(col[:, 0, g:g + k], C), ALU.mult).then_inc(f_sem["opo"], 1)
                            dve.wait_ge(f_sem["opo"], nblk)
                            dve.tensor_tensor(tok2[:, :, :], tok2[:, :, :], res[:, :, :], ALU.add).then_inc(f_sem["t2"], 1)
                            dve.wait_ge(f_sem["t2"], 1)
                            layer_norm(tok3, tok2, (f_sem["c2"], f_sem["c2q"], f_sem["var2"], f_sem["pow2"], big), 1e-5)
                            dve.tensor_tensor(tok3[:, :, :], tok3[:, :, :], bt(col[:, 4, :], C), ALU.mult).then_inc(f_sem["t3"], 1)
                            dve.wait_ge(f_sem["lg"], 1)
                            dve.wait_ge(f_sem["t3"], 1)
                            link(dve.tensor_tensor(rt[:, 0], psum[:, 5, 0:TILES * E].rearrange("p (t e) -> p t e", e=E),
                                                   gb_b[:, :].unsqueeze(1).to_broadcast([P, TILES, E]), ALU.add))
                            link(dve.tensor_reduce(col[:, 2, :], rt[:, 0], AX, ALU.max))
                            link(dve.tensor_tensor(rt[:, 0], rt[:, 0], bt(col[:, 2, :], E), ALU.subtract))
                            dve.engine_nop().then_inc(f_sem["exp_in"], 1)
                            link(dve.tensor_scalar(rt[:, 3], rt[:, 0], 0.0, None, ALU.is_ge))
                            link(dve.tensor_tensor(rt[:, 3], rt[:, 3], eights[:, :].unsqueeze(1).to_broadcast([P, TILES, E]),
                                                   ALU.mult))
                            link(dve.tensor_reduce(col[:, 7, :], rt[:, 3], AX, ALU.max))
                            dve.tensor_tensor(rt[:, 2], eights[:, :].unsqueeze(1).to_broadcast([P, TILES, E]),
                                              bt(col[:, 7, :], E), ALU.is_equal).then_inc(f_sem["oh"], 1)
                            dve.wait_ge(f_sem["exp"], 1)
                            link(dve.tensor_reduce(col[:, 2, :], rt[:, 1], AX, ALU.add))
                            link(dve.reciprocal(col[:, 2, :], col[:, 2, :]))
                            dve.wait_ge(f_sem["rank"], 1)
                            link(dve.tensor_copy(rt[:, 4, 0, :], carry[:, :]))
                            tot = psum[:, 7, 0:TILES * E].rearrange("p (t e) -> p t e", e=E)
                            for j in range(1, TILES):
                                link(dve.tensor_tensor(rt[:, 4, j, :], rt[:, 4, j - 1, :], tot[:, j - 1, :], ALU.add))
                            link(dve.tensor_tensor(carry[:, :], rt[:, 4, TILES - 1, :], tot[:, TILES - 1, :], ALU.add))
                            link(dve.tensor_tensor(rt[:, 4], rt[:, 4], psum[:, 6, 0:TILES * E].rearrange("p (t e) -> p t e", e=E),
                                                   ALU.add))
                            dve.engine_nop().then_inc(f_sem["rank_o"], 1)
                            link(dve.tensor_tensor(rt[:, 4], rt[:, 4], rt[:, 2], ALU.mult))
                            link(dve.tensor_reduce(col[:, 1, :], rt[:, 4], AX, ALU.add))
                            link(dve.tensor_scalar(col[:, 1, :], col[:, 1, :], -1.0, None, ALU.add))
                            link(dve.tensor_scalar(col[:, 3, :], col[:, 1, :], float(CAP), None, ALU.is_ge))
                            link(dve.tensor_scalar(col[:, 7, :], col[:, 7, :], -float(STRIDE), float(E * STRIDE), ALU.mult, ALU.add))
                            link(dve.tensor_scalar(col[:, 4, :], col[:, 3, :], -1.0, 1.0, ALU.mult, ALU.add))
                            gs = gain[:, bass.ds((bi - 1) * TILES, TILES)] if not isinstance(bi, int) else \
                                gain[:, (bi - 1) * TILES:bi * TILES]
                            sg = slot_g[:, bass.ds((bi - 1) * TILES, TILES)] if not isinstance(bi, int) else \
                                slot_g[:, (bi - 1) * TILES:bi * TILES]
                            dve.tensor_tensor(gs, col[:, 4, :], col[:, 2, :], ALU.mult)
                            link(dve.tensor_tensor(col[:, 0, :], col[:, 1, :], col[:, 7, :], ALU.add))
                            link(dve.scalar_tensor_tensor(out=col[:, 0, :], in0=col[:, 3, :], scalar=BIG, in1=col[:, 0, :],
                                                          op0=ALU.mult, op1=ALU.add))
                            dve.tensor_copy(slot_s[:, :], col[:, 0, :]).then_inc(f_sem["slot"], 1)
                            link(dve.tensor_scalar(col[:, 1, :], col[:, 1, :], float(CAP - 1), None, ALU.min))
                            link(dve.tensor_tensor(col[:, 1, :], col[:, 1, :], col[:, 7, :], ALU.add))
                            link(dve.tensor_copy(sg, col[:, 1, :]))

                        if conv:
                            for n, (g, k) in enumerate(GROUPS4):
                                dve.wait_ge(q_sem["oth"], n + 1)
                                dve.tensor_tensor(tok1[:, g:g + k, :],
                                                  psum[:, n, 0:k * P].rearrange("p (t c) -> p t c", c=P)[:, :, 0:C],
                                                  tok1[:, g:g + k, :], ALU.add).then_inc(q_sem["ots"], 1)
                            dve.wait_ge(q_sem["ots"], nblk)
                            link(dve.tensor_tensor(tok1[:, :, :], tok1[:, :, :], bt(rn2[:, :], C), ALU.mult))
                            link(dve.tensor_tensor(tok1[:, :, :], tok1[:, :, :], xtm[:, :, :], ALU.add))
                            layer_norm(xl, tok1, (q_sem["c1"], q_sem["c1q"], q_sem["var"], q_sem["pow"], tmp), 1e-5)
                            link(dve.tensor_tensor(xl[:, :, :], xl[:, :, :], bt(col[:, 4, :], C), ALU.mult))
                            link(dve.tensor_tensor(col[:, 5, :], col[:, 4, :], col[:, 4, :], ALU.mult))
                            link(dve.tensor_tensor(col[:, 5, :], col[:, 5, :], col[:, 7, :], ALU.mult))
                            link(dve.tensor_scalar(col[:, 5, :], col[:, 5, :], 1.0 / C, 1.1920929e-07, ALU.mult, ALU.add))
                            dve.engine_nop().then_inc(q_sem["rv"], 1)
                            link(dve.tensor_tensor(res[:, :, :], xl[:, :, :], tok1[:, :, :], ALU.add))
                            dve.wait_ge(q_sem["pow2"], 1)
                            dve.tensor_tensor(xl[:, :, :], xl[:, :, :], bt(col[:, 6, :], C), ALU.mult).then_inc(q_sem["xn"], 1)
                            dve.wait_ge(q_sem["xt"], 1)
                            flat = psum[:, 0:3, :].rearrange("p b n -> p (b n)")
                            ev = x2[:, PAD:PAD + T].rearrange("p (j h t) -> p j h t", h=2, t=P)
                            od = x2[:, PAD + 1:PAD + 1 + T].rearrange("p (j h t) -> p j h t", h=2, t=P)
                            src = flat[C:P, 0:TILES * C].rearrange("p (j t) -> p j t", t=P)
                            dve.tensor_copy(ev[0:C, :, 1, :], src)
                            dve.tensor_copy(od[C:P, :, 1, :], src).then_inc(q_sem["x2d"], 1)
                            for g in range(TILES // 2):
                                b0 = 2 * (g % 2)
                                dve.wait_ge(q_sem["ip"], g + 1)
                                dve.tensor_tensor(xbc[:, 2 * g:2 * g + 2, :], psum[:, b0:b0 + 2, 0:XBC],
                                                  cb_b[:, :].unsqueeze(1).to_broadcast([P, 2, XBC]), ALU.add)
                                dve.tensor_tensor(dts[:, 0, 2 * g:2 * g + 2, :], psum[:, b0:b0 + 2, XBC + DI:ZX],
                                                  dtb_b[:, :].unsqueeze(1).to_broadcast([P, 2, HEADS]), ALU.add)\
                                   .then_inc(q_sem["pre"], 1)
                            dve.wait_ge(q_sem["pre"], TILES // 2)
                            link(dve.tensor_scalar(dts[:, 1], dts[:, 0], -1.0, None, ALU.mult))
                            dve.tensor_tensor(dts[:, 1], dts[:, 1], dts[:, 0], ALU.min).then_inc(q_sem["spin"], 1)
                            dve.wait_ge(q_sem["e"], 1)
                            dve.tensor_scalar(dts[:, 3], dts[:, 2], 1.0, None, ALU.add).then_inc(q_sem["u"], 1)
                            dve.wait_ge(q_sem["u"], 1)
                            link(dve.scalar_tensor_tensor(out=dts[:, 2], in0=dts[:, 3], scalar=-1.0, in1=dts[:, 2],
                                                          op0=ALU.add, op1=ALU.subtract))
                            link(dve.reciprocal(dts[:, 1], dts[:, 3]))
                            link(dve.tensor_tensor(dts[:, 2], dts[:, 2], dts[:, 1], ALU.mult))
                            dve.wait_ge(q_sem["ln"], 1)
                            link(dve.tensor_tensor(dts[:, 4], dts[:, 4], dts[:, 2], ALU.subtract))
                            link(dve.scalar_tensor_tensor(out=dts[:, 4], in0=dts[:, 0], scalar=0.0, in1=dts[:, 4],
                                                          op0=ALU.max, op1=ALU.add))
                            dve.tensor_tensor(dts[:, 5], dts[:, 4], nega_b[:, :].unsqueeze(1).to_broadcast([P, TILES, HEADS]),
                                              ALU.mult).then_inc(q_sem["a"], 1)
                            for n, (g, k) in enumerate(GROUPS4):
                                dve.wait_ge(q_sem["g"], n + 1)
                                dve.tensor_tensor(gm[:, g:g + k, :], psum[:, n % 2, 0:k * P].rearrange("p (t c) -> p t c", c=P),
                                                  tri_le[:, :].unsqueeze(1).to_broadcast([P, k, P]), ALU.mult)\
                                   .then_inc(q_sem["gm"], 1)
                            dve.wait_ge(q_sem["dec"], 1)
                            for j in range(TILES - 1):
                                n, r = divmod(j, 4)
                                dve.wait_ge(q_sem["ds"], n + 1)
                                if j:
                                    dve.wait_ge(q_sem["st"], j)
                                link(dve.tensor_tensor(sdec[:, :].rearrange("n (h d) -> n h d", h=HEADS),
                                                       states[:, j, :].rearrange("n (h d) -> n h d", h=HEADS),
                                                       bt(dec[0:NS, 2, j, :], HD), ALU.mult))
                                dve.tensor_tensor(states[:, j + 1, :], psum[0:NS, 2 + n % 2, r * P:(r + 1) * P], sdec[:, :],
                                                  ALU.add).then_inc(q_sem["st"], 1)
                            dve.wait_ge(q_sem["yd"], 1)
                            dve.wait_ge(q_sem["ds"], nblk)
                            for n, (g, k) in enumerate(GROUPS4):
                                dve.wait_ge(q_sem["in"], n + 1)
                                link(dve.tensor_tensor(tmp[:, g * P:(g + k) * P].rearrange("p (t h d) -> p (t h) d", t=k, h=HEADS),
                                                       psum[:, 4 + n % 2, 0:k * P].rearrange("p (t h d) -> p (t h) d", t=k, h=HEADS),
                                                       bt(dec[:, 0, g:g + k, :].rearrange("p t h -> p (t h)"), HD), ALU.mult))
                                dve.engine_nop().then_inc(q_sem["ino"], 1)
                            yf = yi[:, :, :].rearrange("p t c -> p (t c)")
                            dve.tensor_tensor(yf, yf, tmp[:, :], ALU.add)
                clear()

            iteration(0, True, False, 1 if B > 1 else None)
            with nc.Fori(1, B) as bi:
                iteration(bi, True, True, (bi + 1) % B)
            iteration(B, False, True, None)

        with ExitStack() as c2:
            def sb2(name, shape, dt=F32):
                return c2.enter_context(nc.sbuf_tensor(name, shape, dt))

            names2 = []

            def sem2(name):
                s = c2.enter_context(nc.semaphore(name))
                names2.append(s)
                return s

            NT = FBLK // P
            HT = NT // 2
            w1s = sb2("w1s", [P, 2, FF])
            w2s = sb2("w2s", [P, 2, C])
            xin = sb2("xin", [P, 3, NT, C])
            xt = sb2("xt", [P, 2, HT * P])
            hs = sb2("hs", [P, 2, 2, HT * P])
            ys = sb2("ys", [P, 2, HT * P])
            yo = sb2("yo", [P, 2, NT, C])
            e_y = [c2.enter_context(nc.semaphore(f"e_y{k}")) for k in range(2)]
            EY = [16 * len(range(k, FB, 2)) for k in range(2)]
            e_w, e_yst = sem2("e_w"), sem2("e_yst")
            e_x = [sem2(f"e_x{k}") for k in range(3)]
            e_xt, e_xts, e_h, e_ha, e_hd, e_yt, e_ys, e_ytt, e_yo, e_half = (
                sem2(n) for n in ("e_xt", "e_xts", "e_h", "e_ha", "e_hd", "e_yt", "e_ys", "e_ytt", "e_yo", "e_half"))

            def clear2():
                ids = sorted(s.num for s in names2)
                assert ids == list(range(ids[0], ids[0] + len(ids)))
                nc.all_engine_barrier()
                nc.sync.sem_clear(range(ids[0], ids[-1] + 1))
                nc.all_engine_barrier()

            with nc.Block() as block:
                @block.vector
                def _(dve):
                    dve.memset(w1s[:, :, :], 0.0)
            clear2()

            def b1_e(e, f):
                return b1_c[:, bass.ds(e, 1), f:f + 1].rearrange("p a b -> p (a b)")

            with nc.Fori(0, E) as e:
                with nc.Block() as block:
                    @block.sync
                    def _(sp):
                        for h in (0, 1):
                            sp.dma_start(w1s[C * h:C * h + C, h, :], w1[bass.ds(e, 1), :, :].rearrange("e c f -> (e c) f"))\
                              .then_inc(e_w, 16)
                            sp.dma_start(w2s[:, h, :], w2[bass.ds(e, 1), h * P:(h + 1) * P, :].rearrange("e f c -> (e f) c"))\
                              .then_inc(e_w, 16)
                        for s in range(FB):
                            if s >= 3:
                                sp.wait_ge(e_xt, s - 2)
                            sp.dma_start(xin[:, s % 3], buf_d[bass.ds(e * STRIDE + s * FBLK, FBLK), :]
                                         .rearrange("(p t) c -> p t c", p=P)).then_inc(e_x[s % 3], 16)

                    @block.gpsimd
                    def _(pool):
                        for s in range(FB):
                            pool.wait_ge(e_yo, 2 * (s + 1))
                            pool.dma_start(yb_d[bass.ds(e * STRIDE + s * FBLK, FBLK), :].rearrange("(p t) c -> p t c", p=P),
                                           yo[:, s % 2]).then_inc(e_y[s % 2], 16)
                        for k in (0, 1):
                            pool.wait_ge(e_y[k], e * EY[k] + EY[k])

                    @block.tensor
                    def _(pe):
                        pe.wait_ge(e_w, 64)

                        def x_t(s):
                            pe.wait_ge(e_x[s % 3], 16 * (s // 3 + 1))
                            if s >= 1:
                                pe.wait_ge(e_xts, s)
                            for k in range(HT):
                                ins = pe.transpose(psum[:, 0, k * P:(k + 1) * P],
                                                   xin[:, s % 3, 2 * k:2 * k + 2, :].rearrange("p t c -> p (t c)"), ident[:, :])
                            ins.then_inc(e_xt, 1)

                        def hid(s, par):
                            n = 2 * s + par
                            if par == 0:
                                pe.wait_ge(e_xts, s + 1)
                            if n >= 2:
                                pe.wait_ge(e_ha, n - 1)
                                pe.wait_ge(e_hd, n - 1)
                            for f in (0, 1):
                                ins = pe.matmul(psum[:, 1 + 2 * par + f, 0:HT * P], w1s[:, par, f * P:(f + 1) * P],
                                                xt[:, s % 2, :], start=True, stop=True)
                            ins.then_inc(e_h, 1)

                        def down(s, par):
                            n = 2 * s + par
                            pe.wait_ge(e_ha, n + 1)
                            pe.wait_ge(e_hd, n + 1)
                            if n >= 1:
                                pe.wait_ge(e_ys, n)
                            for f in (0, 1):
                                ins = pe.matmul(psum[C * f:C * f + C, 5, 0:HT * P], w2s[:, f, :], hs[:, par, f, :],
                                                start=True, stop=True)
                            ins.then_inc(e_yt, 1)

                        def y_t(s, par):
                            n = 2 * s + par
                            pe.wait_ge(e_ys, n + 1)
                            if n >= 2:
                                pe.wait_ge(e_yo, n - 1)
                            for k in range(HT):
                                ins = pe.transpose(psum[:, 6 + par, k * P:(k + 1) * P], ys[:, par, k * P:(k + 1) * P], ident[:, :])
                            ins.then_inc(e_ytt, 1)

                        x_t(0)
                        hid(0, 0)
                        for s in range(FB):
                            hid(s, 1)
                            down(s, 0)
                            if s + 1 < FB:
                                x_t(s + 1)
                            y_t(s, 0)
                            down(s, 1)
                            if s + 1 < FB:
                                hid(s + 1, 0)
                            y_t(s, 1)

                    @block.scalar
                    def _(act):
                        def xt_out(s):
                            act.wait_ge(e_xt, s + 1)
                            if s >= 2:
                                act.wait_ge(e_h, 2 * (s - 1))
                            act.activation(xt[:, s % 2, :], psum[:, 0, 0:HT * P], ACT.Copy).then_inc(e_xts, 1)

                        xt_out(0)
                        for s in range(FB):
                            for par in (0, 1):
                                n = 2 * s + par
                                act.wait_ge(e_h, n + 1)
                                if n >= 2:
                                    act.wait_ge(e_yt, n - 1)
                                act.activation(hs[:, par, 0, :], psum[:, 1 + 2 * par, 0:HT * P], ACT.Relu,
                                               bias=b1_e(e, 0)).then_inc(e_ha, 1)
                                if par == 0 and s + 1 < FB:
                                    xt_out(s + 1)
                                act.wait_ge(e_yt, n + 1)
                                if n >= 2:
                                    act.wait_ge(e_ytt, n - 1)
                                act.activation(ys[:, par, :], psum[:, 5, 0:HT * P], ACT.Copy).then_inc(e_ys, 1)

                    @block.vector
                    def _(dve):
                        half_n = [0]

                        def y_out(s, par):
                            n = 2 * s + par
                            if par == 0 and s >= 2:
                                dve.wait_ge(e_y[s % 2], e * EY[s % 2] + 16 * (s // 2))
                            dve.wait_ge(e_ytt, n + 1)
                            pv = psum[:, 6 + par, 0:HT * P].rearrange("p (k c) -> p k c", c=P)
                            dst = yo[:, s % 2, :, :].rearrange("p (k h) c -> p k h c", h=2)[:, :, par, :]
                            dve.tensor_tensor(dst, pv[:, :, 0:C], b2_b[:, bass.ds(e, 1), :].to_broadcast([P, HT, C]), ALU.add)\
                               .then_inc(e_half, 1)
                            dve.wait_ge(e_half, n + 1)
                            dve.tensor_tensor(dst, pv[:, :, C:P], dst, ALU.add).then_inc(e_yo, 1)

                        for s in range(FB):
                            for par in (0, 1):
                                n = 2 * s + par
                                dve.wait_ge(e_h, n + 1)
                                if n >= 2:
                                    dve.wait_ge(e_yt, n - 1)
                                dve.tensor_scalar(hs[:, par, 1, :], psum[:, 2 + 2 * par, 0:HT * P], b1_e(e, 1), 0.0,
                                                  ALU.add, ALU.max).then_inc(e_hd, 1)
                                if n >= 1:
                                    y_out((n - 1) // 2, (n - 1) % 2)
                        y_out(FB - 1, 1)
                clear2()

        with ExitStack() as c3:
            def sb3(name, shape, dt=F32):
                return c3.enter_context(nc.sbuf_tensor(name, shape, dt))

            names3 = []

            def sem3(name):
                s = c3.enter_context(nc.semaphore(name))
                names3.append(s)
                return s

            NB = 4 if B % 4 == 0 else (2 if B % 2 == 0 else 1)
            yg = sb3("yg", [P, 2, TILES, C])
            t2 = sb3("t2", [P, 2, TILES, C])
            msk = sb3("msk", [P, TILES, C], I32)
            slots = sb3("slots", [P, NB * TILES], I32)
            subst = sb3("subst", [P, 3, C])
            of = sb3("of", [P, 2, TILES // 2, P])
            g_y = [c3.enter_context(nc.semaphore(f"g_y{k}")) for k in range(2)]
            GY = [16 * TILES * len(range(k, NB, 2)) for k in range(2)]
            g_t = [sem3(f"g_t{k}") for k in range(2)]
            g_o = [sem3(f"g_o{k}") for k in range(2)]
            g_slots, g_sum, g_tr, g_of, g_ch = (sem3(n) for n in ("g_slots", "g_sum", "g_tr", "g_of", "g_ch"))

            def clear3():
                ids = sorted(s.num for s in names3)
                assert ids == list(range(ids[0], ids[0] + len(ids)))
                nc.all_engine_barrier()
                nc.sync.sem_clear(range(ids[0], ids[-1] + 1))
                nc.all_engine_barrier()

            with nc.Block() as block:
                @block.vector
                def _(dve):
                    for k, v in enumerate((1e4, -1e4, 0.0)):
                        dve.memset(subst[:, k, :], v)
            clear3()
            with nc.Fori(0, B // NB) as it:
                with nc.Block() as block:
                    @block.gpsimd
                    def _(pool):
                        pool.tensor_copy(slots[:, :], slot_g[:, bass.ds(it * (NB * TILES), NB * TILES)]).then_inc(g_slots, 1)
                        pool.wait_ge(g_slots, 1)
                        for n in range(NB):
                            if n >= 2:
                                pool.wait_ge(g_sum, n - 1)
                            for j in range(TILES):
                                pool.indirect_dma_start(
                                    out=yg[:, n % 2, j, :], out_offset=None, in_=yb_d,
                                    in_offset=bass.IndirectOffsetOnAxis(
                                        ap=slots[:, n * TILES + j:n * TILES + j + 1].bitcast(U32), axis=0),
                                ).then_inc(g_y[n % 2], 16)

                    @block.sync
                    def _(sp):
                        for n in range(NB):
                            if n >= 2:
                                sp.wait_ge(g_tr, n - 1)
                            sp.dma_start(t2[:, n % 2], t2_d[bass.ds(it * (NB * T) + n * T, T), :]
                                         .rearrange("(t p) c -> p t c", p=P)).then_inc(g_t[n % 2], 16)

                    @block.scalar
                    def _(act):
                        for n in range(NB):
                            act.wait_ge(g_tr, n + 1)
                            if n >= 2:
                                act.wait_ge(g_o[n % 2], 32 * (n // 2))
                            b0 = 3 * (n % 2)
                            flat = psum[:, b0:b0 + 3, :].rearrange("p b n -> p (b n)")
                            act.activation(of[:, n % 2].rearrange("p j t -> p (j t)"), flat[:, 0:TILES * C], ACT.Copy)\
                               .then_inc(g_of, 1)
                            act.wait_ge(g_of, n + 1)
                            od = out_d[bass.ds(it * NB + n, 1), :, :].rearrange("b c (j h t) -> (b c) j h t", h=2, t=P)
                            for h in (0, 1):
                                act.dma_start(od[:, :, h, :], of[C * h:C * h + C, n % 2]).then_inc(g_o[n % 2], 16)
                        for k in (0, 1):
                            if k < NB:
                                act.wait_ge(g_o[k], 32 * len(range(k, NB, 2)))

                    @block.tensor
                    def _(pe):
                        for n in range(NB):
                            pe.wait_ge(g_sum, n + 1)
                            if n >= 2:
                                pe.wait_ge(g_of, n - 1)
                            for j in range(TILES // 2):
                                ins = pe.transpose(psum[:, 3 * (n % 2) + j // 4, (j % 4) * P:(j % 4 + 1) * P],
                                                   t2[:, n % 2, 2 * j:2 * j + 2, :].rearrange("p t c -> p (t c)"), ident[:, :])
                            ins.then_inc(g_tr, 1)

                    @block.vector
                    def _(dve):
                        chain = [0]

                        def link(ins):
                            chain[0] += 1
                            ins.then_inc(g_ch, 1)
                            dve.wait_ge(g_ch, chain[0])

                        for n in range(NB):
                            y = yg[:, n % 2]
                            dve.wait_ge(g_y[n % 2], it * GY[n % 2] + 16 * TILES * (n // 2 + 1))
                            gv = gain[:, bass.ds(it * (NB * TILES) + n * TILES, TILES)]
                            link(dve.tensor_tensor(y, y, bt(gv, C), ALU.mult))
                            for op, limit, to in ((ALU.is_gt, FLT_MAX, 0), (ALU.is_lt, -FLT_MAX, 1)):
                                link(dve.tensor_scalar(msk[:, :, :], y, limit, None, op))
                                link(dve.copy_predicated(y, msk[:, :, :], subst[:, to:to + 1, :].to_broadcast([P, TILES, C])))
                            link(dve.tensor_tensor(msk[:, :, :], y, y, ALU.not_equal))
                            link(dve.copy_predicated(y, msk[:, :, :], subst[:, 2:3, :].to_broadcast([P, TILES, C])))
                            dve.wait_ge(g_t[n % 2], 16 * (n // 2 + 1))
                            dve.tensor_tensor(t2[:, n % 2], t2[:, n % 2], y, ALU.add).then_inc(g_sum, 1)
                clear3()


_INS = ['x', 'L0_conv_Wc', 'L0_conv_bc', 'L1_attn_W_in', 'L1_attn_conv_w', 'L1_attn_conv_b', 'L1_attn_dt_bias',
        'L1_attn_A_log', 'L1_attn_Dp', 'L1_attn_gnorm_w', 'L1_attn_norm_w', 'L1_attn_W_out', 'L1_ffn_gate_w',
        'L1_ffn_gate_b', 'L1_ffn_w1', 'L1_ffn_b1', 'L1_ffn_w2', 'L1_ffn_b2']


def kernel(**inputs):
    import numpy as _np
    import concourse.bacc as _bacc
    from concourse import mybir as _mybir
    from concourse.bass_utils import run_bass_kernel_spmd as _run

    nc = _bacc.Bacc("TRN2", target_bir_lowering=False, num_devices=1)
    arrays, args = {}, []
    for name in _INS:
        a = _np.ascontiguousarray(inputs[name])
        arrays[f"in_{name}"] = a
        args.append(nc.dram_tensor(f"in_{name}", a.shape, _mybir.dt.from_np(a.dtype), kind="ExternalInput").ap())
    shape = inputs['x'].shape
    args.append(nc.dram_tensor("out_0", shape, _mybir.dt.float32, kind="ExternalOutput").ap())
    build(nc, *args)
    r = _run(nc, [arrays], core_ids=[0])
    return r.results[0]["out_0"]
```

```python
from contextlib import ExitStack

import concourse.bass as bass
from concourse import mybir

F32 = mybir.dt.float32
F16 = mybir.dt.float16
I32 = mybir.dt.int32
U32 = mybir.dt.uint32
ALU = mybir.AluOpType
ACT = mybir.ActivationFunctionType
AX = mybir.AxisListType.X

P = 128
C = 64
HEADS = 8
HD = 16
NS = 16
DI = HEADS * HD
XBC = DI + 2 * NS
ZX = XBC + DI + HEADS
E = 8
FF = 256
XF_SCALE = 256.0
PB = 384
PAD = 2
BIG = 1.0e6
FBLK = 768
FLT_MAX = 3.4028234663852886e38


def build(nc, x, Wc, bc, W_in, conv_w, conv_b, dt_bias, A_log, Dp, gnorm_w, norm_w, W_out,
          gate_w, gate_b, w1, b1, w2, b2, out):
    B = x.shape[0]
    T = x.shape[2] * x.shape[3]
    TILES = T // P
    NPB = T // PB
    QP = TILES // 2
    UNITS = NPB * QP
    UPC = UNITS // TILES
    assert T % PB == 0 and TILES % 2 == 0 and UNITS % TILES == 0
    CAP = max(1, -(-5 * B * T // (4 * E)))
    FB = -(-CAP // FBLK)
    STRIDE = FB * FBLK
    x_d = x.rearrange("b c h w -> b c (h w)")
    out_d = out.rearrange("b c h w -> b c (h w)")

    with ExitStack() as ctx:
        def sb(name, shape, dt=F32):
            return ctx.enter_context(nc.sbuf_tensor(name, shape, dt))

        def sem(name):
            return ctx.enter_context(nc.semaphore(name))

        buf_d = nc.dram_tensor("expert_in", [E * STRIDE, C], F32).ap()
        yb_d = nc.dram_tensor("expert_out", [E * STRIDE, C], F32).ap()
        t2_d = nc.dram_tensor("tokens_mid", [B * T, C], F32).ap()

        ident = sb("ident", [P, P])
        tri_le = sb("tri_le", [P, P])
        tri_gt = sb("tri_gt", [P, P])
        ones = sb("ones", [P, P])
        fold = sb("fold", [P, P])
        pair = sb("pair", [P, P])
        half = sb("half", [P, TILES])
        eights = sb("eights", [P, E])
        wr = sb("wr", [P, P])
        wa = sb("wa", [P, ZX])
        wb = sb("wb", [P, XBC])
        wo = sb("wo", [P, P])
        gwd = sb("gwd", [P, 2 * E])
        bc_b = sb("bc_b", [P, C])
        cb_b = sb("cb_b", [P, XBC])
        dtb_b = sb("dtb_b", [P, HEADS])
        nega_b = sb("nega_b", [P, HEADS])
        dp_b = sb("dp_b", [P, HEADS])
        gb_b = sb("gb_b", [P, E])
        b1_c = sb("b1_c", [P, E, 2])
        carry = sb("carry", [P, E])
        slot_g = sb("slot_g", [P, B * TILES], I32)
        gain = sb("gain", [P, B * TILES])

        psum = ctx.enter_context(nc.psum_tensor("psum", [P, 8, 512], F32))

        def bank(b, w=512):
            return psum[:, b, 0:w]

        with ExitStack() as c0:
            def sb0(name, shape, dt=F32):
                return c0.enter_context(nc.sbuf_tensor(name, shape, dt))
            wci = sb0("wci", [C, C])
            win = sb0("win", [P, 3, C])
            wout = sb0("wout", [C, DI])
            wt = sb0("wt", [P, ZX])
            nw = sb0("nw", [P, 1])
            gw = sb0("gw", [DI, 1])
            cwb = sb0("cwb", [P, XBC, 4])
            al = sb0("al", [P, HEADS])
            zero = sb0("zero", [P, STRIDE * C // P])
            c_load = c0.enter_context(nc.semaphore("c_load"))
            c_pool = c0.enter_context(nc.semaphore("c_pool"))
            c_dve = c0.enter_context(nc.semaphore("c_dve"))
            c_pe = c0.enter_context(nc.semaphore("c_pe"))
            c_act = c0.enter_context(nc.semaphore("c_act"))
            c_zero = c0.enter_context(nc.semaphore("c_zero"))
            with nc.Block() as block:
                loads = [
                    (wci[:, :], Wc), (win[:, 0, :], W_in[0:P, :]), (win[:, 1, :], W_in[P:2 * P, :]),
                    (win[0:ZX - 2 * P, 2, :], W_in[2 * P:ZX, :]), (wout[:, :], W_out),
                    (nw[0:C, :], norm_w.unsqueeze(1)), (nw[C:P, :], norm_w.unsqueeze(1)), (gw[:, :], gnorm_w.unsqueeze(1)),
                    (cwb[:, :, :], conv_w.partition_broadcast(P)), (al[:, :], A_log.partition_broadcast(P)),
                    (bc_b[:, :], bc.partition_broadcast(P)), (cb_b[:, :], conv_b.partition_broadcast(P)),
                    (dtb_b[:, :], dt_bias.partition_broadcast(P)), (dp_b[:, :], Dp.partition_broadcast(P)),
                    (gb_b[:, :], gate_b.partition_broadcast(P)),
                    (gwd[0:C, 0:E], gate_w), (gwd[C:P, E:2 * E], gate_w),
                    (b1_c[:, :, :], b1.rearrange("e (h f) -> f e h", f=P)),
                ]

                @block.sync
                def _(sp):
                    sp.wait_ge(c_pool, 12)
                    with nc.allow_non_contiguous_dma(reason="small constants"):
                        for dst, src in loads:
                            sp.dma_start(dst, src).then_inc(c_load, 16)
                    sp.wait_ge(c_dve, 1)
                    bz = buf_d.rearrange("(n p r) c -> n p (r c)", p=P, n=E)
                    for n in range(E):
                        sp.dma_start(bz[n], zero[:, :]).then_inc(c_zero, 16)
                    sp.wait_ge(c_load, 16 * len(loads))
                    sp.wait_ge(c_zero, 16 * E)

                @block.gpsimd
                def _(pool):
                    for t in (ident, pair):
                        pool.memset(t[:, :], 0.0).then_inc(c_pool, 1)
                    for t in (tri_le, tri_gt, ones):
                        pool.memset(t[:, :], 1.0).then_inc(c_pool, 1)
                    pool.memset(half[:, :], -0.5).then_inc(c_pool, 1)
                    pool.memset(wr[:, :], 0.0).then_inc(c_pool, 1)
                    pool.memset(wa[:, :], 0.0).then_inc(c_pool, 1)
                    pool.memset(wo[:, :], 0.0).then_inc(c_pool, 1)
                    pool.memset(gwd[:, :], 0.0).then_inc(c_pool, 1)
                    pool.memset(carry[:, :], 0.0).then_inc(c_pool, 1)
                    pool.iota(eights[:, :], pattern=[[-1, E]], base=E, channel_multiplier=0,
                              allow_small_or_imprecise_dtypes=True).then_inc(c_pool, 1)
                    pool.wait_ge(c_pool, 12)
                    pool.affine_select(out=ident[:, :], in_=ident[:, :], compare_op=ALU.not_equal, fill=1.0, base=0,
                                       pattern=[[-1, P]], channel_multiplier=1).then_inc(c_pool, 1)
                    pool.affine_select(out=tri_le[:, :], in_=tri_le[:, :], compare_op=ALU.is_ge, fill=0.0, base=0,
                                       pattern=[[1, P]], channel_multiplier=-1).then_inc(c_pool, 1)
                    pool.affine_select(out=tri_gt[:, :], in_=tri_gt[:, :], compare_op=ALU.is_gt, fill=0.0, base=0,
                                       pattern=[[-1, P]], channel_multiplier=1).then_inc(c_pool, 1)
                    pv = pair[:, :].rearrange("p (g k) -> p g k", k=2)
                    pool.affine_select(out=pv, in_=pv, compare_op=ALU.not_equal, fill=0.5, base=0,
                                       pattern=[[-2, P // 2], [0, 2]], channel_multiplier=1).then_inc(c_pool, 1)
                    pool.wait_ge(c_pool, 16)
                    pool.affine_select(out=pv, in_=pv, compare_op=ALU.not_equal, fill=0.5, base=-1,
                                       pattern=[[-2, P // 2], [0, 2]], channel_multiplier=1).then_inc(c_pool, 1)

                @block.tensor
                def _(pe):
                    pe.wait_ge(c_load, 16 * len(loads))
                    pe.wait_ge(c_pool, 17)
                    pe.transpose(psum[0:C, 0, 0:C], wci[:, :], ident[0:C, 0:C])
                    for k, w in ((0, P), (1, P), (2, ZX - 2 * P)):
                        pe.transpose(psum[0:C, 1, k * P:k * P + w], win[0:w, k, :], ident[0:w, 0:w])
                    pe.transpose(psum[0:DI, 2, 0:C], wout[:, :], ident[0:C, 0:C]).then_inc(c_pe, 1)

                @block.scalar
                def _(act):
                    act.wait_ge(c_load, 16 * len(loads))
                    act.activation(al[:, :], al[:, :], ACT.Exp).then_inc(c_act, 1)

                @block.vector
                def _(dve):
                    dve.memset(zero[:, :], 0.0).then_inc(c_dve, 1)
                    dve.wait_ge(c_pe, 1)
                    dve.wait_ge(c_act, 1)
                    dve.tensor_scalar(nega_b[:, :], al[:, :], -1.0, None, ALU.mult)
                    dve.tensor_scalar(wr[0:C, 0:C], psum[0:C, 0, 0:C], 1.0 / XF_SCALE, None, ALU.mult)
                    dve.tensor_copy(wr[0:C, C:P], ident[0:C, 0:C])
                    for h in (0, 1):
                        rows = slice(C * h, C * h + C)
                        for w in (0, 1):
                            dve.tensor_copy(fold[rows, C * w:C * w + C], ident[rows, rows])
                    dve.tensor_scalar(wo[:, 0:C], psum[0:DI, 2, 0:C], gw[:, 0:1], None, ALU.mult)
                    for h in (0, 1):
                        rows = slice(C * h, C * h + C)
                        dve.tensor_scalar(wt[rows, 0:XBC], psum[0:C, 1, DI:DI + XBC], nw[0:C, 0:1], None, ALU.mult)
                        dve.tensor_scalar(wt[rows, XBC:XBC + DI], psum[0:C, 1, 0:DI], nw[0:C, 0:1], None, ALU.mult)
                        dve.tensor_scalar(wt[rows, XBC + DI:ZX], psum[0:C, 1, DI + XBC:ZX], nw[0:C, 0:1], None,
                                          ALU.mult).then_inc(c_dve, 1)
                    dve.wait_ge(c_dve, 3)
                    dve.tensor_copy(wa[0:C, XBC:ZX], wt[0:C, XBC:ZX])
                    for h in (0, 1):
                        rows = slice(C * h, C * h + C)
                        dve.tensor_tensor(wa[rows, 0:XBC], wt[rows, 0:XBC], cwb[rows, :, 3 - h], ALU.mult)
                        dve.tensor_tensor(wb[rows, :], wt[rows, 0:XBC], cwb[rows, :, 1 - h], ALU.mult)

        with ExitStack() as c1:
            def sb1(name, shape, dt=F32):
                return c1.enter_context(nc.sbuf_tensor(name, shape, dt))

            names = []

            def sem1(name):
                s = c1.enter_context(nc.semaphore(name))
                names.append(s)
                return s

            xd = sb1("xd", [P, T])
            xf = sb1("xf", [P, T])
            st = [sb1(f"st{k}", [P, T], F16) for k in range(2)]
            sw = [sb1(f"sw{k}", [P, T], F16) for k in range(2)]
            gt = [sb1(f"gt{k}", [P, TILES, C]) for k in range(2)]
            xtm = [sb1(f"xtm{k}", [P, TILES, C]) for k in range(2)]
            rn2 = [sb1(f"rn2{k}", [P, TILES]) for k in range(2)]
            osb = [sb1(f"osb{k}", [P, T]) for k in range(2)]
            stats = sb1("stats", [P, NPB, 6])
            mv = sb1("mv", [P, 8])
            rel = sb1("rel", [P, 2, 2, PB])
            scr = sb1("scr", [P, 2, 2, PB])
            gx = xd[:, :].rearrange("p (t c) -> p t c", c=P)
            tok1 = sb1("tok1", [P, TILES, C])
            res = sb1("res", [P, TILES, C])
            xl = sb1("xl", [P, TILES, C])
            tok2 = tok1
            col = sb1("col", [P, 8, TILES])
            tmp = sb1("tmp", [P, T])
            x2 = sb1("x2", [P, T + 2 * PAD])
            gm = x2[:, 2 * PAD:2 * PAD + T].rearrange("p (t c) -> p t c", c=P)
            yt_sb = x2[:, 2 * PAD:2 * PAD + T]
            xbc = sb1("xbc", [P, TILES, XBC])
            zs = sb1("zs", [P, TILES, DI])
            dts = sb1("dts", [P, 6, TILES, HEADS])
            dec = sb1("dec", [P, 3, TILES, HEADS])
            xp = sb1("xp", [P, TILES, DI + HD])
            yi = sb1("yi", [P, TILES, DI])
            tok3 = yi[:, 0:TILES // 2, :].rearrange("p t (h c) -> p (t h) c", c=C)
            xn = yi[:, TILES // 2:TILES, :].rearrange("p t (h c) -> p (t h) c", c=C)
            GROUPS4 = [(g, min(4, TILES - g)) for g in range(0, TILES, 4)]
            NG4 = len(GROUPS4)
            GSLOTS = 4 * ((NG4 - 1) // 4) + GROUPS4[-1][1] if NG4 > 4 else 4
            bct = sb1("bct", [P, 2, GSLOTS, P])
            states = sb1("states", [P, GSLOTS, P])
            sdec = sb1("sdec", [P, P])
            at = [sb1(f"at{k}", [P, HEADS, P]) for k in range(2)]
            el = [sb1(f"el{k}", [P, HEADS, P]) for k in range(2)]
            yts = sb1("yts", [P, 2, P])
            rt = sb1("rt", [P, 5, TILES, E])
            slot_s = sb1("slot_s", [P, TILES], I32)

            scattered = c1.enter_context(nc.semaphore("scattered"))
            x_in = sem1("x_in")
            t2_out = sem1("t2_out")
            dve_s = sem1("dve_s")
            S = {n: sem1(n) for n in (
                "qk", "rel", "sq_act", "sq_dve", "av", "o_out",
                "gn_mean", "gn_dev", "gn_var2", "gn_ve", "gn_rs", "gn_ready", "hh_done", "xf_done",
                "split_done", "gsq_done", "rn2_done", "gt_sum", "gt_done",
                "xl_done", "res_done", "cen1", "sq1", "var1", "pow1", "rv1", "powr", "xn_done", "x2_a", "x2_d", "proj_d", "silu_done",
                "skip_done", "sp_in", "sp_exp", "sp_u", "sp_ln", "a_done", "dec_done", "xp_done", "xpp_done", "bct_done",
                "state_done", "inter_d", "yi_base",
                "at_done", "exp_done", "m_done", "yts_done", "y_done",
                "yz_done", "ysq_done", "yvar", "ypow", "yt_out", "t2_done", "cen2", "sq2", "var2", "pow2", "t3_done",
                "t3t", "sh_done", "pexp", "oh_done")}
            full = [sem1(f"bank_full{k}") for k in range(3)]
            free = [sem1(f"bank_free{k}") for k in range(3)]

            def tile_at(j):
                n = j // 4
                return 32 * (n % 4), 4 * (n // 4) + j % 4

            with nc.Block() as block:
                @block.gpsimd
                def _(pool):
                    pool.memset(x2[:, 0:PAD + 1], 0.0)
                    pool.memset(xp[:, :, DI:DI + HD], 0.0)
                    pool.memset(states[0:NS, 0, :], 0.0)
                    pool.memset(tok3, 0.0)
                    pool.memset(slot_s[:, :], int(BIG))

                @block.sync
                def _(sp):
                    sp.dma_start(xd[0:C, :], x_d[0]).then_inc(x_in, 16)
                    sp.dma_start(xd[C:P, :], x_d[0]).then_inc(x_in, 16)
                    sp.wait_ge(x_in, 32)

            def clear():
                ids = sorted(s.num for s in names)
                assert ids == list(range(ids[0], ids[0] + len(ids)))
                nc.all_engine_barrier()
                nc.sync.sem_clear(range(ids[0], ids[-1] + 1))
                nc.all_engine_barrier()

            clear()

            def bt(ap, n):
                return ap.unsqueeze(len(ap.shape)).to_broadcast(list(ap.shape) + [n])

            def mid(ap, n, w):
                return ap.unsqueeze(1).to_broadcast([P, n, w])

            BANKED = {"ot", "xt", "ip", "bc", "cum", "g", "ds", "in", "d", "yt", "yy", "ytr", "op", "tt", "lg", "rk",
                      "gn1", "gn2", "xtr", "gx"}
            XG = [(g, min(8, TILES - g)) for g in range(0, TILES, 8)]
            PAIRS = [(g // 2, n // 2) for g, n in GROUPS4]

            WEIGHT = dict(ot=1.3, sq1=.1, var1=.6, xl1=.8, xn=.3, xt=.6, ip=.1, scat=0, skip=0, sp1=.8, sp2=.8, sp3=.8, bc=.4, xp=0,
                          cum=.5, xpp=0, g=.2, at=0, ds=.2, st=1.3, yib=0, d=.15, yt=.15, yy=.1, m=.3, gn1=.3, gn2=.3, gn4=.3, hh=.3,
                          split=0, xtr=.1, gx=.2, nrm=.2, val=0, yz=0, ysq=.1, ytr=.1, yvar=.4, op=.5, cen2=.7, sq2=.1, var2=.4,
                          xl2=.3, tt=.2, lg=3, rk=5, gn0=2)
            WEIGHT["in"] = .3

            def plan(ssm, pre):
                prep = []
                if pre:
                    prep = [["gn0"], ["gn1"], ["gn2"], ["gn4", "hh"]]
                    prep += [[("split", k)] for k in range(NPB)] + [[] for _ in range(NG4 + 3)]
                    for k in range(len(XG)):
                        prep[4 + k] += [("xtr", k)]
                    for k in range(NG4):
                        prep[4 + len(XG) + k] += [("gx", k)]
                        prep[6 + len(XG) + k] += [("nrm", k)]
                        prep[7 + len(XG) + k] += [("val", k)]
                seq = []
                if ssm:
                    ips = [("ip", k) for k in range(TILES)]
                    scat = [("scat", k) for k in range(TILES)]
                    for k in range(NG4 + 5):
                        if k < NG4:
                            seq += [("ot", k)]
                        if 4 <= k < NG4 + 4:
                            seq += [("xt", k - 4)]
                        if 1 <= k < NG4 + 1:
                            seq += [("sq1", k - 1), ("var1", k - 1)]
                        if 2 <= k < NG4 + 2:
                            seq += [("xl1", k - 2)]
                        if 3 <= k < NG4 + 3:
                            seq += [("xn", k - 3)]
                        if 5 <= k:
                            g, n = GROUPS4[k - 5]
                            for t in range(g, g + n):
                                seq += [ips[t], scat[t]]
                    bcs = [("bc", k) for k in range(2 * NG4)]
                    gs = [("g", k) for k in range(NG4)]
                    seq += ["sp1", "skip"] + bcs[0:4] + ["sp2"] + bcs[4:7] + ["sp3"] + bcs[7:] + ["xp"] + gs[:1] + ["cum"] + gs[1:2]
                    seq += ["xpp"] + gs[2:] + [("at", 0), ("at", 1)]
                    for k in range(NG4 + 1):
                        if k < NG4:
                            seq += [("ds", k), ("st", k)]
                        if k >= 1:
                            seq += [("in", k - 1)]
                    seq += ["yib"]
                    AFTER = [[], ["yz"], ["ysq"], ["ytr"], ["yvar"], ["op"], ["cen2"], ["sq2"], ["var2"], [], ["xl2"], [], ["tt"]]
                    steps = {}
                    for k, (g, n) in enumerate(GROUPS4):
                        for i, names_ in enumerate(AFTER):
                            steps.setdefault(2 * (g + n + 1) + i, []).extend((x, k) for x in names_)
                    for c in range(TILES + 2):
                        if c < TILES:
                            seq += [("d", 2 * c)]
                        if c >= 2:
                            seq += [("yy", c - 2)]
                        if c < TILES:
                            seq += [("d", 2 * c + 1), ("m", c)]
                        seq += steps.pop(2 * c, [])
                        if c + 2 < TILES:
                            seq += [("at", c + 2)]
                        if 1 <= c < TILES + 1:
                            seq += [("yt", c - 1)]
                        seq += steps.pop(2 * c + 1, [])
                        if c >= 2 and prep:
                            seq += prep.pop(0)
                    for i in sorted(steps):
                        seq += steps[i]
                    seq += ["lg", "rk"]
                prep = sum(prep, [])
                seq += prep
                seq = [(x, 0) if isinstance(x, str) else x for x in seq]
                total = sum(WEIGHT[name] for name, _ in seq)
                at_unit = [[] for _ in range(UNITS)]
                turn = {}
                done = 0.0
                for name, k in seq:
                    at_unit[min(UNITS - 1, int(done / total * UNITS))].append((name, k))
                    done += WEIGHT[name]
                    if name in BANKED:
                        turn[name, k] = len(turn)
                busy = [u for u in range(UNITS) if any(name == "d" for name, _ in at_unit[u])]
                on_dve = [u in busy for u in range(UNITS)]
                return at_unit, turn, on_dve

            def scatter(pool, tiles):
                for j in tiles:
                    pool.indirect_dma_start(
                        out=buf_d, out_offset=bass.IndirectOffsetOnAxis(ap=slot_s[:, j:j + 1].bitcast(U32), axis=0),
                        in_=tok3[:, j, :], in_offset=None, bounds_check=E * STRIDE - 1, oob_is_err=False,
                    ).then_inc(scattered, 16)

            def iteration(bi, par, conv, ssm, pre, nxt):
                at_unit, turn, on_dve = plan(ssm, pre)

                def squared(eng, u):
                    if on_dve[u]:
                        eng.wait_ge(S["sq_dve"], sum(on_dve[:u + 1]))
                    else:
                        eng.wait_ge(S["sq_act"], u + 1 - sum(on_dve[:u + 1]))

                me, ot = par, 1 - par

                def bank_of(name, k):
                    n = turn[name, k]
                    return psum[:, 5 + n % 3, :], n % 3, n // 3

                with nc.Block() as block:
                    @block.sync
                    def _(sp):
                        if ssm:
                            sp.wait_ge(S["t2_done"], NG4)
                            sp.dma_start(t2_d[bass.ds((bi - 1) * T, T), :].rearrange("(t p) c -> p t c", p=P),
                                         tok2[:, :, :]).then_inc(t2_out, 16)
                        if pre and nxt is not None:
                            sp.wait_ge(S["gt_done"], NG4)
                            sp.dma_start(xd[0:C, :], x_d[nxt]).then_inc(x_in, 16)
                            sp.dma_start(xd[C:P, :], x_d[nxt]).then_inc(x_in, 16)
                            sp.wait_ge(x_in, 32)
                        if ssm:
                            sp.wait_ge(t2_out, 16)

                    @block.gpsimd
                    def _(pool):
                        xv = xbc[:, :, 0:DI].rearrange("p t (h d) -> p t h d", h=HEADS)

                        def heads(ap):
                            return ap.rearrange("p t (h d) -> p t h d", h=HEADS)

                        def power(dst, src, ready, done, k=0):
                            pool.wait_ge(ready, k + 1)
                            pool.tensor_tensor(dst, src, half[:, 0:dst.shape[-1]], ALU.pow).then_inc(done, 1)

                        def group(k):
                            g, n = GROUPS4[k]
                            return slice(g, g + n)

                        def stage(name, k):
                            if name == "gn2":
                                power(mv[:, 5:6], mv[:, 4:5], S["gn_ve"], S["gn_rs"])
                            elif name == "var1":
                                power(col[:, 4, group(k)], col[:, 3, group(k)], S["var1"], S["pow1"], k)
                            elif name == "xl1":
                                power(col[:, 6, group(k)], col[:, 5, group(k)], S["rv1"], S["powr"], k)
                                pool.wait_ge(S["xl_done"], k + 1)
                                pool.tensor_tensor(res[:, group(k), :], xl[:, group(k), :], tok1[:, group(k), :], ALU.add)\
                                    .then_inc(S["res_done"], 1)
                            elif name == "split":
                                pool.wait_ge(S["xf_done"], 1)
                                pool.wait_ge(S["hh_done"], 2)
                                w = slice(k * PB, (k + 1) * PB)
                                for n, (rows, high, dst) in enumerate(((slice(0, C), st[ot], sw[ot]), (slice(C, P), sw[ot], st[ot]))):
                                    pool.tensor_tensor(dst[rows, w], xf[rows, w], high[rows, w], ALU.subtract)\
                                        .then_inc(S["split_done"], 1)
                                    pool.wait_ge(S["split_done"], 2 * k + n + 1)
                            elif name == "val":
                                w = group(k)
                                pool.wait_ge(S["rn2_done"], k + 1)
                                pool.tensor_tensor(gt[ot][:, w, :], gx[:, w, 0:C], mid(bc_b[:, :], w.stop - w.start, C), ALU.add)\
                                    .then_inc(S["gt_sum"], 1)
                                pool.wait_ge(S["gt_sum"], k + 1)
                                pool.tensor_tensor(gt[ot][:, w, :], gt[ot][:, w, :], bt(rn2[ot][:, w], C), ALU.mult)\
                                    .then_inc(S["gt_done"], 1)
                            elif name == "skip":
                                pool.wait_ge(scattered, bi * (16 * TILES))
                                pool.wait_ge(S["silu_done"], TILES)
                                pool.tensor_tensor(heads(yi[:, :, :]), xv,
                                                   dp_b[:, :].unsqueeze(1).unsqueeze(3).to_broadcast([P, TILES, HEADS, HD]),
                                                   ALU.mult).then_inc(S["skip_done"], 1)
                            elif name == "xp":
                                pool.wait_ge(S["a_done"], 1)
                                pool.tensor_tensor(heads(xp[:, :, 0:DI]), xv, bt(dts[:, 4], HD), ALU.mult)\
                                    .then_inc(S["xp_done"], 1)
                            elif name == "xpp":
                                pool.wait_ge(S["dec_done"], 1)
                                pool.wait_ge(S["xp_done"], 1)
                                pool.tensor_tensor(heads(tmp[:, :].rearrange("p (t c) -> p t c", c=P)), heads(xp[:, :, 0:DI]),
                                                   bt(dec[:, 1], HD), ALU.mult).then_inc(S["xpp_done"], 1)
                            elif name == "at":
                                if k < 2:
                                    pool.wait_ge(S["a_done"], 1)
                                else:
                                    t = turn["d", 2 * k - 3]
                                    pool.wait_ge(full[t % 3], t // 3 + 1)
                                pool.tensor_tensor(at[k % 2][:, :, :], mid(tri_le[:, :], HEADS, P), bt(dts[:, 5, k, :], P), ALU.mult)\
                                    .then_inc(S["at_done"], 1)
                            elif name == "yib":
                                pool.wait_ge(S["inter_d"], NG4)
                                pool.wait_ge(S["skip_done"], 1)
                                yf = yi[:, :, :].rearrange("p t c -> p (t c)")
                                pool.tensor_tensor(yf, yf, tmp[:, :], ALU.add).then_inc(S["yi_base"], 1)
                            elif name == "yz":
                                w = group(k)
                                pool.wait_ge(S["y_done"], w.stop)
                                pool.tensor_tensor(yi[:, w, :], yi[:, w, :], zs[:, w, :], ALU.mult)\
                                    .then_inc(S["yz_done"], 1)
                            elif name == "yvar":
                                power(col[:, 0, group(k)], col[:, 1, group(k)], S["yvar"], S["ypow"], k)
                            elif name == "var2":
                                power(col[:, 4, group(k)], col[:, 3, group(k)], S["var2"], S["pow2"], k)
                            elif name == "scat":
                                scatter(pool, [k])

                        for u in range(UNITS):
                            for name, k in at_unit[u]:
                                stage(name, k)

                    @block.tensor
                    def _(pe):
                        def qk(u):
                            pb, qp = divmod(u, QP)
                            if u >= 2:
                                squared(pe, u - 2)
                            for h in (0, 1):
                                q = 2 * qp + h
                                o = psum[:, 2 * (u % 2) + h, 0:PB]
                                pe.matmul(o, st[me][:, q * P:(q + 1) * P], st[me][:, pb * PB:(pb + 1) * PB], start=True, stop=False)
                                ins = pe.matmul(o, st[me][:, q * P:(q + 1) * P], sw[me][:, pb * PB:(pb + 1) * PB], start=False,
                                                stop=True)
                            ins.then_inc(S["qk"], 1)

                        def av(u):
                            pb, qp = divmod(u, QP)
                            squared(pe, u)
                            if qp == 0 and pb >= 1:
                                pe.wait_ge(S["o_out"], pb)
                            for h in (0, 1):
                                ins = pe.matmul(psum[C * h:C * h + C, 4, 0:PB], gt[me][:, 2 * qp + h, :], scr[:, u % 2, h, :],
                                                start=(qp == 0), stop=(qp == QP - 1))
                            ins.then_inc(S["av"], 1)

                        def mm(o, a, b, **kw):
                            return pe.matmul(o, a, b, start=True, stop=True, skip_group_check=True)

                        def stage(name, k):
                            if name not in BANKED:
                                return
                            bank, b, used = bank_of(name, k)
                            if used:
                                pe.wait_ge(free[b], used)
                            if name == "gn1":
                                pe.wait_ge(S["gn_mean"], 1)
                                ins = mm(bank[:, 0:1], pair[:, :], mv[:, 0:1])
                            elif name == "gn2":
                                pe.wait_ge(S["gn_var2"], 1)
                                ins = mm(bank[:, 0:1], pair[:, :], mv[:, 3:4])
                            elif name == "xtr":
                                g, n = XG[k]
                                for j in range(g, g + n):
                                    ins = pe.transpose(bank[:, (j - g) * C:(j - g + 1) * C], xd[0:C, j * P:(j + 1) * P],
                                                       ident[0:C, 0:C])
                            elif name == "gx":
                                pe.wait_ge(S["xf_done"], 1)
                                g, n = GROUPS4[k]
                                for j in range(g, g + n):
                                    ins = mm(bank[:, (j - g) * P:(j - g + 1) * P], xf[:, j * P:(j + 1) * P], wr[:, :])
                            elif name == "ot":
                                g, n = GROUPS4[k]
                                for j in range(g, g + n):
                                    ins = mm(bank[:, (j - g) * P:(j - g + 1) * P], osb[ot][:, j * P:(j + 1) * P], fold[:, :])
                            elif name == "xt":
                                pe.wait_ge(S["xn_done"], k + 1)
                                g, n = PAIRS[k]
                                for j in range(g, g + n):
                                    ins = pe.transpose(bank[:, (j - g) * P:(j - g + 1) * P],
                                                       xn[:, 2 * j:2 * j + 2, :].rearrange("p t c -> p (t c)"), ident[:, :])
                            elif name == "ip":
                                pe.wait_ge(S["x2_a"], k // 4 + 1)
                                pe.wait_ge(S["x2_d"], k // 4 + 1)
                                o = PAD + k * P
                                pe.matmul(bank[:, 0:ZX], x2[:, o:o + P], wa[:, :], start=True, stop=False, skip_group_check=True)
                                ins = pe.matmul(bank[:, 0:XBC], x2[:, o - 2:o - 2 + P], wb[:, :], start=False, stop=True,
                                                skip_group_check=True)
                            elif name == "bc":
                                w, n4 = divmod(k, NG4)
                                g, n = GROUPS4[n4]
                                pe.wait_ge(S["silu_done"], TILES)
                                for j in range(g, g + n):
                                    ins = pe.transpose(bank[0:NS, (j - g) * P:(j - g + 1) * P],
                                                       xbc[:, j, DI + NS * w:DI + NS * w + NS], ident[:, :])
                            elif name == "cum":
                                pe.wait_ge(S["a_done"], 1)
                                af = dts[:, 5].rearrange("p t h -> p (t h)")
                                w = TILES * HEADS
                                for n, m in enumerate((tri_le, tri_gt, ones)):
                                    ins = mm(bank[:, n * w:(n + 1) * w], m[:, :], af)
                            elif name == "g":
                                if k == 0:
                                    pe.wait_ge(S["bct_done"], 2 * NG4)
                                g, n = GROUPS4[k]
                                for j in range(g, g + n):
                                    r, s = tile_at(j)
                                    ins = mm(bank[:, (j - g) * P:(j - g + 1) * P], bct[r:r + NS, 0, s, :], bct[r:r + NS, 1, s, :])
                            elif name == "ds":
                                pe.wait_ge(S["xpp_done"], 1)
                                g, n = GROUPS4[k]
                                for j in range(g, g + n):
                                    ins = mm(bank[0:NS, (j - g) * P:(j - g + 1) * P], xbc[:, j, DI:DI + NS],
                                             tmp[:, j * P:(j + 1) * P])
                            elif name == "in":
                                g, n = GROUPS4[k]
                                if g + n - 1 >= 1:
                                    pe.wait_ge(S["state_done"], g + n - 1)
                                for j in range(g, g + n):
                                    r, s = tile_at(j)
                                    ins = mm(bank[:, (j - g) * P:(j - g + 1) * P], bct[r:r + NS, 1, s, :], states[r:r + NS, s, :])
                            elif name == "d":
                                pe.wait_ge(S["at_done"], k // 2 + 1)
                                atf = at[k // 2 % 2][:, :, :].rearrange("p h t -> p (h t)")
                                ins = mm(bank, tri_gt[:, :], atf[:, 512 * (k % 2):512 * (k % 2) + 512])
                            elif name == "yt":
                                pe.wait_ge(S["m_done"], k + 1)
                                for h in range(HEADS):
                                    q, r = h % 4, h // 4
                                    ins = mm(bank[32 * q:32 * q + 32, r * P:(r + 1) * P], xp[:, k, HD * h:HD * h + 2 * HD],
                                             el[k % 2][:, h, :])
                            elif name == "yy":
                                pe.wait_ge(S["yts_done"], k + 1)
                                for r in (0, 1):
                                    ins = pe.transpose(bank[:, r * P:(r + 1) * P], yts[:, r, :], ident[:, :])
                            elif name == "ytr":
                                pe.wait_ge(S["yz_done"], k + 1)
                                g, n = GROUPS4[k]
                                for j in range(g, g + n):
                                    ins = pe.transpose(bank[:, (j - g) * P:(j - g + 1) * P], yi[:, j, :], ident[:, :])
                            elif name == "op":
                                pe.wait_ge(S["yt_out"], k + 1)
                                g, n = GROUPS4[k]
                                for j in range(g, g + n):
                                    ins = mm(bank[:, (j - g) * P:(j - g + 1) * P], yt_sb[:, j * P:(j + 1) * P], wo[:, :])
                            elif name == "tt":
                                pe.wait_ge(S["t3_done"], k + 1)
                                g, n = PAIRS[k]
                                for j in range(g, g + n):
                                    ins = pe.transpose(bank[:, (j - g) * P:(j - g + 1) * P],
                                                       tok3[:, 2 * j:2 * j + 2, :].rearrange("p t c -> p (t c)"), ident[:, :])
                            elif name == "lg":
                                pe.wait_ge(S["t3t"], NG4)
                                for g, n in PAIRS:
                                    for j in range(g, g + n):
                                        o = (2 * g + n + j - g) * P
                                        ins = mm(bank[:, 2 * E * j:2 * E * j + 2 * E], tmp[:, o:o + P], gwd[:, :])
                            elif name == "rk":
                                pe.wait_ge(S["oh_done"], 1)
                                ohf = rt[:, 2].rearrange("p t e -> p (t e)")
                                w = TILES * E
                                mm(bank[:, 0:w], tri_le[:, :], ohf)
                                ins = mm(bank[:, w:2 * w], ones[:, :], ohf)
                            ins.then_inc(full[b], 1)

                        if conv:
                            qk(0)
                            qk(1)
                        for u in range(UNITS):
                            if u == 0:
                                for name, k in at_unit[u]:
                                    stage(name, k)
                            if conv:
                                av(u)
                                if u + 2 < UNITS:
                                    qk(u + 2)
                            if u > 0:
                                for name, k in at_unit[u]:
                                    stage(name, k)

                    @block.scalar
                    def _(act):
                        def relu(u):
                            act.wait_ge(S["qk"], u + 1)
                            if u >= 2:
                                squared(act, u - 2)
                            act.activation(rel[:, u % 2], psum[:, 2 * (u % 2):2 * (u % 2) + 2, 0:PB], ACT.Relu).then_inc(S["rel"], 1)
                            if not on_dve[u]:
                                act.wait_ge(S["rel"], u + 1)
                                if u >= 2:
                                    act.wait_ge(S["av"], u - 1)
                                act.activation(scr[:, u % 2], rel[:, u % 2], ACT.Square).then_inc(S["sq_act"], 1)

                        def o_out(pb):
                            act.wait_ge(S["av"], QP * (pb + 1))
                            act.activation(osb[me][:, pb * PB:(pb + 1) * PB], psum[:, 4, 0:PB], ACT.Copy).then_inc(S["o_out"], 1)

                        def bank(name, k):
                            ap, b, used = bank_of(name, k)
                            act.wait_ge(full[b], used + 1)
                            return ap, free[b]

                        def stage(name, k):
                            if name == "hh":
                                act.wait_ge(S["gn_ready"], 1)
                                for rows, dst in ((slice(0, C), st[ot]), (slice(C, P), sw[ot])):
                                    act.activation(dst[rows, :], xd[rows, :], ACT.Identity, bias=mv[rows, 7:8], scale=mv[rows, 6:7])\
                                       .then_inc(S["hh_done"], 1)
                            elif name == "xtr":
                                if ssm and k == 0:
                                    act.wait_ge(S["cen1"], NG4)
                                g, n = XG[k]
                                ps, fr = bank(name, k)
                                act.activation(xtm[ot][:, g:g + n, :].rearrange("p t c -> p (t c)"), ps[:, 0:n * C], ACT.Copy)\
                                   .then_inc(fr, 1)
                            elif name == "gx":
                                if k == 0:
                                    act.wait_ge(S["hh_done"], 2)
                                    act.wait_ge(S["xf_done"], 1)
                                g, n = GROUPS4[k]
                                ps, fr = bank(name, k)
                                act.activation(xd[:, g * P:(g + n) * P], ps[:, 0:n * P], ACT.Copy).then_inc(fr, 1)
                            elif name == "sq1":
                                act.wait_ge(S["cen1"], k + 1)
                                g, n = GROUPS4[k]
                                act.activation(tmp[:, g * C:(g + n) * C], xl[:, g:g + n, :].rearrange("p t c -> p (t c)"), ACT.Square)\
                                   .then_inc(S["sq1"], 1)
                            elif name == "xt":
                                g, n = PAIRS[k]
                                ps, _ = bank(name, k)
                                src = ps[0:C, 0:n * P].rearrange("p (j t) -> p j t", t=P)
                                w = slice(PAD + 2 * g * P, PAD + 2 * (g + n) * P)
                                v = slice(PAD + 1 + 2 * g * P, PAD + 1 + 2 * (g + n) * P)
                                act.activation(x2[0:C, w].rearrange("p (j h t) -> p j h t", h=2, t=P)[:, :, 0, :], src, ACT.Copy)
                                act.activation(x2[C:P, v].rearrange("p (j h t) -> p j h t", h=2, t=P)[:, :, 0, :], src, ACT.Copy)\
                                   .then_inc(S["x2_a"], 1)
                            elif name == "nrm":
                                t = turn["gx", k]
                                act.wait_ge(free[t % 3], t // 3 + 1)
                                g, n = GROUPS4[k]
                                act.activation(gt[ot][:, g:g + n, :], gx[:, g:g + n, C:P], ACT.Square).then_inc(S["gsq_done"], 1)
                            elif name == "ip":
                                ps, fr = bank(name, k)
                                act.wait_ge(S["proj_d"], k + 1)
                                act.activation(zs[:, k, :], ps[:, XBC:XBC + DI], ACT.Silu).then_inc(fr, 1)
                                act.activation(xbc[:, k, :], xbc[:, k, :], ACT.Silu).then_inc(S["silu_done"], 1)
                            elif name == "sp1":
                                act.wait_ge(S["sp_in"], 1)
                                act.activation(dts[:, 2], dts[:, 1], ACT.Exp).then_inc(S["sp_exp"], 1)
                            elif name == "sp2":
                                act.wait_ge(S["sp_u"], 1)
                                act.activation(dts[:, 4], dts[:, 3], ACT.Ln).then_inc(S["sp_ln"], 1)
                            elif name == "bc":
                                w, n4 = divmod(k, NG4)
                                g, n = GROUPS4[n4]
                                r, s = tile_at(g)
                                ps, fr = bank(name, k)
                                act.activation(bct[r:r + NS, w, s:s + n, :].rearrange("p t c -> p (t c)"), ps[0:NS, 0:n * P],
                                               ACT.Copy).then_inc(fr, 1)
                                b, used = turn[name, k] % 3, turn[name, k] // 3
                                act.wait_ge(free[b], used + 1)
                                act.sem_inc(S["bct_done"], 1)
                            elif name == "cum":
                                ps, fr = bank(name, k)
                                act.activation(dec[:, :, :, :].rearrange("p k t h -> p (k t h)"), ps[:, 0:3 * TILES * HEADS],
                                               ACT.Exp).then_inc(fr, 1)
                                b, used = turn[name, k] % 3, turn[name, k] // 3
                                act.wait_ge(free[b], used + 1)
                                act.sem_inc(S["dec_done"], 1)
                            elif name == "d":
                                c, hf = divmod(k, 2)
                                ps, fr = bank(name, k)
                                act.activation(el[c % 2][:, 4 * hf:4 * hf + 4, :].rearrange("p h t -> p (h t)"), ps, ACT.Exp)\
                                   .then_inc(fr, 1)
                                if hf:
                                    b, used = turn[name, k] % 3, turn[name, k] // 3
                                    act.wait_ge(free[b], used + 1)
                                    act.sem_inc(S["exp_done"], 1)
                            elif name == "yt":
                                if k >= 1:
                                    act.wait_ge(full[turn["yy", k - 1] % 3], turn["yy", k - 1] // 3 + 1)
                                ps, fr = bank(name, k)
                                act.activation(yts[:, :, :].rearrange("p r t -> p (r t)"), ps[:, 0:2 * P], ACT.Copy).then_inc(fr, 1)
                                b, used = turn[name, k] % 3, turn[name, k] // 3
                                act.wait_ge(free[b], used + 1)
                                act.sem_inc(S["yts_done"], 1)
                            elif name == "ysq":
                                act.wait_ge(S["yz_done"], k + 1)
                                g, n = GROUPS4[k]
                                act.activation(tmp[:, g * P:(g + n) * P], yi[:, g:g + n, :].rearrange("p t c -> p (t c)"), ACT.Square)\
                                   .then_inc(S["ysq_done"], 1)
                            elif name == "ytr":
                                g, n = GROUPS4[k]
                                ps, fr = bank(name, k)
                                act.activation(yt_sb[:, g * P:(g + n) * P], ps[:, 0:n * P], ACT.Copy).then_inc(fr, 1)
                                b, used = turn[name, k] % 3, turn[name, k] // 3
                                act.wait_ge(free[b], used + 1)
                                act.sem_inc(S["yt_out"], 1)
                            elif name == "sq2":
                                act.wait_ge(S["cen2"], k + 1)
                                g, n = GROUPS4[k]
                                act.activation(tmp[:, g * P:g * P + n * C], tok3[:, g:g + n, :].rearrange("p t c -> p (t c)"), ACT.Square)\
                                   .then_inc(S["sq2"], 1)
                            elif name == "tt":
                                g, n = PAIRS[k]
                                ps, fr = bank(name, k)
                                act.activation(tmp[:, (2 * g + n) * P:(2 * g + 2 * n) * P], ps[:, 0:n * P], ACT.Copy).then_inc(fr, 1)
                                b, used = turn[name, k] % 3, turn[name, k] // 3
                                act.wait_ge(free[b], used + 1)
                                act.sem_inc(S["t3t"], 1)
                            elif name == "lg":
                                act.wait_ge(S["sh_done"], 1)
                                act.activation(rt[:, 1], rt[:, 0], ACT.Exp).then_inc(S["pexp"], 1)

                        if conv:
                            relu(0)
                            relu(1)
                        for u in range(UNITS):
                            if u == 0:
                                for name, k in at_unit[u]:
                                    stage(name, k)
                            if conv:
                                if u + 2 < UNITS:
                                    relu(u + 2)
                                if u % QP == QP - 1:
                                    o_out(u // QP)
                            if u > 0:
                                for name, k in at_unit[u]:
                                    stage(name, k)

                    @block.vector
                    def _(dve):
                        chain = [0]

                        def link(ins):
                            chain[0] += 1
                            ins.then_inc(dve_s, 1)
                            dve.wait_ge(dve_s, chain[0])

                        def bank(name, k):
                            ap, b, used = bank_of(name, k)
                            dve.wait_ge(full[b], used + 1)
                            return ap, free[b]

                        def square(u):
                            if not on_dve[u]:
                                return
                            dve.wait_ge(S["rel"], u + 1)
                            if u >= 2:
                                dve.wait_ge(S["av"], u - 1)
                            dve.tensor_tensor(scr[:, u % 2], rel[:, u % 2], psum[:, 2 * (u % 2):2 * (u % 2) + 2, 0:PB],
                                              ALU.mult).then_inc(S["sq_dve"], 1)

                        def center(dst, src, w, done):
                            link(dve.tensor_reduce(col[:, 2, w], src[:, w, :], AX, ALU.add))
                            link(dve.tensor_scalar(col[:, 2, w], col[:, 2, w], 1.0 / C, None, ALU.mult))
                            dve.tensor_tensor(dst[:, w, :], src[:, w, :], bt(col[:, 2, w], C), ALU.subtract).then_inc(done, 1)

                        def variance(squares, w, squared, k, done):
                            dve.wait_ge(squared, k + 1)
                            link(dve.tensor_reduce(col[:, 7, w], squares.rearrange("p (t c) -> p t c", c=C), AX, ALU.add))
                            dve.tensor_scalar(col[:, 3, w], col[:, 7, w], 1.0 / C, 1e-5, ALU.mult, ALU.add).then_inc(done, 1)

                        def group(k):
                            g, n = GROUPS4[k]
                            return slice(g, g + n)

                        def three(ap, n, w=P):
                            return ap[:, 0:n * w].rearrange("p (t c) -> p t c", c=w)

                        def stage(name, k):
                            if name == "gn0":
                                for n in range(NPB):
                                    ins = dve.bn_stats(stats[:, n, :], xd[:, n * PB:(n + 1) * PB])
                                link(ins)
                                link(dve.bn_aggr(mv[:, 0:2], stats[:, :, :]))
                                dve.engine_nop().then_inc(S["gn_mean"], 1)
                            elif name == "gn1":
                                ps, fr = bank(name, k)
                                link(dve.tensor_copy(mv[:, 2:3], ps[:, 0:1]))
                                dve.engine_nop().then_inc(fr, 1)
                                link(dve.tensor_tensor(mv[:, 4:5], mv[:, 0:1], mv[:, 2:3], ALU.subtract))
                                link(dve.scalar_tensor_tensor(out=mv[:, 3:4], in0=mv[:, 4:5], scalar=mv[:, 4:5], in1=mv[:, 1:2],
                                                              op0=ALU.mult, op1=ALU.add))
                                dve.engine_nop().then_inc(S["gn_var2"], 1)
                            elif name == "gn2":
                                ps, fr = bank(name, k)
                                link(dve.tensor_scalar(mv[:, 4:5], ps[:, 0:1], 1e-5, None, ALU.add))
                                dve.engine_nop().then_inc(fr, 1)
                                dve.engine_nop().then_inc(S["gn_ve"], 1)
                            elif name == "gn4":
                                dve.wait_ge(S["gn_rs"], 1)
                                link(dve.tensor_scalar(mv[:, 6:7], mv[:, 5:6], XF_SCALE, None, ALU.mult))
                                dve.scalar_tensor_tensor(out=mv[:, 7:8], in0=mv[:, 2:3], scalar=-1.0, in1=mv[:, 6:7],
                                                         op0=ALU.mult, op1=ALU.mult).then_inc(S["gn_ready"], 1)
                            elif name == "hh":
                                dve.wait_ge(S["gn_ready"], 1)
                                dve.tensor_scalar(xf[:, :], xd[:, :], mv[:, 6:7], mv[:, 7:8], ALU.mult, ALU.add)\
                                   .then_inc(S["xf_done"], 1)
                            elif name == "nrm":
                                w = group(k)
                                dve.wait_ge(S["gsq_done"], k + 1)
                                link(dve.tensor_reduce(rn2[ot][:, w], gt[ot][:, w, :], AX, ALU.add))
                                link(dve.tensor_scalar(rn2[ot][:, w], rn2[ot][:, w], (1e-8 * XF_SCALE) ** 2, None, ALU.max))
                                dve.reciprocal(rn2[ot][:, w], rn2[ot][:, w]).then_inc(S["rn2_done"], 1)
                            elif name == "ot":
                                ps, fr = bank(name, k)
                                w = group(k)
                                n = w.stop - w.start
                                dve.tensor_tensor(tok1[:, w, :], three(ps, n)[:, :, 0:C], bt(rn2[ot][:, w], C), ALU.mult)\
                                   .then_inc(fr, 1)
                                dve.wait_ge(fr, turn[name, k] // 3 + 1)
                                link(dve.tensor_tensor(tok1[:, w, :], tok1[:, w, :], xtm[ot][:, w, :], ALU.add))
                                center(xl, tok1, w, S["cen1"])
                            elif name == "var1":
                                w = group(k)
                                variance(tmp[:, C * w.start:C * w.stop], w, S["sq1"], k, S["var1"])
                            elif name == "xl1":
                                w = group(k)
                                dve.wait_ge(S["pow1"], k + 1)
                                link(dve.tensor_tensor(col[:, 5, w], col[:, 4, w], col[:, 4, w], ALU.mult))
                                link(dve.tensor_tensor(col[:, 5, w], col[:, 5, w], col[:, 7, w], ALU.mult))
                                dve.tensor_scalar(col[:, 5, w], col[:, 5, w], 1.0 / C, 1.1920929e-07, ALU.mult, ALU.add)\
                                   .then_inc(S["rv1"], 1)
                                dve.tensor_tensor(xl[:, w, :], xl[:, w, :], bt(col[:, 4, w], C), ALU.mult).then_inc(S["xl_done"], 1)
                            elif name == "xn":
                                w = group(k)
                                dve.wait_ge(S["powr"], k + 1)
                                dve.wait_ge(S["xl_done"], k + 1)
                                dve.tensor_tensor(xn[:, w, :], xl[:, w, :], bt(col[:, 6, w], C), ALU.mult).then_inc(S["xn_done"], 1)
                            elif name == "xt":
                                g, n = PAIRS[k]
                                ps, fr = bank(name, k)
                                dve.wait_ge(S["x2_a"], k + 1)
                                src = ps[C:P, 0:n * P].rearrange("p (j t) -> p j t", t=P)
                                w = slice(PAD + 2 * g * P, PAD + 2 * (g + n) * P)
                                v = slice(PAD + 1 + 2 * g * P, PAD + 1 + 2 * (g + n) * P)
                                dve.tensor_copy(x2[0:C, w].rearrange("p (j h t) -> p j h t", h=2, t=P)[:, :, 1, :], src)
                                link(dve.tensor_copy(x2[C:P, v].rearrange("p (j h t) -> p j h t", h=2, t=P)[:, :, 1, :], src))
                                dve.engine_nop().then_inc(S["x2_d"], 1)
                                dve.engine_nop().then_inc(fr, 1)
                            elif name == "ip":
                                ps, _ = bank(name, k)
                                dve.tensor_tensor(xbc[:, k, :], ps[:, 0:XBC], cb_b[:, :], ALU.add)
                                dve.tensor_tensor(dts[:, 0, k, :], ps[:, XBC + DI:ZX], dtb_b[:, :], ALU.add)\
                                   .then_inc(S["proj_d"], 1)
                            elif name == "sp1":
                                dve.wait_ge(S["proj_d"], TILES)
                                link(dve.tensor_scalar(dts[:, 1], dts[:, 0], -1.0, None, ALU.mult))
                                dve.tensor_tensor(dts[:, 1], dts[:, 1], dts[:, 0], ALU.min).then_inc(S["sp_in"], 1)
                            elif name == "sp2":
                                dve.wait_ge(S["sp_exp"], 1)
                                dve.tensor_scalar(dts[:, 3], dts[:, 2], 1.0, None, ALU.add).then_inc(S["sp_u"], 1)
                                dve.wait_ge(S["sp_u"], 1)
                                link(dve.scalar_tensor_tensor(out=dts[:, 2], in0=dts[:, 3], scalar=-1.0, in1=dts[:, 2],
                                                              op0=ALU.add, op1=ALU.subtract))
                                link(dve.reciprocal(dts[:, 1], dts[:, 3]))
                                link(dve.tensor_tensor(dts[:, 2], dts[:, 2], dts[:, 1], ALU.mult))
                            elif name == "sp3":
                                dve.wait_ge(S["sp_ln"], 1)
                                link(dve.tensor_tensor(dts[:, 4], dts[:, 4], dts[:, 2], ALU.subtract))
                                link(dve.scalar_tensor_tensor(out=dts[:, 4], in0=dts[:, 0], scalar=0.0, in1=dts[:, 4],
                                                              op0=ALU.max, op1=ALU.add))
                                dve.tensor_tensor(dts[:, 5], dts[:, 4], mid(nega_b[:, :], TILES, HEADS), ALU.mult)\
                                   .then_inc(S["a_done"], 1)
                            elif name == "g":
                                g, n = GROUPS4[k]
                                ps, fr = bank(name, k)
                                dve.tensor_tensor(gm[:, g:g + n, :], three(ps, n), mid(tri_le[:, :], n, P), ALU.mult).then_inc(fr, 1)
                                dve.wait_ge(fr, turn[name, k] // 3 + 1)
                            elif name == "st":
                                g, n = GROUPS4[k]
                                ps, fr = bank("ds", k)
                                if k == 0:
                                    dve.wait_ge(S["dec_done"], 1)
                                for j in range(g, min(g + n, TILES - 1)):
                                    r, s = tile_at(j)
                                    r1, s1 = tile_at(j + 1)
                                    if j:
                                        dve.wait_ge(S["state_done"], j)
                                    link(dve.tensor_tensor(sdec[r:r + NS, :].rearrange("n (h d) -> n h d", h=HEADS),
                                                           states[r:r + NS, s, :].rearrange("n (h d) -> n h d", h=HEADS),
                                                           bt(dec[r:r + NS, 2, j, :], HD), ALU.mult))
                                    dve.tensor_tensor(states[r1:r1 + NS, s1, :], ps[0:NS, (j - g) * P:(j - g + 1) * P],
                                                      sdec[r:r + NS, :], ALU.add).then_inc(S["state_done"], 1)
                                dve.wait_ge(S["state_done"], min(g + n, TILES - 1))
                                dve.engine_nop().then_inc(fr, 1)
                            elif name == "in":
                                g, n = GROUPS4[k]
                                ps, fr = bank(name, k)
                                link(dve.tensor_tensor(
                                    tmp[:, g * P:(g + n) * P].rearrange("p (t h d) -> p (t h) d", t=n, h=HEADS),
                                    ps[:, 0:n * P].rearrange("p (t h d) -> p (t h) d", t=n, h=HEADS),
                                    bt(dec[:, 0, g:g + n, :].rearrange("p t h -> p (t h)"), HD), ALU.mult))
                                dve.engine_nop().then_inc(fr, 1)
                                dve.engine_nop().then_inc(S["inter_d"], 1)
                            elif name == "m":
                                dve.wait_ge(S["exp_done"], k + 1)
                                e_ = el[k % 2]
                                dve.tensor_tensor(e_[:, :, :], e_[:, :, :], mid(gm[:, k, :], HEADS, P), ALU.mult)\
                                   .then_inc(S["m_done"], 1)
                            elif name == "yy":
                                if k == 0:
                                    dve.wait_ge(S["yi_base"], 1)
                                ps, fr = bank(name, k)
                                yv = yi[:, k, :].rearrange("p (h d) -> p h d", h=HEADS)
                                dve.tensor_tensor(yv, yv, ps[:, 0:2 * P].rearrange("p (h d) -> p h d", d=32)[:, :, 0:HD], ALU.add)\
                                   .then_inc(S["y_done"], 1)
                                dve.wait_ge(S["y_done"], k + 1)
                                dve.engine_nop().then_inc(fr, 1)
                            elif name == "yvar":
                                w = group(k)
                                dve.wait_ge(S["ysq_done"], k + 1)
                                link(dve.tensor_reduce(col[:, 1, w], three(tmp, TILES)[:, w, :], AX, ALU.add))
                                dve.tensor_scalar(col[:, 1, w], col[:, 1, w], 1.0 / DI, 1e-5, ALU.mult, ALU.add).then_inc(S["yvar"], 1)
                            elif name == "op":
                                if k == 0:
                                    dve.wait_ge(S["res_done"], NG4)
                                dve.wait_ge(S["ypow"], k + 1)
                                w = group(k)
                                ps, fr = bank(name, k)
                                dve.tensor_tensor(tok2[:, w, :], three(ps, w.stop - w.start)[:, :, 0:C], bt(col[:, 0, w], C), ALU.mult)\
                                   .then_inc(fr, 1)
                                dve.wait_ge(fr, turn[name, k] // 3 + 1)
                                dve.tensor_tensor(tok2[:, w, :], tok2[:, w, :], res[:, w, :], ALU.add).then_inc(S["t2_done"], 1)
                            elif name == "cen2":
                                dve.wait_ge(S["t2_done"], k + 1)
                                center(tok3, tok2, group(k), S["cen2"])
                            elif name == "var2":
                                w = group(k)
                                o = w.start * P
                                variance(tmp[:, o:o + (w.stop - w.start) * C], w, S["sq2"], k, S["var2"])
                            elif name == "xl2":
                                w = group(k)
                                dve.wait_ge(S["pow2"], k + 1)
                                dve.tensor_tensor(tok3[:, w, :], tok3[:, w, :], bt(col[:, 4, w], C), ALU.mult).then_inc(S["t3_done"], 1)
                            elif name == "lg":
                                ps, fr = bank(name, k)
                                link(dve.tensor_tensor(rt[:, 0], three(ps, TILES, E), mid(gb_b[:, :], TILES, E), ALU.add))
                                dve.engine_nop().then_inc(fr, 1)
                                link(dve.tensor_reduce(col[:, 2, :], rt[:, 0], AX, ALU.max))
                                link(dve.tensor_tensor(rt[:, 0], rt[:, 0], bt(col[:, 2, :], E), ALU.subtract))
                                dve.engine_nop().then_inc(S["sh_done"], 1)
                                link(dve.tensor_scalar(rt[:, 3], rt[:, 0], 0.0, None, ALU.is_ge))
                                link(dve.tensor_tensor(rt[:, 3], rt[:, 3], mid(eights[:, :], TILES, E), ALU.mult))
                                link(dve.tensor_reduce(col[:, 7, :], rt[:, 3], AX, ALU.max))
                                dve.tensor_tensor(rt[:, 2], mid(eights[:, :], TILES, E), bt(col[:, 7, :], E), ALU.is_equal)\
                                   .then_inc(S["oh_done"], 1)
                            elif name == "rk":
                                dve.wait_ge(S["pexp"], 1)
                                link(dve.tensor_reduce(col[:, 2, :], rt[:, 1], AX, ALU.add))
                                link(dve.reciprocal(col[:, 2, :], col[:, 2, :]))
                                ps, fr = bank(name, k)
                                dve.tensor_copy(rt[:, 4, 0, :], carry[:, :])
                                tot = ps[:, TILES * E:2 * TILES * E].rearrange("p (t e) -> p t e", e=E)
                                link(dve.tensor_copy(rt[:, 4, 1:TILES, :], tot[:, 0:TILES - 1, :]))
                                a, far = 4, 1
                                while far < TILES:
                                    dve.tensor_copy(rt[:, 7 - a, 0:far, :], rt[:, a, 0:far, :])
                                    link(dve.tensor_tensor(rt[:, 7 - a, far:TILES, :], rt[:, a, far:TILES, :],
                                                           rt[:, a, 0:TILES - far, :], ALU.add))
                                    a, far = 7 - a, 2 * far
                                link(dve.tensor_tensor(carry[:, :], rt[:, a, TILES - 1, :], tot[:, TILES - 1, :], ALU.add))
                                link(dve.tensor_tensor(rt[:, 4], rt[:, a], three(ps, TILES, E), ALU.add))
                                dve.engine_nop().then_inc(fr, 1)
                                link(dve.tensor_tensor(rt[:, 4], rt[:, 4], rt[:, 2], ALU.mult))
                                link(dve.tensor_reduce(col[:, 1, :], rt[:, 4], AX, ALU.add))
                                link(dve.tensor_scalar(col[:, 1, :], col[:, 1, :], -1.0, None, ALU.add))
                                link(dve.tensor_scalar(col[:, 3, :], col[:, 1, :], float(CAP), None, ALU.is_ge))
                                link(dve.tensor_scalar(col[:, 7, :], col[:, 7, :], -float(STRIDE), float(E * STRIDE), ALU.mult, ALU.add))
                                link(dve.tensor_tensor(col[:, 0, :], col[:, 1, :], col[:, 7, :], ALU.add))
                                link(dve.scalar_tensor_tensor(out=col[:, 0, :], in0=col[:, 3, :], scalar=BIG, in1=col[:, 0, :],
                                                              op0=ALU.mult, op1=ALU.add))
                                dve.wait_ge(S["yi_base"], 1)
                                dve.tensor_copy(slot_s[:, :], col[:, 0, :])
                                w = bass.ds((bi - 1) * TILES, TILES)
                                link(dve.tensor_scalar(col[:, 4, :], col[:, 3, :], -1.0, 1.0, ALU.mult, ALU.add))
                                dve.tensor_tensor(gain[:, w], col[:, 4, :], col[:, 2, :], ALU.mult)
                                link(dve.tensor_scalar(col[:, 1, :], col[:, 1, :], float(CAP - 1), None, ALU.min))
                                link(dve.tensor_tensor(col[:, 1, :], col[:, 1, :], col[:, 7, :], ALU.add))
                                link(dve.tensor_copy(slot_g[:, w], col[:, 1, :]))

                        if conv:
                            square(0)
                        for u in range(UNITS):
                            if conv and u + 1 < UNITS:
                                square(u + 1)
                            for name, k in at_unit[u]:
                                stage(name, k)
                clear()

            assert B % 2 == 0 and B >= 4
            iteration(-1, 1, False, False, True, 1)
            iteration(0, 0, True, False, True, 2)
            with nc.Fori(1, B - 1, 2) as bi:
                iteration(bi, 1, True, True, True, (bi + 2) % B)
                iteration(bi + 1, 0, True, True, True, (bi + 3) % B)
            iteration(B - 1, 1, True, True, False, None)
            iteration(B, 0, False, True, False, None)
            with nc.Block() as block:
                @block.gpsimd
                def _(pool):
                    scatter(pool, range(TILES))
                    pool.wait_ge(scattered, (B + 1) * 16 * TILES)
            nc.all_engine_barrier()

        with ExitStack() as c2:
            def sb2(name, shape, dt=F32):
                return c2.enter_context(nc.sbuf_tensor(name, shape, dt))

            names2 = []

            def sem2(name):
                s = c2.enter_context(nc.semaphore(name))
                names2.append(s)
                return s

            NT = FBLK // P
            HT = NT // 2
            b2_b = sb2("b2_b", [P, E, C])
            w1s = sb2("w1s", [P, 2, FF])
            w2s = sb2("w2s", [P, 2, C])
            xin = sb2("xin", [P, 3, NT, C])
            xt = sb2("xt", [P, 2, HT * P])
            hs = sb2("hs", [P, 2, 2, HT * P])
            ys = sb2("ys", [P, 2, HT * P])
            yo = sb2("yo", [P, 2, NT, C])
            e_y = [c2.enter_context(nc.semaphore(f"e_y{k}")) for k in range(2)]
            EY = [16 * len(range(k, FB, 2)) for k in range(2)]
            e_w, e_yst = sem2("e_w"), sem2("e_yst")
            e_x = [sem2(f"e_x{k}") for k in range(3)]
            e_xt, e_xts, e_h, e_ha, e_hd, e_yt, e_ys, e_ytt, e_yo, e_half = (
                sem2(n) for n in ("e_xt", "e_xts", "e_h", "e_ha", "e_hd", "e_yt", "e_ys", "e_ytt", "e_yo", "e_half"))

            def clear2():
                ids = sorted(s.num for s in names2)
                assert ids == list(range(ids[0], ids[0] + len(ids)))
                nc.all_engine_barrier()
                nc.sync.sem_clear(range(ids[0], ids[-1] + 1))
                nc.all_engine_barrier()

            with nc.Block() as block:
                @block.vector
                def _(dve):
                    dve.memset(w1s[:, :, :], 0.0)

                @block.sync
                def _(sp):
                    sp.dma_start(b2_b[:, :, :], b2.partition_broadcast(P)).then_inc(e_w, 16)
                    sp.wait_ge(e_w, 16)
            clear2()

            def b1_e(e, f):
                return b1_c[:, bass.ds(e, 1), f:f + 1].rearrange("p a b -> p (a b)")

            with nc.Fori(0, E) as e:
                with nc.Block() as block:
                    @block.sync
                    def _(sp):
                        for h in (0, 1):
                            sp.dma_start(w1s[C * h:C * h + C, h, :], w1[bass.ds(e, 1), :, :].rearrange("e c f -> (e c) f"))\
                              .then_inc(e_w, 16)
                            sp.dma_start(w2s[:, h, :], w2[bass.ds(e, 1), h * P:(h + 1) * P, :].rearrange("e f c -> (e f) c"))\
                              .then_inc(e_w, 16)
                        for s in range(FB):
                            if s >= 3:
                                sp.wait_ge(e_xt, s - 2)
                            sp.dma_start(xin[:, s % 3], buf_d[bass.ds(e * STRIDE + s * FBLK, FBLK), :]
                                         .rearrange("(p t) c -> p t c", p=P)).then_inc(e_x[s % 3], 16)

                    @block.gpsimd
                    def _(pool):
                        for s in range(FB):
                            pool.wait_ge(e_yo, 2 * (s + 1))
                            pool.dma_start(yb_d[bass.ds(e * STRIDE + s * FBLK, FBLK), :].rearrange("(p t) c -> p t c", p=P),
                                           yo[:, s % 2]).then_inc(e_y[s % 2], 16)
                        for k in (0, 1):
                            pool.wait_ge(e_y[k], e * EY[k] + EY[k])

                    @block.tensor
                    def _(pe):
                        pe.wait_ge(e_w, 64)

                        def x_t(s):
                            pe.wait_ge(e_x[s % 3], 16 * (s // 3 + 1))
                            if s >= 1:
                                pe.wait_ge(e_xts, s)
                            for k in range(HT):
                                ins = pe.transpose(psum[:, 0, k * P:(k + 1) * P],
                                                   xin[:, s % 3, 2 * k:2 * k + 2, :].rearrange("p t c -> p (t c)"), ident[:, :])
                            ins.then_inc(e_xt, 1)

                        def hid(s, par):
                            n = 2 * s + par
                            if par == 0:
                                pe.wait_ge(e_xts, s + 1)
                            if n >= 2:
                                pe.wait_ge(e_ha, n - 1)
                                pe.wait_ge(e_hd, n - 1)
                            for f in (0, 1):
                                ins = pe.matmul(psum[:, 1 + 2 * par + f, 0:HT * P], w1s[:, par, f * P:(f + 1) * P],
                                                xt[:, s % 2, :], start=True, stop=True)
                            ins.then_inc(e_h, 1)

                        def down(s, par):
                            n = 2 * s + par
                            pe.wait_ge(e_ha, n + 1)
                            pe.wait_ge(e_hd, n + 1)
                            if n >= 1:
                                pe.wait_ge(e_ys, n)
                            for f in (0, 1):
                                ins = pe.matmul(psum[C * f:C * f + C, 5, 0:HT * P], w2s[:, f, :], hs[:, par, f, :],
                                                start=True, stop=True)
                            ins.then_inc(e_yt, 1)

                        def y_t(s, par):
                            n = 2 * s + par
                            pe.wait_ge(e_ys, n + 1)
                            if n >= 2:
                                pe.wait_ge(e_yo, n - 1)
                            for k in range(HT):
                                ins = pe.transpose(psum[:, 6 + par, k * P:(k + 1) * P], ys[:, par, k * P:(k + 1) * P], ident[:, :])
                            ins.then_inc(e_ytt, 1)

                        x_t(0)
                        hid(0, 0)
                        for s in range(FB):
                            hid(s, 1)
                            down(s, 0)
                            if s + 1 < FB:
                                x_t(s + 1)
                            y_t(s, 0)
                            down(s, 1)
                            if s + 1 < FB:
                                hid(s + 1, 0)
                            y_t(s, 1)

                    @block.scalar
                    def _(act):
                        def xt_out(s):
                            act.wait_ge(e_xt, s + 1)
                            if s >= 2:
                                act.wait_ge(e_h, 2 * (s - 1))
                            act.activation(xt[:, s % 2, :], psum[:, 0, 0:HT * P], ACT.Copy).then_inc(e_xts, 1)

                        xt_out(0)
                        for s in range(FB):
                            for par in (0, 1):
                                n = 2 * s + par
                                act.wait_ge(e_h, n + 1)
                                if n >= 2:
                                    act.wait_ge(e_yt, n - 1)
                                act.activation(hs[:, par, 0, :], psum[:, 1 + 2 * par, 0:HT * P], ACT.Relu,
                                               bias=b1_e(e, 0)).then_inc(e_ha, 1)
                                if par == 0 and s + 1 < FB:
                                    xt_out(s + 1)
                                act.wait_ge(e_yt, n + 1)
                                if n >= 2:
                                    act.wait_ge(e_ytt, n - 1)
                                act.activation(ys[:, par, :], psum[:, 5, 0:HT * P], ACT.Copy).then_inc(e_ys, 1)

                    @block.vector
                    def _(dve):
                        half_n = [0]

                        def y_out(s, par):
                            n = 2 * s + par
                            if par == 0 and s >= 2:
                                dve.wait_ge(e_y[s % 2], e * EY[s % 2] + 16 * (s // 2))
                            dve.wait_ge(e_ytt, n + 1)
                            pv = psum[:, 6 + par, 0:HT * P].rearrange("p (k c) -> p k c", c=P)
                            dst = yo[:, s % 2, :, :].rearrange("p (k h) c -> p k h c", h=2)[:, :, par, :]
                            dve.tensor_tensor(dst, pv[:, :, 0:C], b2_b[:, bass.ds(e, 1), :].to_broadcast([P, HT, C]), ALU.add)\
                               .then_inc(e_half, 1)
                            dve.wait_ge(e_half, n + 1)
                            dve.tensor_tensor(dst, pv[:, :, C:P], dst, ALU.add).then_inc(e_yo, 1)

                        for s in range(FB):
                            for par in (0, 1):
                                n = 2 * s + par
                                dve.wait_ge(e_h, n + 1)
                                if n >= 2:
                                    dve.wait_ge(e_yt, n - 1)
                                dve.tensor_scalar(hs[:, par, 1, :], psum[:, 2 + 2 * par, 0:HT * P], b1_e(e, 1), 0.0,
                                                  ALU.add, ALU.max).then_inc(e_hd, 1)
                                if n >= 1:
                                    y_out((n - 1) // 2, (n - 1) % 2)
                        y_out(FB - 1, 1)
                clear2()

        with ExitStack() as c3:
            def sb3(name, shape, dt=F32):
                return c3.enter_context(nc.sbuf_tensor(name, shape, dt))

            names3 = []

            def sem3(name):
                s = c3.enter_context(nc.semaphore(name))
                names3.append(s)
                return s

            NB = 4 if B % 4 == 0 else (2 if B % 2 == 0 else 1)
            yg = sb3("yg", [P, 2, TILES, C])
            t2 = sb3("t2", [P, 2, TILES, C])
            msk = sb3("msk", [P, TILES, C], I32)
            slots = sb3("slots", [P, NB * TILES], I32)
            subst = sb3("subst", [P, 3, C])
            of = sb3("of", [P, 2, TILES // 2, P])
            g_y = [c3.enter_context(nc.semaphore(f"g_y{k}")) for k in range(2)]
            GY = [16 * TILES * len(range(k, NB, 2)) for k in range(2)]
            g_t = [sem3(f"g_t{k}") for k in range(2)]
            g_o = [sem3(f"g_o{k}") for k in range(2)]
            g_slots, g_sum, g_tr, g_of, g_ch = (sem3(n) for n in ("g_slots", "g_sum", "g_tr", "g_of", "g_ch"))

            def clear3():
                ids = sorted(s.num for s in names3)
                assert ids == list(range(ids[0], ids[0] + len(ids)))
                nc.all_engine_barrier()
                nc.sync.sem_clear(range(ids[0], ids[-1] + 1))
                nc.all_engine_barrier()

            with nc.Block() as block:
                @block.vector
                def _(dve):
                    for k, v in enumerate((1e4, -1e4, 0.0)):
                        dve.memset(subst[:, k, :], v)
            clear3()
            with nc.Fori(0, B // NB) as it:
                with nc.Block() as block:
                    @block.gpsimd
                    def _(pool):
                        pool.tensor_copy(slots[:, :], slot_g[:, bass.ds(it * (NB * TILES), NB * TILES)]).then_inc(g_slots, 1)
                        pool.wait_ge(g_slots, 1)
                        for n in range(NB):
                            if n >= 2:
                                pool.wait_ge(g_sum, n - 1)
                            for j in range(TILES):
                                pool.indirect_dma_start(
                                    out=yg[:, n % 2, j, :], out_offset=None, in_=yb_d,
                                    in_offset=bass.IndirectOffsetOnAxis(
                                        ap=slots[:, n * TILES + j:n * TILES + j + 1].bitcast(U32), axis=0),
                                ).then_inc(g_y[n % 2], 16)

                    @block.sync
                    def _(sp):
                        for n in range(NB):
                            if n >= 2:
                                sp.wait_ge(g_tr, n - 1)
                            sp.dma_start(t2[:, n % 2], t2_d[bass.ds(it * (NB * T) + n * T, T), :]
                                         .rearrange("(t p) c -> p t c", p=P)).then_inc(g_t[n % 2], 16)

                    @block.scalar
                    def _(act):
                        for n in range(NB):
                            act.wait_ge(g_tr, n + 1)
                            if n >= 2:
                                act.wait_ge(g_o[n % 2], 32 * (n // 2))
                            b0 = 3 * (n % 2)
                            flat = psum[:, b0:b0 + 3, :].rearrange("p b n -> p (b n)")
                            act.activation(of[:, n % 2].rearrange("p j t -> p (j t)"), flat[:, 0:TILES * C], ACT.Copy)\
                               .then_inc(g_of, 1)
                            act.wait_ge(g_of, n + 1)
                            od = out_d[bass.ds(it * NB + n, 1), :, :].rearrange("b c (j h t) -> (b c) j h t", h=2, t=P)
                            for h in (0, 1):
                                act.dma_start(od[:, :, h, :], of[C * h:C * h + C, n % 2]).then_inc(g_o[n % 2], 16)
                        for k in (0, 1):
                            if k < NB:
                                act.wait_ge(g_o[k], 32 * len(range(k, NB, 2)))

                    @block.tensor
                    def _(pe):
                        for n in range(NB):
                            pe.wait_ge(g_sum, n + 1)
                            if n >= 2:
                                pe.wait_ge(g_of, n - 1)
                            for j in range(TILES // 2):
                                ins = pe.transpose(psum[:, 3 * (n % 2) + j // 4, (j % 4) * P:(j % 4 + 1) * P],
                                                   t2[:, n % 2, 2 * j:2 * j + 2, :].rearrange("p t c -> p (t c)"), ident[:, :])
                            ins.then_inc(g_tr, 1)

                    @block.vector
                    def _(dve):
                        chain = [0]

                        def link(ins):
                            chain[0] += 1
                            ins.then_inc(g_ch, 1)
                            dve.wait_ge(g_ch, chain[0])

                        for n in range(NB):
                            y = yg[:, n % 2]
                            dve.wait_ge(g_y[n % 2], it * GY[n % 2] + 16 * TILES * (n // 2 + 1))
                            gv = gain[:, bass.ds(it * (NB * TILES) + n * TILES, TILES)]
                            link(dve.tensor_tensor(y, y, bt(gv, C), ALU.mult))
                            for op, limit, to in ((ALU.is_gt, FLT_MAX, 0), (ALU.is_lt, -FLT_MAX, 1)):
                                link(dve.tensor_scalar(msk[:, :, :], y, limit, None, op))
                                link(dve.copy_predicated(y, msk[:, :, :], subst[:, to:to + 1, :].to_broadcast([P, TILES, C])))
                            link(dve.tensor_tensor(msk[:, :, :], y, y, ALU.not_equal))
                            link(dve.copy_predicated(y, msk[:, :, :], subst[:, 2:3, :].to_broadcast([P, TILES, C])))
                            dve.wait_ge(g_t[n % 2], 16 * (n // 2 + 1))
                            dve.tensor_tensor(t2[:, n % 2], t2[:, n % 2], y, ALU.add).then_inc(g_sum, 1)
                clear3()


_INS = ['x', 'L0_conv_Wc', 'L0_conv_bc', 'L1_attn_W_in', 'L1_attn_conv_w', 'L1_attn_conv_b', 'L1_attn_dt_bias',
        'L1_attn_A_log', 'L1_attn_Dp', 'L1_attn_gnorm_w', 'L1_attn_norm_w', 'L1_attn_W_out', 'L1_ffn_gate_w',
        'L1_ffn_gate_b', 'L1_ffn_w1', 'L1_ffn_b1', 'L1_ffn_w2', 'L1_ffn_b2']


def kernel(**inputs):
    import numpy as _np
    import concourse.bacc as _bacc
    from concourse import mybir as _mybir
    from concourse.bass_utils import run_bass_kernel_spmd as _run

    nc = _bacc.Bacc("TRN2", target_bir_lowering=False, num_devices=1)
    arrays, args = {}, []
    for name in _INS:
        a = _np.ascontiguousarray(inputs[name])
        arrays[f"in_{name}"] = a
        args.append(nc.dram_tensor(f"in_{name}", a.shape, _mybir.dt.from_np(a.dtype), kind="ExternalInput").ap())
    shape = inputs['x'].shape
    args.append(nc.dram_tensor("out_0", shape, _mybir.dt.float32, kind="ExternalOutput").ap())
    build(nc, *args)
    r = _run(nc, [arrays], core_ids=[0])
    return r.results[0]["out_0"]
```

```python
from contextlib import ExitStack
from math import gcd

import concourse.bass as bass
from concourse import mybir

F32 = mybir.dt.float32
F16 = mybir.dt.float16
I32 = mybir.dt.int32
U32 = mybir.dt.uint32
ALU = mybir.AluOpType
ACT = mybir.ActivationFunctionType
AX = mybir.AxisListType.X

P = 128
C = 64
HEADS = 8
HD = 16
NS = 16
DI = HEADS * HD
XBC = DI + 2 * NS
ZX = XBC + DI + HEADS
E = 8
FF = 256
XF_SCALE = 256.0
PB = 384
PAD = 2
BIG = 1.0e6
FBLK = 768
FLT_MAX = 3.4028234663852886e38


def build(nc, x, Wc, bc, W_in, conv_w, conv_b, dt_bias, A_log, Dp, gnorm_w, norm_w, W_out,
          gate_w, gate_b, w1, b1, w2, b2, out):
    B = x.shape[0]
    T = x.shape[2] * x.shape[3]
    TILES = T // P
    NPB = T // PB
    QP = TILES // 2
    UNITS = NPB * QP
    assert T % PB == 0 and TILES % 2 == 0
    CAP = max(1, -(-5 * B * T // (4 * E)))
    FB = -(-CAP // FBLK)
    STRIDE = FB * FBLK
    x_d = x.rearrange("b c h w -> b c (h w)")
    out_d = out.rearrange("b c h w -> b c (h w)")

    with ExitStack() as ctx:
        def sb(name, shape, dt=F32):
            return ctx.enter_context(nc.sbuf_tensor(name, shape, dt))

        def sem(name):
            return ctx.enter_context(nc.semaphore(name))

        buf_d = nc.dram_tensor("expert_in", [E * STRIDE, C], F32).ap()
        id_d = nc.dram_tensor("expert_token", [E * STRIDE, 1], I32).ap()
        y_d = nc.dram_tensor("expert_out", [B * T, C], F32).ap()
        t2_d = nc.dram_tensor("tokens_mid", [B * T, C], F32).ap()

        ident = sb("ident", [P, P])
        tri_le = sb("tri_le", [P, P])
        tri_gt = sb("tri_gt", [P, P])
        ones = sb("ones", [P, P])
        fold = sb("fold", [P, P])
        pair = sb("pair", [P, P])
        half = sb("half", [P, TILES])
        eights = sb("eights", [P, E])
        wr = sb("wr", [P, P])
        wa = sb("wa", [P, ZX])
        wb = sb("wb", [P, XBC])
        wo = sb("wo", [P, P])
        gwd = sb("gwd", [P, 2 * E])
        bc_b = sb("bc_b", [P, C])
        cb_b = sb("cb_b", [P, XBC])
        dtb_b = sb("dtb_b", [P, HEADS])
        nega_b = sb("nega_b", [P, HEADS])
        dp_b = sb("dp_b", [P, HEADS])
        gb_b = sb("gb_b", [P, E])
        b1_c = sb("b1_c", [P, E, 2])
        carry = sb("carry", [P, E])
        ZW = gcd(PB, T * C // P)
        zero = sb("zero", [P, ZW])
        nobody = sb("nobody", [P, E * FBLK // P], I32)
        gain = sb("gain", [P, B * TILES])

        psum = ctx.enter_context(nc.psum_tensor("psum", [P, 8, 512], F32))
        filled = sem("filled")
        FILLS = E + 1

        def zeros(eng, d, r0, n):
            return eng.dma_start(d[bass.ds(r0, n), :].rearrange("(p r) c -> p (r c)", p=P).rearrange("p (r c) -> p r c", c=ZW),
                                 zero[:, :].unsqueeze(1).to_broadcast([P, n * C // (P * ZW), ZW]))

        def fill_rows(eng, experts):
            for e in experts:
                zeros(eng, buf_d, e * STRIDE, STRIDE).then_inc(filled, 16)

        with ExitStack() as c0:
            def sb0(name, shape, dt=F32):
                return c0.enter_context(nc.sbuf_tensor(name, shape, dt))
            wci = sb0("wci", [C, C])
            win = sb0("win", [P, 3, C])
            wout = sb0("wout", [C, DI])
            wt = sb0("wt", [P, ZX])
            nw = sb0("nw", [P, 1])
            gw = sb0("gw", [DI, 1])
            cwb = sb0("cwb", [P, XBC, 4])
            al = sb0("al", [P, HEADS])
            c_load = c0.enter_context(nc.semaphore("c_load"))
            c_pool = c0.enter_context(nc.semaphore("c_pool"))
            c_dve = c0.enter_context(nc.semaphore("c_dve"))
            c_pe = c0.enter_context(nc.semaphore("c_pe"))
            c_act = c0.enter_context(nc.semaphore("c_act"))
            with nc.Block() as block:
                loads = [
                    (wci[:, :], Wc), (win[:, 0, :], W_in[0:P, :]), (win[:, 1, :], W_in[P:2 * P, :]),
                    (win[0:ZX - 2 * P, 2, :], W_in[2 * P:ZX, :]), (wout[:, :], W_out),
                    (nw[0:C, :], norm_w.unsqueeze(1)), (nw[C:P, :], norm_w.unsqueeze(1)), (gw[:, :], gnorm_w.unsqueeze(1)),
                    (cwb[:, :, :], conv_w.partition_broadcast(P)), (al[:, :], A_log.partition_broadcast(P)),
                    (bc_b[:, :], bc.partition_broadcast(P)), (cb_b[:, :], conv_b.partition_broadcast(P)),
                    (dtb_b[:, :], dt_bias.partition_broadcast(P)), (dp_b[:, :], Dp.partition_broadcast(P)),
                    (gb_b[:, :], gate_b.partition_broadcast(P)),
                    (gwd[0:C, 0:E], gate_w), (gwd[C:P, E:2 * E], gate_w),
                    (b1_c[:, :, :], b1.rearrange("e (h f) -> f e h", f=P)),
                ]

                @block.sync
                def _(sp):
                    sp.wait_ge(c_pool, 12)
                    with nc.allow_non_contiguous_dma(reason="small constants"):
                        for dst, src in loads:
                            sp.dma_start(dst, src).then_inc(c_load, 16)
                    sp.wait_ge(c_load, 16 * len(loads))

                @block.gpsimd
                def _(pool):
                    for t in (ident, pair):
                        pool.memset(t[:, :], 0.0).then_inc(c_pool, 1)
                    for t in (tri_le, tri_gt, ones):
                        pool.memset(t[:, :], 1.0).then_inc(c_pool, 1)
                    pool.memset(half[:, :], -0.5).then_inc(c_pool, 1)
                    pool.memset(wr[:, :], 0.0).then_inc(c_pool, 1)
                    pool.memset(wa[:, :], 0.0).then_inc(c_pool, 1)
                    pool.memset(wo[:, :], 0.0).then_inc(c_pool, 1)
                    pool.memset(gwd[:, :], 0.0).then_inc(c_pool, 1)
                    pool.memset(carry[:, :], 0.0).then_inc(c_pool, 1)
                    pool.iota(eights[:, :], pattern=[[-1, E]], base=E, channel_multiplier=0,
                              allow_small_or_imprecise_dtypes=True).then_inc(c_pool, 1)
                    pool.wait_ge(c_pool, 12)
                    pool.affine_select(out=ident[:, :], in_=ident[:, :], compare_op=ALU.not_equal, fill=1.0, base=0,
                                       pattern=[[-1, P]], channel_multiplier=1).then_inc(c_pool, 1)
                    pool.affine_select(out=tri_le[:, :], in_=tri_le[:, :], compare_op=ALU.is_ge, fill=0.0, base=0,
                                       pattern=[[1, P]], channel_multiplier=-1).then_inc(c_pool, 1)
                    pool.affine_select(out=tri_gt[:, :], in_=tri_gt[:, :], compare_op=ALU.is_gt, fill=0.0, base=0,
                                       pattern=[[-1, P]], channel_multiplier=1).then_inc(c_pool, 1)
                    pv = pair[:, :].rearrange("p (g k) -> p g k", k=2)
                    pool.affine_select(out=pv, in_=pv, compare_op=ALU.not_equal, fill=0.5, base=0,
                                       pattern=[[-2, P // 2], [0, 2]], channel_multiplier=1).then_inc(c_pool, 1)
                    pool.wait_ge(c_pool, 16)
                    pool.affine_select(out=pv, in_=pv, compare_op=ALU.not_equal, fill=0.5, base=-1,
                                       pattern=[[-2, P // 2], [0, 2]], channel_multiplier=1).then_inc(c_pool, 1)

                @block.tensor
                def _(pe):
                    pe.wait_ge(c_load, 16 * len(loads))
                    pe.wait_ge(c_pool, 17)
                    pe.transpose(psum[0:C, 0, 0:C], wci[:, :], ident[0:C, 0:C])
                    for k, w in ((0, P), (1, P), (2, ZX - 2 * P)):
                        pe.transpose(psum[0:C, 1, k * P:k * P + w], win[0:w, k, :], ident[0:w, 0:w])
                    pe.transpose(psum[0:DI, 2, 0:C], wout[:, :], ident[0:C, 0:C]).then_inc(c_pe, 1)

                @block.scalar
                def _(act):
                    act.wait_ge(c_load, 16 * len(loads))
                    act.activation(al[:, :], al[:, :], ACT.Exp).then_inc(c_act, 1)
                    act.wait_ge(c_dve, 2)
                    w = nobody.shape[1]
                    act.dma_start(id_d.rearrange("(p r w) c -> p r (w c)", p=P, w=w),
                                  nobody[:, :].unsqueeze(1).to_broadcast([P, FB, w])).then_inc(filled, 16)
                    fill_rows(act, range(E // 2))

                @block.vector
                def _(dve):
                    dve.memset(zero[:, :], 0.0).then_inc(c_dve, 1)
                    dve.memset(nobody[:, :], int(BIG)).then_inc(c_dve, 1)
                    dve.wait_ge(c_pe, 1)
                    dve.wait_ge(c_act, 1)
                    dve.tensor_scalar(nega_b[:, :], al[:, :], -1.0, None, ALU.mult)
                    dve.tensor_scalar(wr[0:C, 0:C], psum[0:C, 0, 0:C], 1.0 / XF_SCALE, None, ALU.mult)
                    dve.tensor_copy(wr[0:C, C:P], ident[0:C, 0:C])
                    for h in (0, 1):
                        rows = slice(C * h, C * h + C)
                        for w in (0, 1):
                            dve.tensor_copy(fold[rows, C * w:C * w + C], ident[rows, rows])
                    dve.tensor_scalar(wo[:, 0:C], psum[0:DI, 2, 0:C], gw[:, 0:1], None, ALU.mult)
                    for h in (0, 1):
                        rows = slice(C * h, C * h + C)
                        dve.tensor_scalar(wt[rows, 0:XBC], psum[0:C, 1, DI:DI + XBC], nw[0:C, 0:1], None, ALU.mult)
                        dve.tensor_scalar(wt[rows, XBC:XBC + DI], psum[0:C, 1, 0:DI], nw[0:C, 0:1], None, ALU.mult)
                        dve.tensor_scalar(wt[rows, XBC + DI:ZX], psum[0:C, 1, DI + XBC:ZX], nw[0:C, 0:1], None,
                                          ALU.mult).then_inc(c_dve, 1)
                    dve.wait_ge(c_dve, 4)
                    dve.tensor_copy(wa[0:C, XBC:ZX], wt[0:C, XBC:ZX])
                    for h in (0, 1):
                        rows = slice(C * h, C * h + C)
                        dve.tensor_tensor(wa[rows, 0:XBC], wt[rows, 0:XBC], cwb[rows, :, 3 - h], ALU.mult)
                        dve.tensor_tensor(wb[rows, :], wt[rows, 0:XBC], cwb[rows, :, 1 - h], ALU.mult)

        with ExitStack() as c1:
            def sb1(name, shape, dt=F32):
                return c1.enter_context(nc.sbuf_tensor(name, shape, dt))

            names = []

            def sem1(name):
                s = c1.enter_context(nc.semaphore(name))
                names.append(s)
                return s

            xd = sb1("xd", [P, T])
            xf = sb1("xf", [P, T])
            st = [sb1(f"st{k}", [P, T], F16) for k in range(2)]
            sw = [sb1(f"sw{k}", [P, T], F16) for k in range(2)]
            gt = [sb1(f"gt{k}", [P, TILES, C]) for k in range(2)]
            xtm = [sb1(f"xtm{k}", [P, TILES, C]) for k in range(2)]
            rn2 = [sb1(f"rn2{k}", [P, TILES]) for k in range(2)]
            osb = [sb1(f"osb{k}", [P, T]) for k in range(2)]
            stats = sb1("stats", [P, NPB, 6])
            mv = sb1("mv", [P, 8])
            rel = sb1("rel", [P, 2, 2, PB])
            scr = sb1("scr", [P, 2, 2, PB])
            gx = xd[:, :].rearrange("p (t c) -> p t c", c=P)
            tok1 = sb1("tok1", [P, TILES, C])
            res = sb1("res", [P, TILES, C])
            xl = sb1("xl", [P, TILES, C])
            tok2 = tok1
            col = sb1("col", [P, 8, TILES])
            tmp = sb1("tmp", [P, T])
            x2 = sb1("x2", [P, T + 2 * PAD])
            gm = x2[:, 2 * PAD:2 * PAD + T].rearrange("p (t c) -> p t c", c=P)
            yt_sb = x2[:, 2 * PAD:2 * PAD + T]
            xbc = sb1("xbc", [P, TILES, XBC])
            zs = sb1("zs", [P, TILES, DI])
            dts = sb1("dts", [P, 6, TILES, HEADS])
            dec = sb1("dec", [P, 3, TILES, HEADS])
            xp = sb1("xp", [P, TILES, DI + HD])
            yi = sb1("yi", [P, TILES, DI])
            tok3 = yi[:, 0:TILES // 2, :].rearrange("p t (h c) -> p (t h) c", c=C)
            xn = yi[:, TILES // 2:TILES, :].rearrange("p t (h c) -> p (t h) c", c=C)
            GROUPS4 = [(g, min(4, TILES - g)) for g in range(0, TILES, 4)]
            NG4 = len(GROUPS4)
            b_t = sb1("b_t", [P, NG4, P])
            c_t = sb1("c_t", [P, NG4, 4, P])
            states = sb1("states", [P, NG4, P])
            sdec = sb1("sdec", [P, P])
            at = [sb1(f"at{k}", [P, HEADS, P]) for k in range(2)]
            el = [sb1(f"el{k}", [P, HEADS, P]) for k in range(2)]
            yts = sb1("yts", [P, 2, P])
            rt = sb1("rt", [P, 5, TILES, E])
            slot_s = sb1("slot_s", [P, TILES], I32)
            id_s = sb1("id_s", [P, TILES], I32)
            token = sb1("token", [P, TILES])

            scattered = c1.enter_context(nc.semaphore("scattered"))
            x_in = sem1("x_in")
            t2_out = sem1("t2_out")
            dve_s = sem1("dve_s")
            S = {n: sem1(n) for n in (
                "qk", "rel", "sq_act", "sq_dve", "av", "o_out",
                "gn_mean", "gn_var2", "gn_ve", "gn_rs", "gn_ready", "hh_done", "xf_done",
                "split_done", "gsq_done", "rn2_done", "gt_sum", "gt_done",
                "xl_done", "res_done", "cen1", "sq1", "var1", "pow1", "rv1", "powr", "xn_done", "x2_a", "x2_d", "proj_d", "silu_done",
                "skip_done", "sp_in", "sp_exp", "sp_u", "sp_ln", "a_done", "dec_done", "xp_done", "xpp_done", "bt_done", "ct_done",
                "state_done", "inter_d", "yi_base",
                "at_done", "exp_done", "m_done", "yts_done", "y_done",
                "yz_done", "ysq_done", "yvar", "ypow", "yt_out", "t2_done", "cen2", "sq2", "var2", "pow2", "t3_done",
                "t3t", "sh_done", "pexp", "oh_done")}
            full = [sem1(f"bank_full{k}") for k in range(3)]
            free = [sem1(f"bank_free{k}") for k in range(3)]

            def tile_at(j):
                return 32 * (j % 4), j // 4

            with nc.Block() as block:
                @block.gpsimd
                def _(pool):
                    pool.memset(x2[:, 0:PAD + 1], 0.0)
                    pool.memset(xp[:, :, DI:DI + HD], 0.0)
                    for t in (states[:, :, :], b_t[:, :, :], c_t[:, :, :, :]):
                        pool.memset(t, 0.0)
                    pool.memset(tok3, 0.0)
                    pool.memset(slot_s[:, :], int(BIG))
                    pool.memset(id_s[:, :], 0)
                    pool.iota(token[:, :], pattern=[[P, TILES]], base=0, channel_multiplier=1,
                              allow_small_or_imprecise_dtypes=True)

                @block.sync
                def _(sp):
                    sp.dma_start(xd[0:C, :], x_d[0]).then_inc(x_in, 16)
                    sp.dma_start(xd[C:P, :], x_d[0]).then_inc(x_in, 16)
                    sp.wait_ge(x_in, 32)

            def clear():
                ids = sorted(s.num for s in names)
                assert ids == list(range(ids[0], ids[0] + len(ids)))
                nc.all_engine_barrier()
                nc.sync.sem_clear(range(ids[0], ids[-1] + 1))
                nc.all_engine_barrier()

            clear()

            def bt(ap, n):
                return ap.unsqueeze(len(ap.shape)).to_broadcast(list(ap.shape) + [n])

            def mid(ap, n, w):
                return ap.unsqueeze(1).to_broadcast([P, n, w])

            BANKED = {"ot", "xt", "ip", "bc", "cum", "g", "ds", "in", "d", "yt", "yy", "ytr", "op", "tt", "lg", "rk",
                      "gn1", "gn2", "xtr", "gx"}
            XG = [(g, min(8, TILES - g)) for g in range(0, TILES, 8)]
            PAIRS = [(g // 2, n // 2) for g, n in GROUPS4]

            WEIGHT = dict(ot=1.3, sq1=0.1, var1=0.6, xl1=0.8, xn=0.3, xt=0.6, ip=0.1, scat=0, skip=0, sp1=0.8, sp2=2.362, sp3=0.8,
                          bc=0.5, xp=0, cum=0.85, xpp=0, g=0.2, at=0, ds=0.2, st=1.3, yib=0, d=0.15, yt=0.15, yy=0.1, m=0.09,
                          gn1=0.3, gn2=0.09, gn4=0.312, hh=0.3, split=0, xtr=0.1, gx=0.2, nrm=0.128, val=0, yz=0, ysq=0.1, ytr=0.1,
                          yvar=0.4, op=0.5, cen2=0.7, sq2=0.1, var2=1.05, xl2=0.3, tt=0.2, lg=3, rk=5, gn0=2)
            WEIGHT["in"] = 0.3

            def plan(ssm, pre):
                prep = []
                if pre:
                    prep = [[("gn0", 0)], [("gn0", 1)], ["gn1"], ["gn2"], ["gn4"]] + [[("hh", k)] for k in range(4)]
                    h = len(prep)
                    prep += [[("split", k)] for k in range(NPB)] + [[] for _ in range(NG4 + 3)]
                    for k in range(len(XG)):
                        prep[h + k] += [("xtr", k)]
                    for k in range(NG4):
                        prep[h + len(XG) + k] += [("gx", k)]
                        prep[h + 2 + len(XG) + k] += [("nrm", k)]
                        prep[h + 3 + len(XG) + k] += [("val", k)]

                def next_prep():
                    return prep.pop(0) if prep else []

                seq = []
                if ssm:
                    ips = [("ip", k) for k in range(TILES)]
                    scat = [("scat", k) for k in range(TILES)]
                    for k in range(NG4 + 5):
                        if k < NG4:
                            seq += [("ot", k)]
                        if 4 <= k < NG4 + 4:
                            seq += [("xt", k - 4)]
                        if 1 <= k < NG4 + 1:
                            seq += [("sq1", k - 1), ("var1", k - 1)]
                        if 2 <= k < NG4 + 2:
                            seq += [("xl1", k - 2)]
                        if 3 <= k < NG4 + 3:
                            seq += [("xn", k - 3)]
                        if 5 <= k:
                            g, n = GROUPS4[k - 5]
                            for t in range(g, g + n):
                                seq += [ips[t], scat[t]]
                    seq += ["sp1", "skip", ("bc", 0), ("bc", 1), "sp2", ("bc", 2), ("bc", 3), "sp3", ("bc", 4), ("xp", 0), ("xp", 1)]
                    for k in range(NG4):
                        seq += [("g", k)] + next_prep()
                        if k == 0:
                            seq += ["cum"]
                        seq += [("xp", k + 2)] * (k + 2 < NG4) + [("xpp", k - 1)] * (k > 0)
                    seq += [("xpp", NG4 - 1), ("at", 0), ("at", 1)]
                    for k in range(NG4 + 1):
                        if k < NG4:
                            seq += [("ds", k), ("st", k)] + next_prep()
                        if k >= 1:
                            seq += [("in", k - 1)]
                    seq += ["yib"]
                    AFTER = [[], ["yz"], ["ysq"], ["ytr"], ["yvar"], ["op"], ["cen2"], ["sq2"], ["var2"], [], ["xl2"], [], ["tt"]]
                    steps = {}
                    for k, (g, n) in enumerate(GROUPS4):
                        for i, names_ in enumerate(AFTER):
                            steps.setdefault(2 * (g + n + 1) + i, []).extend((x, k) for x in names_)
                    for c in range(TILES + 2):
                        if c < TILES:
                            seq += [("d", 2 * c)]
                        if c >= 2:
                            seq += [("yy", c - 2)]
                        if c < TILES:
                            seq += [("d", 2 * c + 1), ("m", c)]
                        seq += steps.pop(2 * c, [])
                        if c + 2 < TILES:
                            seq += [("at", c + 2)]
                        if 1 <= c < TILES + 1:
                            seq += [("yt", c - 1)]
                        seq += steps.pop(2 * c + 1, [])
                        if c >= 1:
                            seq += next_prep()
                    for i in sorted(steps):
                        seq += steps[i]
                    seq += ["lg", "rk"]
                prep = sum(prep, [])
                seq += prep
                seq = [(x, 0) if isinstance(x, str) else x for x in seq]

                total = sum(WEIGHT[name] for name, _ in seq)
                at_unit = [[] for _ in range(UNITS)]
                turn = {}
                done = 0.0
                for name, k in seq:
                    at_unit[min(UNITS - 1, int(done / total * UNITS))].append((name, k))
                    done += WEIGHT[name]
                    if name in BANKED:
                        turn[name, k] = len(turn)
                busy = [u for u in range(UNITS) if any(name == "d" for name, _ in at_unit[u])]
                on_dve = [u in busy for u in range(UNITS)]
                return at_unit, turn, on_dve

            def scatter(pool, tiles):
                for j in tiles:
                    for dst, src in ((buf_d, tok3[:, j, :]), (id_d, id_s[:, j:j + 1])):
                        pool.indirect_dma_start(
                            out=dst, out_offset=bass.IndirectOffsetOnAxis(ap=slot_s[:, j:j + 1].bitcast(U32), axis=0),
                            in_=src, in_offset=None, bounds_check=E * STRIDE - 1, oob_is_err=False,
                        ).then_inc(scattered, 16)

            def iteration(bi, par, conv, ssm, pre, nxt):
                at_unit, turn, on_dve = plan(ssm, pre)

                def squared(eng, u):
                    if on_dve[u]:
                        eng.wait_ge(S["sq_dve"], sum(on_dve[:u + 1]))
                    else:
                        eng.wait_ge(S["sq_act"], u + 1 - sum(on_dve[:u + 1]))

                me, ot = par, 1 - par

                def bank_of(name, k):
                    n = turn[name, k]
                    return psum[:, 5 + n % 3, :], n % 3, n // 3

                with nc.Block() as block:
                    @block.sync
                    def _(sp):
                        if conv and not ssm:
                            fill_rows(sp, range(E // 2, E))
                        if ssm:
                            zeros(sp, y_d, (bi - 1) * T, T).then_inc(t2_out, 16)
                            sp.wait_ge(S["t2_done"], NG4)
                            sp.dma_start(t2_d[bass.ds((bi - 1) * T, T), :].rearrange("(t p) c -> p t c", p=P),
                                         tok2[:, :, :]).then_inc(t2_out, 16)
                        if pre and nxt is not None:
                            sp.wait_ge(S["gt_done"], NG4)
                            sp.dma_start(xd[0:C, :], x_d[nxt]).then_inc(x_in, 16)
                            sp.dma_start(xd[C:P, :], x_d[nxt]).then_inc(x_in, 16)
                            sp.wait_ge(x_in, 32)
                        if ssm:
                            sp.wait_ge(t2_out, 32)

                    @block.gpsimd
                    def _(pool):
                        xv = xbc[:, :, 0:DI].rearrange("p t (h d) -> p t h d", h=HEADS)

                        def heads(ap):
                            return ap.rearrange("p t (h d) -> p t h d", h=HEADS)

                        def power(dst, src, ready, done, k=0):
                            pool.wait_ge(ready, k + 1)
                            pool.tensor_tensor(dst, src, half[:, 0:dst.shape[-1]], ALU.pow).then_inc(done, 1)

                        def group(k):
                            g, n = GROUPS4[k]
                            return slice(g, g + n)

                        def stage(name, k):
                            if name == "gn2":
                                power(mv[:, 5:6], mv[:, 4:5], S["gn_ve"], S["gn_rs"])
                            elif name == "var1":
                                power(col[:, 4, group(k)], col[:, 3, group(k)], S["var1"], S["pow1"], k)
                            elif name == "xl1":
                                power(col[:, 6, group(k)], col[:, 5, group(k)], S["rv1"], S["powr"], k)
                                pool.wait_ge(S["xl_done"], k + 1)
                                pool.tensor_tensor(res[:, group(k), :], xl[:, group(k), :], tok1[:, group(k), :], ALU.add)\
                                    .then_inc(S["res_done"], 1)
                            elif name == "split":
                                pool.wait_ge(S["xf_done"], 2)
                                pool.wait_ge(S["hh_done"], 4)
                                w = slice(k * PB, (k + 1) * PB)
                                for n, (rows, high, dst) in enumerate(((slice(0, C), st[ot], sw[ot]), (slice(C, P), sw[ot], st[ot]))):
                                    pool.tensor_tensor(dst[rows, w], xf[rows, w], high[rows, w], ALU.subtract)\
                                        .then_inc(S["split_done"], 1)
                                    pool.wait_ge(S["split_done"], 2 * k + n + 1)
                            elif name == "val":
                                w = group(k)
                                pool.wait_ge(S["rn2_done"], k + 1)
                                pool.tensor_tensor(gt[ot][:, w, :], gx[:, w, 0:C], mid(bc_b[:, :], w.stop - w.start, C), ALU.add)\
                                    .then_inc(S["gt_sum"], 1)
                                pool.wait_ge(S["gt_sum"], k + 1)
                                pool.tensor_tensor(gt[ot][:, w, :], gt[ot][:, w, :], bt(rn2[ot][:, w], C), ALU.mult)\
                                    .then_inc(S["gt_done"], 1)
                            elif name == "skip":
                                pool.wait_ge(scattered, bi * (32 * TILES))
                                pool.wait_ge(S["silu_done"], TILES)
                                pool.tensor_tensor(heads(yi[:, :, :]), xv,
                                                   dp_b[:, :].unsqueeze(1).unsqueeze(3).to_broadcast([P, TILES, HEADS, HD]),
                                                   ALU.mult).then_inc(S["skip_done"], 1)
                            elif name == "xp":
                                w = group(k)
                                pool.wait_ge(S["a_done"], 1)
                                pool.tensor_tensor(heads(xp[:, w, 0:DI]), xv[:, w], bt(dts[:, 4, w], HD), ALU.mult)\
                                    .then_inc(S["xp_done"], 1)
                            elif name == "at":
                                if k < 2:
                                    pool.wait_ge(S["a_done"], 1)
                                else:
                                    t = turn["d", 2 * k - 3]
                                    pool.wait_ge(full[t % 3], t // 3 + 1)
                                pool.tensor_tensor(at[k % 2][:, :, :], mid(tri_le[:, :], HEADS, P), bt(dts[:, 5, k, :], P), ALU.mult)\
                                    .then_inc(S["at_done"], 1)
                            elif name == "yib":
                                pool.wait_ge(S["inter_d"], NG4)
                                pool.wait_ge(S["skip_done"], 1)
                                yf = yi[:, :, :].rearrange("p t c -> p (t c)")
                                pool.tensor_tensor(yf, yf, tmp[:, :], ALU.add).then_inc(S["yi_base"], 1)
                            elif name == "yz":
                                w = group(k)
                                pool.wait_ge(S["y_done"], w.stop)
                                pool.tensor_tensor(yi[:, w, :], yi[:, w, :], zs[:, w, :], ALU.mult)\
                                    .then_inc(S["yz_done"], 1)
                            elif name == "yvar":
                                power(col[:, 0, group(k)], col[:, 1, group(k)], S["yvar"], S["ypow"], k)
                            elif name == "var2":
                                power(col[:, 4, group(k)], col[:, 3, group(k)], S["var2"], S["pow2"], k)
                            elif name == "scat":
                                if k == 0:
                                    pool.wait_ge(filled, 16 * FILLS)
                                scatter(pool, [k])

                        for u in range(UNITS):
                            for name, k in at_unit[u]:
                                stage(name, k)

                    @block.tensor
                    def _(pe):
                        def qk(u):
                            pb, qp = divmod(u, QP)
                            if u >= 2:
                                squared(pe, u - 2)
                            for h in (0, 1):
                                q = 2 * qp + h
                                o = psum[:, 2 * (u % 2) + h, 0:PB]
                                pe.matmul(o, st[me][:, q * P:(q + 1) * P], st[me][:, pb * PB:(pb + 1) * PB], start=True, stop=False)
                                ins = pe.matmul(o, st[me][:, q * P:(q + 1) * P], sw[me][:, pb * PB:(pb + 1) * PB], start=False,
                                                stop=True)
                            ins.then_inc(S["qk"], 1)

                        def av(u):
                            pb, qp = divmod(u, QP)
                            squared(pe, u)
                            if qp == 0 and pb >= 1:
                                pe.wait_ge(S["o_out"], pb)
                            for h in (0, 1):
                                ins = pe.matmul(psum[C * h:C * h + C, 4, 0:PB], gt[me][:, 2 * qp + h, :], scr[:, u % 2, h, :],
                                                start=(qp == 0), stop=(qp == QP - 1))
                            ins.then_inc(S["av"], 1)

                        def mm(o, a, b, **kw):
                            return pe.matmul(o, a, b, start=True, stop=True, skip_group_check=True)

                        def stage(name, k):
                            if name not in BANKED:
                                return
                            bank, b, used = bank_of(name, k)
                            if used:
                                pe.wait_ge(free[b], used)
                            if name == "gn1":
                                pe.wait_ge(S["gn_mean"], 1)
                                ins = mm(bank[:, 0:1], pair[:, :], mv[:, 0:1])
                            elif name == "gn2":
                                pe.wait_ge(S["gn_var2"], 1)
                                ins = mm(bank[:, 0:1], pair[:, :], mv[:, 3:4])
                            elif name == "xtr":
                                g, n = XG[k]
                                for j in range(g, g + n):
                                    ins = pe.transpose(bank[:, (j - g) * C:(j - g + 1) * C], xd[0:C, j * P:(j + 1) * P],
                                                       ident[0:C, 0:C])
                            elif name == "gx":
                                pe.wait_ge(S["xf_done"], 2)
                                g, n = GROUPS4[k]
                                for j in range(g, g + n):
                                    ins = mm(bank[:, (j - g) * P:(j - g + 1) * P], xf[:, j * P:(j + 1) * P], wr[:, :])
                            elif name == "ot":
                                g, n = GROUPS4[k]
                                for j in range(g, g + n):
                                    ins = mm(bank[:, (j - g) * P:(j - g + 1) * P], osb[ot][:, j * P:(j + 1) * P], fold[:, :])
                            elif name == "xt":
                                pe.wait_ge(S["xn_done"], k + 1)
                                g, n = PAIRS[k]
                                for j in range(g, g + n):
                                    ins = pe.transpose(bank[:, (j - g) * P:(j - g + 1) * P],
                                                       xn[:, 2 * j:2 * j + 2, :].rearrange("p t c -> p (t c)"), ident[:, :])
                            elif name == "ip":
                                pe.wait_ge(S["x2_a"], k // 4 + 1)
                                pe.wait_ge(S["x2_d"], k // 4 + 1)
                                o = PAD + k * P
                                pe.matmul(bank[:, 0:ZX], x2[:, o:o + P], wa[:, :], start=True, stop=False, skip_group_check=True)
                                ins = pe.matmul(bank[:, 0:XBC], x2[:, o - 2:o - 2 + P], wb[:, :], start=False, stop=True,
                                                skip_group_check=True)
                            elif name == "bc":
                                g, n = GROUPS4[k]
                                pe.wait_ge(S["silu_done"], TILES)
                                for j in range(g, g + n):
                                    r, _ = tile_at(j)
                                    mm(bank[r:r + 2 * NS, 0:P], xbc[:, j, DI:XBC], ident[:, :])
                                    ins = mm(bank[r:r + NS, P:2 * P], xbc[:, j, DI + NS:XBC], ident[:, :])
                            elif name == "cum":
                                pe.wait_ge(S["a_done"], 1)
                                af = dts[:, 5].rearrange("p t h -> p (t h)")
                                w = TILES * HEADS
                                for n, m in enumerate((tri_le, tri_gt, ones)):
                                    ins = mm(bank[:, n * w:(n + 1) * w], m[:, :], af)
                            elif name == "g":
                                pe.wait_ge(S["ct_done"], k + 1)
                                n = GROUPS4[k][1]
                                ins = mm(bank[:, 0:n * P], b_t[:, k, :], c_t[:, k, 0:n, :].rearrange("p t c -> p (t c)"))
                            elif name == "ds":
                                pe.wait_ge(S["xpp_done"], k + 1)
                                g, n = GROUPS4[k]
                                for j in range(g, g + n):
                                    ins = mm(bank[0:NS, (j - g) * P:(j - g + 1) * P], xbc[:, j, DI:DI + NS],
                                             tmp[:, j * P:(j + 1) * P])
                            elif name == "in":
                                g, n = GROUPS4[k]
                                if g + n - 1 >= 1:
                                    pe.wait_ge(S["state_done"], g + n - 1)
                                for j in range(g, g + n):
                                    ins = mm(bank[:, (j - g) * P:(j - g + 1) * P], c_t[:, k, j - g, :], states[:, k, :])
                            elif name == "d":
                                pe.wait_ge(S["at_done"], k // 2 + 1)
                                atf = at[k // 2 % 2][:, :, :].rearrange("p h t -> p (h t)")
                                ins = mm(bank, tri_gt[:, :], atf[:, 512 * (k % 2):512 * (k % 2) + 512])
                            elif name == "yt":
                                pe.wait_ge(S["m_done"], k + 1)
                                for h in range(HEADS):
                                    q, r = h % 4, h // 4
                                    ins = mm(bank[32 * q:32 * q + 32, r * P:(r + 1) * P], xp[:, k, HD * h:HD * h + 2 * HD],
                                             el[k % 2][:, h, :])
                            elif name == "yy":
                                pe.wait_ge(S["yts_done"], k + 1)
                                for r in (0, 1):
                                    ins = pe.transpose(bank[:, r * P:(r + 1) * P], yts[:, r, :], ident[:, :])
                            elif name == "ytr":
                                pe.wait_ge(S["yz_done"], k + 1)
                                g, n = GROUPS4[k]
                                for j in range(g, g + n):
                                    ins = pe.transpose(bank[:, (j - g) * P:(j - g + 1) * P], yi[:, j, :], ident[:, :])
                            elif name == "op":
                                pe.wait_ge(S["yt_out"], k + 1)
                                g, n = GROUPS4[k]
                                for j in range(g, g + n):
                                    ins = mm(bank[:, (j - g) * P:(j - g + 1) * P], yt_sb[:, j * P:(j + 1) * P], wo[:, :])
                            elif name == "tt":
                                pe.wait_ge(S["t3_done"], k + 1)
                                g, n = PAIRS[k]
                                for j in range(g, g + n):
                                    ins = pe.transpose(bank[:, (j - g) * P:(j - g + 1) * P],
                                                       tok3[:, 2 * j:2 * j + 2, :].rearrange("p t c -> p (t c)"), ident[:, :])
                            elif name == "lg":
                                pe.wait_ge(S["t3t"], NG4)
                                for g, n in PAIRS:
                                    for j in range(g, g + n):
                                        o = (2 * g + n + j - g) * P
                                        ins = mm(bank[:, 2 * E * j:2 * E * j + 2 * E], tmp[:, o:o + P], gwd[:, :])
                            elif name == "rk":
                                pe.wait_ge(S["oh_done"], 1)
                                ohf = rt[:, 2].rearrange("p t e -> p (t e)")
                                w = TILES * E
                                mm(bank[:, 0:w], tri_le[:, :], ohf)
                                ins = mm(bank[:, w:2 * w], ones[:, :], ohf)
                            ins.then_inc(full[b], 1)

                        if conv:
                            qk(0)
                            qk(1)
                        for u in range(UNITS):
                            if u == 0:
                                for name, k in at_unit[u]:
                                    stage(name, k)
                            if conv:
                                av(u)
                                if u + 2 < UNITS:
                                    qk(u + 2)
                            if u > 0:
                                for name, k in at_unit[u]:
                                    stage(name, k)

                    @block.scalar
                    def _(act):
                        def relu(u):
                            act.wait_ge(S["qk"], u + 1)
                            if u >= 2:
                                squared(act, u - 2)
                            act.activation(rel[:, u % 2], psum[:, 2 * (u % 2):2 * (u % 2) + 2, 0:PB], ACT.Relu).then_inc(S["rel"], 1)
                            if not on_dve[u]:
                                act.wait_ge(S["rel"], u + 1)
                                if u >= 2:
                                    act.wait_ge(S["av"], u - 1)
                                act.activation(scr[:, u % 2], rel[:, u % 2], ACT.Square).then_inc(S["sq_act"], 1)

                        def o_out(pb):
                            act.wait_ge(S["av"], QP * (pb + 1))
                            act.activation(osb[me][:, pb * PB:(pb + 1) * PB], psum[:, 4, 0:PB], ACT.Copy).then_inc(S["o_out"], 1)

                        def bank(name, k):
                            ap, b, used = bank_of(name, k)
                            act.wait_ge(full[b], used + 1)
                            return ap, free[b]

                        def stage(name, k):
                            if name == "hh":
                                act.wait_ge(S["gn_ready"], 1)
                                rows, dst = ((slice(0, C), st[ot]), (slice(C, P), sw[ot]))[k % 2]
                                w = slice(k // 2 * T // 2, (k // 2 + 1) * T // 2)
                                act.activation(dst[rows, w], xd[rows, w], ACT.Identity, bias=mv[rows, 7:8], scale=mv[rows, 6:7])\
                                   .then_inc(S["hh_done"], 1)
                            elif name == "xtr":
                                if ssm and k == 0:
                                    act.wait_ge(S["cen1"], NG4)
                                g, n = XG[k]
                                ps, fr = bank(name, k)
                                act.activation(xtm[ot][:, g:g + n, :].rearrange("p t c -> p (t c)"), ps[:, 0:n * C], ACT.Copy)\
                                   .then_inc(fr, 1)
                            elif name == "gx":
                                if k == 0:
                                    act.wait_ge(S["hh_done"], 4)
                                    act.wait_ge(S["xf_done"], 2)
                                g, n = GROUPS4[k]
                                ps, fr = bank(name, k)
                                act.activation(xd[:, g * P:(g + n) * P], ps[:, 0:n * P], ACT.Copy).then_inc(fr, 1)
                            elif name == "sq1":
                                act.wait_ge(S["cen1"], k + 1)
                                g, n = GROUPS4[k]
                                act.activation(tmp[:, g * C:(g + n) * C], xl[:, g:g + n, :].rearrange("p t c -> p (t c)"), ACT.Square)\
                                   .then_inc(S["sq1"], 1)
                            elif name == "xt":
                                g, n = PAIRS[k]
                                ps, _ = bank(name, k)
                                src = ps[0:C, 0:n * P].rearrange("p (j t) -> p j t", t=P)
                                w = slice(PAD + 2 * g * P, PAD + 2 * (g + n) * P)
                                v = slice(PAD + 1 + 2 * g * P, PAD + 1 + 2 * (g + n) * P)
                                act.activation(x2[0:C, w].rearrange("p (j h t) -> p j h t", h=2, t=P)[:, :, 0, :], src, ACT.Copy)
                                act.activation(x2[C:P, v].rearrange("p (j h t) -> p j h t", h=2, t=P)[:, :, 0, :], src, ACT.Copy)\
                                   .then_inc(S["x2_a"], 1)
                            elif name == "nrm":
                                t = turn["gx", k]
                                act.wait_ge(free[t % 3], t // 3 + 1)
                                g, n = GROUPS4[k]
                                act.activation(gt[ot][:, g:g + n, :], gx[:, g:g + n, C:P], ACT.Square).then_inc(S["gsq_done"], 1)
                            elif name == "ip":
                                ps, fr = bank(name, k)
                                act.wait_ge(S["proj_d"], k + 1)
                                act.activation(zs[:, k, :], ps[:, XBC:XBC + DI], ACT.Silu).then_inc(fr, 1)
                                act.activation(xbc[:, k, :], xbc[:, k, :], ACT.Silu).then_inc(S["silu_done"], 1)
                            elif name == "sp1":
                                act.wait_ge(S["sp_in"], 1)
                                act.activation(dts[:, 2], dts[:, 1], ACT.Exp).then_inc(S["sp_exp"], 1)
                            elif name == "sp2":
                                act.wait_ge(S["sp_u"], 1)
                                act.activation(dts[:, 4], dts[:, 3], ACT.Ln).then_inc(S["sp_ln"], 1)
                            elif name == "bc":
                                r = 32 * GROUPS4[k][1]
                                ps, _ = bank(name, k)
                                act.activation(b_t[0:r, k, :], ps[0:r, 0:P], ACT.Copy).then_inc(S["bt_done"], 1)
                            elif name == "cum":
                                ps, fr = bank(name, k)
                                act.activation(dec[:, :, :, :].rearrange("p k t h -> p (k t h)"), ps[:, 0:3 * TILES * HEADS],
                                               ACT.Exp).then_inc(fr, 1)
                                b, used = turn[name, k] % 3, turn[name, k] // 3
                                act.wait_ge(free[b], used + 1)
                                act.sem_inc(S["dec_done"], 1)
                            elif name == "d":
                                c, hf = divmod(k, 2)
                                ps, fr = bank(name, k)
                                act.activation(el[c % 2][:, 4 * hf:4 * hf + 4, :].rearrange("p h t -> p (h t)"), ps, ACT.Exp)\
                                   .then_inc(fr, 1)
                                if hf:
                                    b, used = turn[name, k] % 3, turn[name, k] // 3
                                    act.wait_ge(free[b], used + 1)
                                    act.sem_inc(S["exp_done"], 1)
                            elif name == "yt":
                                if k >= 1:
                                    act.wait_ge(full[turn["yy", k - 1] % 3], turn["yy", k - 1] // 3 + 1)
                                ps, fr = bank(name, k)
                                act.activation(yts[:, :, :].rearrange("p r t -> p (r t)"), ps[:, 0:2 * P], ACT.Copy).then_inc(fr, 1)
                                b, used = turn[name, k] % 3, turn[name, k] // 3
                                act.wait_ge(free[b], used + 1)
                                act.sem_inc(S["yts_done"], 1)
                            elif name == "ysq":
                                act.wait_ge(S["yz_done"], k + 1)
                                g, n = GROUPS4[k]
                                act.activation(tmp[:, g * P:(g + n) * P], yi[:, g:g + n, :].rearrange("p t c -> p (t c)"), ACT.Square)\
                                   .then_inc(S["ysq_done"], 1)
                            elif name == "ytr":
                                g, n = GROUPS4[k]
                                ps, fr = bank(name, k)
                                act.activation(yt_sb[:, g * P:(g + n) * P], ps[:, 0:n * P], ACT.Copy).then_inc(fr, 1)
                                b, used = turn[name, k] % 3, turn[name, k] // 3
                                act.wait_ge(free[b], used + 1)
                                act.sem_inc(S["yt_out"], 1)
                            elif name == "sq2":
                                act.wait_ge(S["cen2"], k + 1)
                                g, n = GROUPS4[k]
                                act.activation(tmp[:, g * P:g * P + n * C], tok3[:, g:g + n, :].rearrange("p t c -> p (t c)"), ACT.Square)\
                                   .then_inc(S["sq2"], 1)
                            elif name == "tt":
                                g, n = PAIRS[k]
                                ps, fr = bank(name, k)
                                act.activation(tmp[:, (2 * g + n) * P:(2 * g + 2 * n) * P], ps[:, 0:n * P], ACT.Copy).then_inc(fr, 1)
                                b, used = turn[name, k] % 3, turn[name, k] // 3
                                act.wait_ge(free[b], used + 1)
                                act.sem_inc(S["t3t"], 1)
                            elif name == "lg":
                                act.wait_ge(S["sh_done"], 1)
                                act.activation(rt[:, 1], rt[:, 0], ACT.Exp).then_inc(S["pexp"], 1)

                        if conv:
                            relu(0)
                            relu(1)
                        for u in range(UNITS):
                            if u == 0:
                                for name, k in at_unit[u]:
                                    stage(name, k)
                            if conv:
                                if u + 2 < UNITS:
                                    relu(u + 2)
                                if u % QP == QP - 1:
                                    o_out(u // QP)
                            if u > 0:
                                for name, k in at_unit[u]:
                                    stage(name, k)

                    @block.vector
                    def _(dve):
                        chain = [0]

                        def link(ins):
                            chain[0] += 1
                            ins.then_inc(dve_s, 1)
                            dve.wait_ge(dve_s, chain[0])

                        def bank(name, k):
                            ap, b, used = bank_of(name, k)
                            dve.wait_ge(full[b], used + 1)
                            return ap, free[b]

                        def square(u):
                            if not on_dve[u]:
                                return
                            dve.wait_ge(S["rel"], u + 1)
                            if u >= 2:
                                dve.wait_ge(S["av"], u - 1)
                            dve.tensor_tensor(scr[:, u % 2], rel[:, u % 2], psum[:, 2 * (u % 2):2 * (u % 2) + 2, 0:PB],
                                              ALU.mult).then_inc(S["sq_dve"], 1)

                        def center(dst, src, w, done):
                            link(dve.tensor_reduce(col[:, 2, w], src[:, w, :], AX, ALU.add))
                            link(dve.tensor_scalar(col[:, 2, w], col[:, 2, w], 1.0 / C, None, ALU.mult))
                            dve.tensor_tensor(dst[:, w, :], src[:, w, :], bt(col[:, 2, w], C), ALU.subtract).then_inc(done, 1)

                        def variance(squares, w, squared, k, done):
                            dve.wait_ge(squared, k + 1)
                            link(dve.tensor_reduce(col[:, 7, w], squares.rearrange("p (t c) -> p t c", c=C), AX, ALU.add))
                            dve.tensor_scalar(col[:, 3, w], col[:, 7, w], 1.0 / C, 1e-5, ALU.mult, ALU.add).then_inc(done, 1)

                        def group(k):
                            g, n = GROUPS4[k]
                            return slice(g, g + n)

                        def three(ap, n, w=P):
                            return ap[:, 0:n * w].rearrange("p (t c) -> p t c", c=w)

                        def stage(name, k):
                            if name == "gn0":
                                for n in range(k * NPB // 2, (k + 1) * NPB // 2):
                                    ins = dve.bn_stats(stats[:, n, :], xd[:, n * PB:(n + 1) * PB])
                                if k == 1:
                                    link(ins)
                                    link(dve.bn_aggr(mv[:, 0:2], stats[:, :, :]))
                                    dve.engine_nop().then_inc(S["gn_mean"], 1)
                            elif name == "gn1":
                                ps, fr = bank(name, k)
                                link(dve.tensor_copy(mv[:, 2:3], ps[:, 0:1]))
                                dve.engine_nop().then_inc(fr, 1)
                                link(dve.tensor_tensor(mv[:, 4:5], mv[:, 0:1], mv[:, 2:3], ALU.subtract))
                                link(dve.scalar_tensor_tensor(out=mv[:, 3:4], in0=mv[:, 4:5], scalar=mv[:, 4:5], in1=mv[:, 1:2],
                                                              op0=ALU.mult, op1=ALU.add))
                                dve.engine_nop().then_inc(S["gn_var2"], 1)
                            elif name == "gn2":
                                ps, fr = bank(name, k)
                                link(dve.tensor_scalar(mv[:, 4:5], ps[:, 0:1], 1e-5, None, ALU.add))
                                dve.engine_nop().then_inc(fr, 1)
                                dve.engine_nop().then_inc(S["gn_ve"], 1)
                            elif name == "gn4":
                                dve.wait_ge(S["gn_rs"], 1)
                                link(dve.tensor_scalar(mv[:, 6:7], mv[:, 5:6], XF_SCALE, None, ALU.mult))
                                dve.scalar_tensor_tensor(out=mv[:, 7:8], in0=mv[:, 2:3], scalar=-1.0, in1=mv[:, 6:7],
                                                         op0=ALU.mult, op1=ALU.mult).then_inc(S["gn_ready"], 1)
                            elif name == "hh":
                                dve.wait_ge(S["gn_ready"], 1)
                                if k < 2:
                                    w = slice(k * T // 2, (k + 1) * T // 2)
                                    dve.tensor_scalar(xf[:, w], xd[:, w], mv[:, 6:7], mv[:, 7:8], ALU.mult, ALU.add)\
                                       .then_inc(S["xf_done"], 1)
                            elif name == "nrm":
                                w = group(k)
                                dve.wait_ge(S["gsq_done"], k + 1)
                                link(dve.tensor_reduce(rn2[ot][:, w], gt[ot][:, w, :], AX, ALU.add))
                                link(dve.tensor_scalar(rn2[ot][:, w], rn2[ot][:, w], (1e-8 * XF_SCALE) ** 2, None, ALU.max))
                                dve.reciprocal(rn2[ot][:, w], rn2[ot][:, w]).then_inc(S["rn2_done"], 1)
                            elif name == "ot":
                                ps, fr = bank(name, k)
                                w = group(k)
                                n = w.stop - w.start
                                dve.tensor_tensor(tok1[:, w, :], three(ps, n)[:, :, 0:C], bt(rn2[ot][:, w], C), ALU.mult)\
                                   .then_inc(fr, 1)
                                dve.wait_ge(fr, turn[name, k] // 3 + 1)
                                link(dve.tensor_tensor(tok1[:, w, :], tok1[:, w, :], xtm[ot][:, w, :], ALU.add))
                                center(xl, tok1, w, S["cen1"])
                            elif name == "var1":
                                w = group(k)
                                variance(tmp[:, C * w.start:C * w.stop], w, S["sq1"], k, S["var1"])
                            elif name == "xl1":
                                w = group(k)
                                dve.wait_ge(S["pow1"], k + 1)
                                link(dve.tensor_tensor(col[:, 5, w], col[:, 4, w], col[:, 4, w], ALU.mult))
                                link(dve.tensor_tensor(col[:, 5, w], col[:, 5, w], col[:, 7, w], ALU.mult))
                                dve.tensor_scalar(col[:, 5, w], col[:, 5, w], 1.0 / C, 1.1920929e-07, ALU.mult, ALU.add)\
                                   .then_inc(S["rv1"], 1)
                                dve.tensor_tensor(xl[:, w, :], xl[:, w, :], bt(col[:, 4, w], C), ALU.mult).then_inc(S["xl_done"], 1)
                            elif name == "xn":
                                w = group(k)
                                dve.wait_ge(S["powr"], k + 1)
                                dve.wait_ge(S["xl_done"], k + 1)
                                dve.tensor_tensor(xn[:, w, :], xl[:, w, :], bt(col[:, 6, w], C), ALU.mult).then_inc(S["xn_done"], 1)
                            elif name == "xt":
                                g, n = PAIRS[k]
                                ps, fr = bank(name, k)
                                dve.wait_ge(S["x2_a"], k + 1)
                                src = ps[C:P, 0:n * P].rearrange("p (j t) -> p j t", t=P)
                                w = slice(PAD + 2 * g * P, PAD + 2 * (g + n) * P)
                                v = slice(PAD + 1 + 2 * g * P, PAD + 1 + 2 * (g + n) * P)
                                dve.tensor_copy(x2[0:C, w].rearrange("p (j h t) -> p j h t", h=2, t=P)[:, :, 1, :], src)
                                link(dve.tensor_copy(x2[C:P, v].rearrange("p (j h t) -> p j h t", h=2, t=P)[:, :, 1, :], src))
                                dve.engine_nop().then_inc(S["x2_d"], 1)
                                dve.engine_nop().then_inc(fr, 1)
                            elif name == "ip":
                                ps, _ = bank(name, k)
                                dve.tensor_tensor(xbc[:, k, :], ps[:, 0:XBC], cb_b[:, :], ALU.add)
                                dve.tensor_tensor(dts[:, 0, k, :], ps[:, XBC + DI:ZX], dtb_b[:, :], ALU.add)\
                                   .then_inc(S["proj_d"], 1)
                            elif name == "sp1":
                                dve.wait_ge(S["proj_d"], TILES)
                                link(dve.tensor_scalar(dts[:, 1], dts[:, 0], -1.0, None, ALU.mult))
                                dve.tensor_tensor(dts[:, 1], dts[:, 1], dts[:, 0], ALU.min).then_inc(S["sp_in"], 1)
                            elif name == "sp2":
                                dve.wait_ge(S["sp_exp"], 1)
                                dve.tensor_scalar(dts[:, 3], dts[:, 2], 1.0, None, ALU.add).then_inc(S["sp_u"], 1)
                                dve.wait_ge(S["sp_u"], 1)
                                link(dve.scalar_tensor_tensor(out=dts[:, 2], in0=dts[:, 3], scalar=-1.0, in1=dts[:, 2],
                                                              op0=ALU.add, op1=ALU.subtract))
                                link(dve.reciprocal(dts[:, 1], dts[:, 3]))
                                link(dve.tensor_tensor(dts[:, 2], dts[:, 2], dts[:, 1], ALU.mult))
                            elif name == "sp3":
                                dve.wait_ge(S["sp_ln"], 1)
                                link(dve.tensor_tensor(dts[:, 4], dts[:, 4], dts[:, 2], ALU.subtract))
                                link(dve.scalar_tensor_tensor(out=dts[:, 4], in0=dts[:, 0], scalar=0.0, in1=dts[:, 4],
                                                              op0=ALU.max, op1=ALU.add))
                                dve.tensor_tensor(dts[:, 5], dts[:, 4], mid(nega_b[:, :], TILES, HEADS), ALU.mult)\
                                   .then_inc(S["a_done"], 1)
                            elif name == "xpp":
                                w = group(k)
                                dve.wait_ge(S["dec_done"], 1)
                                dve.wait_ge(S["xp_done"], k + 1)
                                dve.tensor_tensor(three(tmp, TILES)[:, w, :].rearrange("p t (h d) -> p t h d", h=HEADS),
                                                  xp[:, w, 0:DI].rearrange("p t (h d) -> p t h d", h=HEADS),
                                                  bt(dec[:, 1, w], HD), ALU.mult).then_inc(S["xpp_done"], 1)
                            elif name == "bc":
                                ps, fr = bank(name, k)
                                dve.wait_ge(S["bt_done"], k + 1)
                                for q in range(GROUPS4[k][1]):
                                    r = slice(32 * q, 32 * q + NS)
                                    ins = dve.tensor_copy(c_t[r, k, q, :], ps[r, P:2 * P])
                                link(ins)
                                dve.engine_nop().then_inc(fr, 1)
                                dve.engine_nop().then_inc(S["ct_done"], 1)
                            elif name == "g":
                                g, n = GROUPS4[k]
                                ps, fr = bank(name, k)
                                dve.tensor_tensor(gm[:, g:g + n, :], three(ps, n), mid(tri_le[:, :], n, P), ALU.mult).then_inc(fr, 1)
                                dve.wait_ge(fr, turn[name, k] // 3 + 1)
                            elif name == "st":
                                g, n = GROUPS4[k]
                                ps, fr = bank("ds", k)
                                if k == 0:
                                    dve.wait_ge(S["dec_done"], 1)
                                for j in range(g, min(g + n, TILES - 1)):
                                    r, s = tile_at(j)
                                    r1, s1 = tile_at(j + 1)
                                    if j:
                                        dve.wait_ge(S["state_done"], j)
                                    link(dve.tensor_tensor(sdec[r:r + NS, :].rearrange("n (h d) -> n h d", h=HEADS),
                                                           states[r:r + NS, s, :].rearrange("n (h d) -> n h d", h=HEADS),
                                                           bt(dec[r:r + NS, 2, j, :], HD), ALU.mult))
                                    dve.tensor_tensor(states[r1:r1 + NS, s1, :], ps[0:NS, (j - g) * P:(j - g + 1) * P],
                                                      sdec[r:r + NS, :], ALU.add).then_inc(S["state_done"], 1)
                                dve.wait_ge(S["state_done"], min(g + n, TILES - 1))
                                dve.engine_nop().then_inc(fr, 1)
                            elif name == "in":
                                g, n = GROUPS4[k]
                                ps, fr = bank(name, k)
                                link(dve.tensor_tensor(
                                    tmp[:, g * P:(g + n) * P].rearrange("p (t h d) -> p (t h) d", t=n, h=HEADS),
                                    ps[:, 0:n * P].rearrange("p (t h d) -> p (t h) d", t=n, h=HEADS),
                                    bt(dec[:, 0, g:g + n, :].rearrange("p t h -> p (t h)"), HD), ALU.mult))
                                dve.engine_nop().then_inc(fr, 1)
                                dve.engine_nop().then_inc(S["inter_d"], 1)
                            elif name == "m":
                                dve.wait_ge(S["exp_done"], k + 1)
                                e_ = el[k % 2]
                                dve.tensor_tensor(e_[:, :, :], e_[:, :, :], mid(gm[:, k, :], HEADS, P), ALU.mult)\
                                   .then_inc(S["m_done"], 1)
                            elif name == "yy":
                                if k == 0:
                                    dve.wait_ge(S["yi_base"], 1)
                                ps, fr = bank(name, k)
                                yv = yi[:, k, :].rearrange("p (h d) -> p h d", h=HEADS)
                                dve.tensor_tensor(yv, yv, ps[:, 0:2 * P].rearrange("p (h d) -> p h d", d=32)[:, :, 0:HD], ALU.add)\
                                   .then_inc(S["y_done"], 1)
                                dve.wait_ge(S["y_done"], k + 1)
                                dve.engine_nop().then_inc(fr, 1)
                            elif name == "yvar":
                                w = group(k)
                                dve.wait_ge(S["ysq_done"], k + 1)
                                link(dve.tensor_reduce(col[:, 1, w], three(tmp, TILES)[:, w, :], AX, ALU.add))
                                dve.tensor_scalar(col[:, 1, w], col[:, 1, w], 1.0 / DI, 1e-5, ALU.mult, ALU.add).then_inc(S["yvar"], 1)
                            elif name == "op":
                                if k == 0:
                                    dve.wait_ge(S["res_done"], NG4)
                                dve.wait_ge(S["ypow"], k + 1)
                                w = group(k)
                                ps, fr = bank(name, k)
                                dve.tensor_tensor(tok2[:, w, :], three(ps, w.stop - w.start)[:, :, 0:C], bt(col[:, 0, w], C), ALU.mult)\
                                   .then_inc(fr, 1)
                                dve.wait_ge(fr, turn[name, k] // 3 + 1)
                                dve.tensor_tensor(tok2[:, w, :], tok2[:, w, :], res[:, w, :], ALU.add).then_inc(S["t2_done"], 1)
                            elif name == "cen2":
                                dve.wait_ge(S["t2_done"], k + 1)
                                center(tok3, tok2, group(k), S["cen2"])
                            elif name == "var2":
                                w = group(k)
                                o = w.start * P
                                variance(tmp[:, o:o + (w.stop - w.start) * C], w, S["sq2"], k, S["var2"])
                            elif name == "xl2":
                                w = group(k)
                                dve.wait_ge(S["pow2"], k + 1)
                                dve.tensor_tensor(tok3[:, w, :], tok3[:, w, :], bt(col[:, 4, w], C), ALU.mult).then_inc(S["t3_done"], 1)
                            elif name == "lg":
                                ps, fr = bank(name, k)
                                link(dve.tensor_tensor(rt[:, 0], three(ps, TILES, E), mid(gb_b[:, :], TILES, E), ALU.add))
                                dve.engine_nop().then_inc(fr, 1)
                                link(dve.tensor_reduce(col[:, 2, :], rt[:, 0], AX, ALU.max))
                                link(dve.tensor_tensor(rt[:, 0], rt[:, 0], bt(col[:, 2, :], E), ALU.subtract))
                                dve.engine_nop().then_inc(S["sh_done"], 1)
                                link(dve.tensor_scalar(rt[:, 3], rt[:, 0], 0.0, None, ALU.is_ge))
                                link(dve.tensor_tensor(rt[:, 3], rt[:, 3], mid(eights[:, :], TILES, E), ALU.mult))
                                link(dve.tensor_reduce(col[:, 7, :], rt[:, 3], AX, ALU.max))
                                dve.tensor_tensor(rt[:, 2], mid(eights[:, :], TILES, E), bt(col[:, 7, :], E), ALU.is_equal)\
                                   .then_inc(S["oh_done"], 1)
                            elif name == "rk":
                                dve.wait_ge(S["pexp"], 1)
                                link(dve.tensor_reduce(col[:, 2, :], rt[:, 1], AX, ALU.add))
                                link(dve.reciprocal(col[:, 2, :], col[:, 2, :]))
                                ps, fr = bank(name, k)
                                dve.tensor_copy(rt[:, 4, 0, :], carry[:, :])
                                tot = ps[:, TILES * E:2 * TILES * E].rearrange("p (t e) -> p t e", e=E)
                                link(dve.tensor_copy(rt[:, 4, 1:TILES, :], tot[:, 0:TILES - 1, :]))
                                a, far = 4, 1
                                while far < TILES:
                                    dve.tensor_copy(rt[:, 7 - a, 0:far, :], rt[:, a, 0:far, :])
                                    link(dve.tensor_tensor(rt[:, 7 - a, far:TILES, :], rt[:, a, far:TILES, :],
                                                           rt[:, a, 0:TILES - far, :], ALU.add))
                                    a, far = 7 - a, 2 * far
                                link(dve.tensor_tensor(carry[:, :], rt[:, a, TILES - 1, :], tot[:, TILES - 1, :], ALU.add))
                                link(dve.tensor_tensor(rt[:, 4], rt[:, a], three(ps, TILES, E), ALU.add))
                                dve.engine_nop().then_inc(fr, 1)
                                link(dve.tensor_tensor(rt[:, 4], rt[:, 4], rt[:, 2], ALU.mult))
                                link(dve.tensor_reduce(col[:, 1, :], rt[:, 4], AX, ALU.add))
                                link(dve.tensor_scalar(col[:, 1, :], col[:, 1, :], -1.0, None, ALU.add))
                                link(dve.tensor_scalar(col[:, 3, :], col[:, 1, :], float(CAP), None, ALU.is_ge))
                                link(dve.tensor_scalar(col[:, 7, :], col[:, 7, :], -float(STRIDE), float(E * STRIDE), ALU.mult, ALU.add))
                                link(dve.tensor_tensor(col[:, 0, :], col[:, 1, :], col[:, 7, :], ALU.add))
                                link(dve.scalar_tensor_tensor(out=col[:, 0, :], in0=col[:, 3, :], scalar=BIG, in1=col[:, 0, :],
                                                              op0=ALU.mult, op1=ALU.add))
                                dve.wait_ge(S["yi_base"], 1)
                                dve.tensor_copy(slot_s[:, :], col[:, 0, :])
                                link(dve.tensor_copy(id_s[:, :], token[:, :]))
                                dve.tensor_scalar(token[:, :], token[:, :], float(T), None, ALU.add)
                                link(dve.tensor_scalar(col[:, 4, :], col[:, 3, :], -1.0, 1.0, ALU.mult, ALU.add))
                                dve.tensor_tensor(gain[:, bass.ds((bi - 1) * TILES, TILES)], col[:, 4, :], col[:, 2, :], ALU.mult)

                        if conv:
                            square(0)
                        for u in range(UNITS):
                            if conv and u + 1 < UNITS:
                                square(u + 1)
                            for name, k in at_unit[u]:
                                stage(name, k)
                clear()

            assert B % 2 == 0 and B >= 4
            iteration(-1, 1, False, False, True, 1)
            iteration(0, 0, True, False, True, 2)
            with nc.Fori(1, B - 1, 2) as bi:
                iteration(bi, 1, True, True, True, (bi + 2) % B)
                iteration(bi + 1, 0, True, True, True, (bi + 3) % B)
            iteration(B - 1, 1, True, True, False, None)
            iteration(B, 0, False, True, False, None)
            with nc.Block() as block:
                @block.gpsimd
                def _(pool):
                    scatter(pool, range(TILES))
                    pool.wait_ge(scattered, (B + 1) * 32 * TILES)
            nc.all_engine_barrier()

        with ExitStack() as c2:
            def sb2(name, shape, dt=F32):
                return c2.enter_context(nc.sbuf_tensor(name, shape, dt))

            names2 = []

            def sem2(name):
                s = c2.enter_context(nc.semaphore(name))
                names2.append(s)
                return s

            NT = FBLK // P
            HT = NT // 2
            b2_b = sb2("b2_b", [P, E, C])
            w1s = sb2("w1s", [P, 2, FF])
            w2s = sb2("w2s", [P, 2, C])
            w1_all = sb2("w1_all", [P, E, FF])
            w2_all = sb2("w2_all", [P, E, 2, C])
            LAG = 2
            YB = 4
            who_all = sb2("who_all", [P, LAG + E * FB, NT], I32)
            xin = sb2("xin", [P, 3, NT, C])
            xt = sb2("xt", [P, 2, HT * P])
            hs = sb2("hs", [P, 2, 2, HT * P])
            ys = sb2("ys", [P, 2, HT * P])
            yo = sb2("yo", [P, YB, NT, C])
            who = sb2("who", [P, FB, NT], I32)
            e_y = [c2.enter_context(nc.semaphore(f"e_y{k}")) for k in range(YB)]
            SCAT = [(i - LAG if i >= LAG else FB + i - LAG) % YB for i in range(FB)]
            EY = [16 * NT * SCAT.count(k) for k in range(YB)]
            e_w, e_who = sem2("e_w"), sem2("e_who")
            e_x = [sem2(f"e_x{k}") for k in range(3)]
            e_xt, e_xts, e_h, e_ha, e_hd, e_yt, e_ys, e_ytt, e_yo, e_half = (
                sem2(n) for n in ("e_xt", "e_xts", "e_h", "e_ha", "e_hd", "e_yt", "e_ys", "e_ytt", "e_yo", "e_half"))

            def clear2():
                ids = sorted(s.num for s in names2)
                assert ids == list(range(ids[0], ids[0] + len(ids)))
                nc.all_engine_barrier()
                nc.sync.sem_clear(range(ids[0], ids[-1] + 1))
                nc.all_engine_barrier()

            AHEAD = min(3, FB)

            def scatter_rows(pool, i):
                for t in range(NT):
                    pool.indirect_dma_start(
                        out=y_d, out_offset=bass.IndirectOffsetOnAxis(ap=who[:, i, t:t + 1].bitcast(U32), axis=0),
                        in_=yo[:, SCAT[i], t, :], in_offset=None, bounds_check=B * T - 1, oob_is_err=False,
                    ).then_inc(e_y[SCAT[i]], 16)

            def rows(sp, e, s):
                sp.dma_start(xin[:, s % 3], buf_d[bass.ds(e * STRIDE + s * FBLK, FBLK), :]
                             .rearrange("(p t) c -> p t c", p=P)).then_inc(e_x[s % 3], 16)

            with nc.Block() as block:
                @block.vector
                def _(dve):
                    dve.memset(w1s[:, :, :], 0.0)
                    dve.memset(yo[:, :, :, :], 0.0)
                    dve.memset(who_all[:, 0:LAG, :], int(BIG))

                @block.sync
                def _(sp):
                    sp.dma_start(b2_b[:, :, :], b2.partition_broadcast(P)).then_inc(e_w, 16)
                    sp.dma_start(who_all[:, LAG:LAG + E * FB, :], id_d.rearrange("(s p t) c -> p s (t c)", p=P, t=NT))\
                      .then_inc(e_w, 16)
                    for h in (0, 1):
                        sp.dma_start(w1_all[C * h:C * h + C, :, :], w1.rearrange("e c f -> c e f")).then_inc(e_w, 16)
                        sp.dma_start(w2_all[:, :, h, :], w2[:, h * P:(h + 1) * P, :].rearrange("e f c -> f e c")).then_inc(e_w, 16)
                    for s in range(AHEAD):
                        rows(sp, 0, s)
                    sp.wait_ge(e_w, 16 * 6)
                    for s in range(AHEAD):
                        sp.wait_ge(e_x[s], 16)
            clear2()

            def b1_e(e, f):
                return b1_c[:, bass.ds(e, 1), f:f + 1].rearrange("p a b -> p (a b)")

            with nc.Fori(0, E) as e:
                with nc.Block() as block:
                    @block.sync
                    def _(sp):
                        for s in range(AHEAD, FB):
                            sp.wait_ge(e_xt, s - 2)
                            rows(sp, e, s)
                        for k in range(AHEAD):
                            last = max(range(k, FB, 3))
                            sp.wait_ge(e_xt, last + 1)
                            rows(sp, (e + 1) % E, k)
                        for k in range(AHEAD):
                            sp.wait_ge(e_x[k], 16 * len(range(k, FB, 3)))

                    @block.gpsimd
                    def _(pool):
                        pool.tensor_copy(who[:, :, :], who_all[:, bass.ds(e * FB, FB), :]).then_inc(e_who, 1)
                        pool.wait_ge(e_who, 1)
                        for i in range(FB):
                            if i >= LAG:
                                pool.wait_ge(e_yo, 2 * (i - LAG + 1))
                            scatter_rows(pool, i)
                        for k in range(YB):
                            if EY[k]:
                                pool.wait_ge(e_y[k], e * EY[k] + EY[k])

                    @block.tensor
                    def _(pe):
                        pe.wait_ge(e_w, 3)

                        def x_t(s):
                            if s >= AHEAD:
                                pe.wait_ge(e_x[s % 3], 16 * (s // 3))
                            if s >= 1:
                                pe.wait_ge(e_xts, s)
                            for k in range(HT):
                                ins = pe.transpose(psum[:, 0, k * P:(k + 1) * P],
                                                   xin[:, s % 3, 2 * k:2 * k + 2, :].rearrange("p t c -> p (t c)"), ident[:, :])
                            ins.then_inc(e_xt, 1)

                        def hid(s, par):
                            n = 2 * s + par
                            if par == 0:
                                pe.wait_ge(e_xts, s + 1)
                            if n >= 2:
                                pe.wait_ge(e_ha, n - 1)
                                pe.wait_ge(e_hd, n - 1)
                            for f in (0, 1):
                                ins = pe.matmul(psum[:, 1 + 2 * par + f, 0:HT * P], w1s[:, par, f * P:(f + 1) * P],
                                                xt[:, s % 2, :], start=True, stop=True)
                            ins.then_inc(e_h, 1)

                        def down(s, par):
                            n = 2 * s + par
                            pe.wait_ge(e_ha, n + 1)
                            pe.wait_ge(e_hd, n + 1)
                            if n >= 1:
                                pe.wait_ge(e_ys, n)
                            for f in (0, 1):
                                ins = pe.matmul(psum[C * f:C * f + C, 5, 0:HT * P], w2s[:, f, :], hs[:, par, f, :],
                                                start=True, stop=True)
                            ins.then_inc(e_yt, 1)

                        def y_t(s, par):
                            n = 2 * s + par
                            pe.wait_ge(e_ys, n + 1)
                            if n >= 2:
                                pe.wait_ge(e_yo, n - 1)
                            for k in range(HT):
                                ins = pe.transpose(psum[:, 6 + par, k * P:(k + 1) * P], ys[:, par, k * P:(k + 1) * P], ident[:, :])
                            ins.then_inc(e_ytt, 1)

                        x_t(0)
                        hid(0, 0)
                        for s in range(FB):
                            hid(s, 1)
                            down(s, 0)
                            if s + 1 < FB:
                                x_t(s + 1)
                            y_t(s, 0)
                            down(s, 1)
                            if s + 1 < FB:
                                hid(s + 1, 0)
                            y_t(s, 1)

                    @block.scalar
                    def _(act):
                        act.activation(w1s[0:C, 0, :], w1_all[0:C, bass.ds(e, 1), :].rearrange("c e f -> c (e f)"), ACT.Copy)\
                            .then_inc(e_w, 1)
                        act.activation(w2s[:, :, :].rearrange("p h c -> p (h c)"),
                                       w2_all[:, bass.ds(e, 1), :, :].rearrange("p e h c -> p (e h c)"), ACT.Copy).then_inc(e_w, 1)

                        def xt_out(s):
                            act.wait_ge(e_xt, s + 1)
                            if s >= 2:
                                act.wait_ge(e_h, 2 * (s - 1))
                            act.activation(xt[:, s % 2, :], psum[:, 0, 0:HT * P], ACT.Copy).then_inc(e_xts, 1)

                        xt_out(0)
                        for s in range(FB):
                            for par in (0, 1):
                                n = 2 * s + par
                                act.wait_ge(e_h, n + 1)
                                if n >= 2:
                                    act.wait_ge(e_yt, n - 1)
                                act.activation(hs[:, par, 0, :], psum[:, 1 + 2 * par, 0:HT * P], ACT.Relu,
                                               bias=b1_e(e, 0)).then_inc(e_ha, 1)
                                if par == 0 and s + 1 < FB:
                                    xt_out(s + 1)
                                act.wait_ge(e_yt, n + 1)
                                if n >= 2:
                                    act.wait_ge(e_ytt, n - 1)
                                act.activation(ys[:, par, :], psum[:, 5, 0:HT * P], ACT.Copy).then_inc(e_ys, 1)

                    @block.vector
                    def _(dve):
                        dve.tensor_copy(w1s[C:P, 1, :], w1_all[C:P, bass.ds(e, 1), :].rearrange("c e f -> c (e f)"))\
                            .then_inc(e_w, 1)

                        def y_out(s, par):
                            n = 2 * s + par
                            q = s % YB
                            before = SCAT[:min(FB, s + LAG)].count(q)
                            if par == 0 and before:
                                dve.wait_ge(e_y[q], e * EY[q] + 16 * NT * before)
                            dve.wait_ge(e_ytt, n + 1)
                            pv = psum[:, 6 + par, 0:HT * P].rearrange("p (k c) -> p k c", c=P)
                            dst = yo[:, q, :, :].rearrange("p (k h) c -> p k h c", h=2)[:, :, par, :]
                            dve.tensor_tensor(dst, pv[:, :, 0:C], b2_b[:, bass.ds(e, 1), :].to_broadcast([P, HT, C]), ALU.add)\
                               .then_inc(e_half, 1)
                            dve.wait_ge(e_half, n + 1)
                            dve.tensor_tensor(dst, pv[:, :, C:P], dst, ALU.add).then_inc(e_yo, 1)

                        for s in range(FB):
                            for par in (0, 1):
                                n = 2 * s + par
                                dve.wait_ge(e_h, n + 1)
                                if n >= 2:
                                    dve.wait_ge(e_yt, n - 1)
                                dve.tensor_scalar(hs[:, par, 1, :], psum[:, 2 + 2 * par, 0:HT * P], b1_e(e, 1), 0.0,
                                                  ALU.add, ALU.max).then_inc(e_hd, 1)
                                if n >= 1:
                                    y_out((n - 1) // 2, (n - 1) % 2)
                        y_out(FB - 1, 1)
                clear2()
            with nc.Block() as block:
                @block.gpsimd
                def _(pool):
                    pool.tensor_copy(who[:, 0:LAG, :], who_all[:, E * FB:E * FB + LAG, :]).then_inc(e_who, 1)
                    pool.wait_ge(e_who, 1)
                    for i in range(LAG):
                        scatter_rows(pool, i)
                    for k in range(YB):
                        if SCAT[:LAG].count(k):
                            pool.wait_ge(e_y[k], E * EY[k] + 16 * NT * SCAT[:LAG].count(k))
            clear2()

        with ExitStack() as c3:
            def sb3(name, shape, dt=F32):
                return c3.enter_context(nc.sbuf_tensor(name, shape, dt))

            names3 = []

            def sem3(name):
                s = c3.enter_context(nc.semaphore(name))
                names3.append(s)
                return s

            NB = max(n for n in (1, 2, 4, 8) if B % n == 0)
            R = min(4, NB)
            yg = sb3("yg", [P, R, TILES, C])
            t2 = sb3("t2", [P, R, TILES, C])
            msk = sb3("msk", [P, TILES, C], I32)
            subst = sb3("subst", [P, 3, C])
            of = sb3("of", [P, 2, TILES // 2, P])
            g_t = [sem3(f"g_t{k}") for k in range(R)]
            g_o = [sem3(f"g_o{k}") for k in range(2)]
            g_mul, g_fix, g_sum, g_tr, g_of, g_ch = (sem3(n) for n in ("g_mul", "g_fix", "g_sum", "g_tr", "g_of", "g_ch"))

            def clear3():
                ids = sorted(s.num for s in names3)
                assert ids == list(range(ids[0], ids[0] + len(ids)))
                nc.all_engine_barrier()
                nc.sync.sem_clear(range(ids[0], ids[-1] + 1))
                nc.all_engine_barrier()

            with nc.Block() as block:
                @block.vector
                def _(dve):
                    for k, v in enumerate((1e4, -1e4, 0.0)):
                        dve.memset(subst[:, k, :], v)
            clear3()
            with nc.Fori(0, B // NB) as it:
                with nc.Block() as block:
                    @block.gpsimd
                    def _(pool):
                        def times_gain(n):
                            y = yg[:, n % R]
                            pool.wait_ge(g_t[n % R], 32 * (n // R + 1))
                            gv = gain[:, bass.ds(it * (NB * TILES) + n * TILES, TILES)]
                            pool.tensor_tensor(y, y, bt(gv, C), ALU.mult).then_inc(g_mul, 1)

                        times_gain(0)
                        for n in range(NB):
                            if n + 1 < NB:
                                times_gain(n + 1)
                            pool.wait_ge(g_fix, n + 1)
                            pool.tensor_tensor(t2[:, n % R], t2[:, n % R], yg[:, n % R], ALU.add).then_inc(g_sum, 1)

                    @block.sync
                    def _(sp):
                        for n in range(NB):
                            if n >= R:
                                sp.wait_ge(g_tr, n - R + 1)
                            for dst, src in ((yg, y_d), (t2, t2_d)):
                                sp.dma_start(dst[:, n % R], src[bass.ds(it * (NB * T) + n * T, T), :]
                                             .rearrange("(t p) c -> p t c", p=P)).then_inc(g_t[n % R], 16)

                    @block.scalar
                    def _(act):
                        for n in range(NB):
                            act.wait_ge(g_tr, n + 1)
                            if n >= 2:
                                act.wait_ge(g_o[n % 2], 32 * (n // 2))
                            b0 = 3 * (n % 2)
                            flat = psum[:, b0:b0 + 3, :].rearrange("p b n -> p (b n)")
                            act.activation(of[:, n % 2].rearrange("p j t -> p (j t)"), flat[:, 0:TILES * C], ACT.Copy)\
                               .then_inc(g_of, 1)
                            act.wait_ge(g_of, n + 1)
                            od = out_d[bass.ds(it * NB + n, 1), :, :].rearrange("b c (j h t) -> (b c) j h t", h=2, t=P)
                            for h in (0, 1):
                                act.dma_start(od[:, :, h, :], of[C * h:C * h + C, n % 2]).then_inc(g_o[n % 2], 16)
                        for k in (0, 1):
                            if k < NB:
                                act.wait_ge(g_o[k], 32 * len(range(k, NB, 2)))

                    @block.tensor
                    def _(pe):
                        for n in range(NB):
                            pe.wait_ge(g_sum, n + 1)
                            if n >= 2:
                                pe.wait_ge(g_of, n - 1)
                            for j in range(TILES // 2):
                                ins = pe.transpose(psum[:, 3 * (n % 2) + j // 4, (j % 4) * P:(j % 4 + 1) * P],
                                                   t2[:, n % R, 2 * j:2 * j + 2, :].rearrange("p t c -> p (t c)"), ident[:, :])
                            ins.then_inc(g_tr, 1)

                    @block.vector
                    def _(dve):
                        chain = [0]

                        def link(ins):
                            chain[0] += 1
                            ins.then_inc(g_ch, 1)
                            dve.wait_ge(g_ch, chain[0])

                        for n in range(NB):
                            y = yg[:, n % R]
                            dve.wait_ge(g_mul, n + 1)
                            if n >= 1:
                                dve.wait_ge(g_fix, n)
                            for op, limit, to in ((ALU.is_gt, FLT_MAX, 0), (ALU.is_lt, -FLT_MAX, 1)):
                                link(dve.tensor_scalar(msk[:, :, :], y, limit, None, op))
                                link(dve.copy_predicated(y, msk[:, :, :], subst[:, to:to + 1, :].to_broadcast([P, TILES, C])))
                            link(dve.tensor_tensor(msk[:, :, :], y, y, ALU.not_equal))
                            dve.copy_predicated(y, msk[:, :, :], subst[:, 2:3, :].to_broadcast([P, TILES, C])).then_inc(g_fix, 1)
                clear3()


_INS = ['x', 'L0_conv_Wc', 'L0_conv_bc', 'L1_attn_W_in', 'L1_attn_conv_w', 'L1_attn_conv_b', 'L1_attn_dt_bias',
        'L1_attn_A_log', 'L1_attn_Dp', 'L1_attn_gnorm_w', 'L1_attn_norm_w', 'L1_attn_W_out', 'L1_ffn_gate_w',
        'L1_ffn_gate_b', 'L1_ffn_w1', 'L1_ffn_b1', 'L1_ffn_w2', 'L1_ffn_b2']


def kernel(**inputs):
    import numpy as _np
    import concourse.bacc as _bacc
    from concourse import mybir as _mybir
    from concourse.bass_utils import run_bass_kernel_spmd as _run

    nc = _bacc.Bacc("TRN2", target_bir_lowering=False, num_devices=1)
    arrays, args = {}, []
    for name in _INS:
        a = _np.ascontiguousarray(inputs[name])
        arrays[f"in_{name}"] = a
        args.append(nc.dram_tensor(f"in_{name}", a.shape, _mybir.dt.from_np(a.dtype), kind="ExternalInput").ap())
    shape = inputs['x'].shape
    args.append(nc.dram_tensor("out_0", shape, _mybir.dt.float32, kind="ExternalOutput").ap())
    build(nc, *args)
    r = _run(nc, [arrays], core_ids=[0])
    return r.results[0]["out_0"]
```
